# Optimizing a Trainium2 kernel written in Bass

```python
import numpy as np
import jax
import jax.numpy as jnp

def _softmax(x, axis=-1):
    return jax.nn.softmax(x, axis=axis)

def _gelu(x):
    return jax.nn.gelu(x, approximate=True)

def _silu(x):
    return jax.nn.silu(x)

def _sigmoid(x):
    return jax.nn.sigmoid(x)

def _layernorm(x, axis=-1, eps=1e-05):
    m = jnp.mean(x, axis=axis, keepdims=True)
    v = jnp.var(x, axis=axis, keepdims=True)
    return (x - m) / jnp.sqrt(v + eps)

def _scatter_add(tgt, idx, src, axis=0):
    return tgt.at[idx].add(src)

def _segment_sum(src, seg, n):
    return jax.ops.segment_sum(src, seg, n)
kernel_name = 'mk_adaln_d2_jaxref_r8_ddb0ee'

def setup_inputs(seed: int=0):
    np.random.seed(seed)
    _w = jnp.asarray

    def _L0_attn_setup():
        import jax, jax.numpy as jnp
        import numpy as np
        H, KV, HD, HID = (32, 8, 128, 512)
        THETA, FACTOR, HI_FF, LO_FF, ORIG_MAX = (500000.0, 8.0, 4.0, 1.0, 1024)

        def _llama3_inv_freq():
            inv = 1.0 / THETA ** (np.arange(0, HD, 2, dtype=np.float64) / HD)
            wavelen = 2.0 * np.pi / inv
            low_wl = ORIG_MAX / LO_FF
            high_wl = ORIG_MAX / HI_FF
            smooth = (ORIG_MAX / wavelen - LO_FF) / (HI_FF - LO_FF)
            scaled = np.where(wavelen > low_wl, inv / FACTOR, inv)
            mid = (wavelen <= low_wl) & (wavelen >= high_wl)
            scaled = np.where(mid, (1 - smooth) * inv / FACTOR + smooth * inv, scaled)
            return scaled.astype(np.float32)

        def _rope_cos_sin(T):
            inv = _llama3_inv_freq()
            pos = np.arange(T, dtype=np.float32)
            freqs = pos[:, None] * inv[None, :]
            emb = np.concatenate([freqs, freqs], axis=-1)
            return (jnp.asarray(np.cos(emb)), jnp.asarray(np.sin(emb)))

        def _rotate_half(x):
            x1, x2 = jnp.split(x, 2, axis=-1)
            return jnp.concatenate([-x2, x1], axis=-1)
        key = jax.random.key(seed)
        ks = jax.random.split(key, 5)
        s = 1.0 / np.sqrt(HID)
        return {'x': jax.random.normal(ks[0], (1, 256, HID), jnp.float32), 'wq': jax.random.normal(ks[1], (HID, H * HD), jnp.float32) * s, 'wk': jax.random.normal(ks[2], (HID, KV * HD), jnp.float32) * s, 'wv': jax.random.normal(ks[3], (HID, KV * HD), jnp.float32) * s, 'wo': jax.random.normal(ks[4], (H * HD, HID), jnp.float32) * s}
    _L0_attn_in = _L0_attn_setup()

    def _L0_ffn_setup():
        import jax, jax.numpy as jnp
        import numpy as np
        key = jax.random.key(seed)
        k1, k2 = jax.random.split(key)
        B, S, D_IN, D_OUT = (4, 256, 512, 512)
        input = jax.random.normal(k1, (B, S, D_IN), dtype=jnp.float32)
        bound = 1.0 / np.sqrt(D_IN)
        weight = jax.random.uniform(k2, (D_OUT, D_IN), dtype=jnp.float32, minval=-bound, maxval=bound)
        scale_param = jnp.ones((D_OUT,), dtype=jnp.float32)
        return {'input': input, 'weight': weight, 'scale_param': scale_param}
    _L0_ffn_in = _L0_ffn_setup()
    _L0_c = _w((lambda *s: np.random.randn(*s).astype(np.float32) * 0.05)(4, 512))
    _L0_wmod = _w((lambda *s: np.random.randn(*s).astype(np.float32) * 0.05)(512, 6 * 512) * 512 ** (-0.5))

    def _L1_attn_setup():
        import jax, jax.numpy as jnp
        import numpy as np
        HIDDEN = 512
        NUM_HEADS = 32
        HEAD_DIM = HIDDEN // NUM_HEADS
        THRESH = 0.001
        key = jax.random.key(seed)
        ks = jax.random.split(key, 9)
        w_std = 0.02
        x = jax.random.normal(ks[0], (4, 512, HIDDEN), dtype=jnp.float32)
        Wq = jax.random.normal(ks[1], (HIDDEN, HIDDEN), dtype=jnp.float32) * w_std
        bq = jax.random.normal(ks[2], (HIDDEN,), dtype=jnp.float32) * w_std
        Wk = jax.random.normal(ks[3], (HIDDEN, HIDDEN), dtype=jnp.float32) * w_std
        bk = jax.random.normal(ks[4], (HIDDEN,), dtype=jnp.float32) * w_std
        Wv = jax.random.normal(ks[5], (HIDDEN, HIDDEN), dtype=jnp.float32) * w_std
        bv = jax.random.normal(ks[6], (HIDDEN,), dtype=jnp.float32) * w_std
        Wo = jax.random.normal(ks[7], (HIDDEN, HIDDEN), dtype=jnp.float32) * w_std
        bo = jax.random.normal(ks[8], (HIDDEN,), dtype=jnp.float32) * w_std
        return {'x': x, 'Wq': Wq, 'bq': bq, 'Wk': Wk, 'bk': bk, 'Wv': Wv, 'bv': bv, 'Wo': Wo, 'bo': bo}
    _L1_attn_in = _L1_attn_setup()

    def _L1_ffn_setup():
        import jax, jax.numpy as jnp
        import numpy as np
        R = 16
        LORA_ALPHA = 16
        SCALING = LORA_ALPHA / R
        key = jax.random.key(seed)
        kx, kr, ka = jax.random.split(key, 3)
        B, S, D, DO, E = (4, 256, 512, 512, 8)
        x = jax.random.normal(kx, (B, S, D), dtype=jnp.float32)
        bound_r = 1.0 / np.sqrt(D)
        route_w = jax.random.uniform(kr, (E, D), jnp.float32, -bound_r, bound_r)
        bound_a = 1.0 / np.sqrt(D)
        A = jax.random.uniform(ka, (E, R, D), jnp.float32, -bound_a, bound_a)
        kb = jax.random.fold_in(key, 7)
        Bw = jax.random.normal(kb, (E, DO, R), dtype=jnp.float32) * 0.02
        return {'x': x, 'route_w': route_w, 'A': A, 'Bw': Bw}
    _L1_ffn_in = _L1_ffn_setup()
    _L1_c = _w((lambda *s: np.random.randn(*s).astype(np.float32) * 0.05)(4, 512))
    _L1_wmod = _w((lambda *s: np.random.randn(*s).astype(np.float32) * 0.05)(512, 6 * 512) * 512 ** (-0.5))
    _d = {'L0_attn_x': _L0_attn_in['x'], 'L0_attn_wq': _L0_attn_in['wq'], 'L0_attn_wk': _L0_attn_in['wk'], 'L0_attn_wv': _L0_attn_in['wv'], 'L0_attn_wo': _L0_attn_in['wo'], 'L0_ffn_weight': _L0_ffn_in['weight'], 'L0_ffn_scale_param': _L0_ffn_in['scale_param'], 'L0_c': _L0_c, 'L0_wmod': _L0_wmod, 'L1_attn_Wq': _L1_attn_in['Wq'], 'L1_attn_bq': _L1_attn_in['bq'], 'L1_attn_Wk': _L1_attn_in['Wk'], 'L1_attn_bk': _L1_attn_in['bk'], 'L1_attn_Wv': _L1_attn_in['Wv'], 'L1_attn_bv': _L1_attn_in['bv'], 'L1_attn_Wo': _L1_attn_in['Wo'], 'L1_attn_bo': _L1_attn_in['bo'], 'L1_ffn_route_w': _L1_ffn_in['route_w'], 'L1_ffn_A': _L1_ffn_in['A'], 'L1_ffn_Bw': _L1_ffn_in['Bw'], 'L1_c': _L1_c, 'L1_wmod': _L1_wmod}
    _x0 = _d['L0_attn_x']
    _d['L0_attn_x'] = jax.random.normal(jax.random.fold_in(jax.random.key(seed), 1), (4, 512, 512), dtype=_x0.dtype)
    del _x0
    return _d

def reference(L0_attn_x, L0_attn_wq, L0_attn_wk, L0_attn_wv, L0_attn_wo, L0_ffn_weight, L0_ffn_scale_param, L0_c, L0_wmod, L1_attn_Wq, L1_attn_bq, L1_attn_Wk, L1_attn_bk, L1_attn_Wv, L1_attn_bv, L1_attn_Wo, L1_attn_bo, L1_ffn_route_w, L1_ffn_A, L1_ffn_Bw, L1_c, L1_wmod):

    def _L0_attn_ref(x, wq, wk, wv, wo):
        import jax, jax.numpy as jnp
        import numpy as np
        H, KV, HD, HID = (32, 8, 128, 512)
        THETA, FACTOR, HI_FF, LO_FF, ORIG_MAX = (500000.0, 8.0, 4.0, 1.0, 1024)

        def _llama3_inv_freq():
            inv = 1.0 / THETA ** (np.arange(0, HD, 2, dtype=np.float64) / HD)
            wavelen = 2.0 * np.pi / inv
            low_wl = ORIG_MAX / LO_FF
            high_wl = ORIG_MAX / HI_FF
            smooth = (ORIG_MAX / wavelen - LO_FF) / (HI_FF - LO_FF)
            scaled = np.where(wavelen > low_wl, inv / FACTOR, inv)
            mid = (wavelen <= low_wl) & (wavelen >= high_wl)
            scaled = np.where(mid, (1 - smooth) * inv / FACTOR + smooth * inv, scaled)
            return scaled.astype(np.float32)

        def _rope_cos_sin(T):
            inv = _llama3_inv_freq()
            pos = np.arange(T, dtype=np.float32)
            freqs = pos[:, None] * inv[None, :]
            emb = np.concatenate([freqs, freqs], axis=-1)
            return (jnp.asarray(np.cos(emb)), jnp.asarray(np.sin(emb)))

        def _rotate_half(x):
            x1, x2 = jnp.split(x, 2, axis=-1)
            return jnp.concatenate([-x2, x1], axis=-1)
        B, T, _ = x.shape
        q = (x @ wq).reshape(B, T, H, HD).transpose(0, 2, 1, 3)
        k = (x @ wk).reshape(B, T, KV, HD).transpose(0, 2, 1, 3)
        v = (x @ wv).reshape(B, T, KV, HD).transpose(0, 2, 1, 3)
        cos, sin = _rope_cos_sin(T)
        q = q * cos + _rotate_half(q) * sin
        k = k * cos + _rotate_half(k) * sin
        rep = H // KV
        k = jnp.repeat(k, rep, axis=1)
        v = jnp.repeat(v, rep, axis=1)
        scores = jnp.einsum('bhtd,bhsd->bhts', q, k) * (1.0 / np.sqrt(HD))
        mask = jnp.tril(jnp.ones((T, T), dtype=bool))
        scores = jnp.where(mask, scores, -jnp.inf)
        att = jax.nn.softmax(scores, axis=-1)
        out = jnp.einsum('bhts,bhsd->bhtd', att, v)
        out = out.transpose(0, 2, 1, 3).reshape(B, T, H * HD)
        return out @ wo

    def _L0_ffn_ref(input, weight, scale_param):
        import jax, jax.numpy as jnp
        import numpy as np
        row_scale = jnp.clip(jnp.mean(jnp.abs(weight), axis=1), 1e-08, None)
        binary_weight = jnp.sign(weight / row_scale[:, None])
        out = jnp.einsum('bsi,oi->bso', input, binary_weight)
        out = out * row_scale[None, None, :] * scale_param[None, None, :]
        return jnp.nan_to_num(out, nan=0.0, posinf=1000000.0, neginf=-1000000.0)

    def _L1_attn_ref(x, Wq, bq, Wk, bk, Wv, bv, Wo, bo):
        import jax, jax.numpy as jnp
        import numpy as np
        HIDDEN = 512
        NUM_HEADS = 32
        HEAD_DIM = HIDDEN // NUM_HEADS
        THRESH = 0.001
        B, S, Hd = x.shape
        H, D = (NUM_HEADS, HEAD_DIM)
        q = (x @ Wq.T + bq).reshape(B, S, H, D)
        k = (x @ Wk.T + bk).reshape(B, S, H, D)
        v = (x @ Wv.T + bv).reshape(B, S, H, D)
        inv_sqrt_d = np.float32(1.0 / np.sqrt(D))
        scores = jnp.einsum('bshd,bsgd->bshg', q, k) * inv_sqrt_d
        scores = jnp.where(scores > THRESH, scores, -jnp.inf)
        attn = jax.nn.softmax(scores, axis=-1)
        out = jnp.einsum('bshg,bsgd->bshd', attn, v).reshape(B, S, Hd)
        return out @ Wo.T + bo

    def _L1_ffn_ref(x, route_w, A, Bw):
        import jax, jax.numpy as jnp
        import numpy as np
        R = 16
        LORA_ALPHA = 16
        SCALING = LORA_ALPHA / R
        logits = jnp.einsum('bsd,ed->bse', x, route_w)
        topk_v, topk_idx = jax.lax.top_k(logits, 1)
        E = logits.shape[-1]
        route_weight = jax.nn.one_hot(topk_idx[..., 0], E, dtype=logits.dtype) * topk_v
        h = jnp.einsum('bsd,erd->bser', x, A)
        wh = route_weight[..., None] * h
        out = jnp.einsum('bser,eor->bso', wh, Bw) * SCALING
        return out
    x = L0_attn_x
    mod = (_silu(L0_c) @ L0_wmod).reshape(L0_c.shape[0], 6, 1, -1)
    sa, ca, ga, sb, cb, gb = (mod[:, 0], mod[:, 1], mod[:, 2], mod[:, 3], mod[:, 4], mod[:, 5])
    ga = (2 * (ga >= 0) - 1) * jnp.maximum(jnp.abs(ga), 0.25)
    gb = (2 * (gb >= 0) - 1) * jnp.maximum(jnp.abs(gb), 0.25)
    h = _layernorm(x, axis=-1) * (1 + ca) + sa
    x = x + ga * _L0_attn_ref(h, L0_attn_wq, L0_attn_wk, L0_attn_wv, L0_attn_wo)
    h = _layernorm(x, axis=-1) * (1 + cb) + sb
    x = x + gb * _L0_ffn_ref(h, L0_ffn_weight, L0_ffn_scale_param)
    mod = (_silu(L1_c) @ L1_wmod).reshape(L1_c.shape[0], 6, 1, -1)
    sa, ca, ga, sb, cb, gb = (mod[:, 0], mod[:, 1], mod[:, 2], mod[:, 3], mod[:, 4], mod[:, 5])
    ga = (2 * (ga >= 0) - 1) * jnp.maximum(jnp.abs(ga), 0.25)
    gb = (2 * (gb >= 0) - 1) * jnp.maximum(jnp.abs(gb), 0.25)
    h = _layernorm(x, axis=-1) * (1 + ca) + sa
    x = x + ga * _L1_attn_ref(h, L1_attn_Wq, L1_attn_bq, L1_attn_Wk, L1_attn_bk, L1_attn_Wv, L1_attn_bv, L1_attn_Wo, L1_attn_bo)
    h = _layernorm(x, axis=-1) * (1 + cb) + sb
    x = x + gb * _L1_ffn_ref(h, L1_ffn_route_w, L1_ffn_A, L1_ffn_Bw)
    return x

_drawn_inputs = setup_inputs


def setup_inputs(seed=0):
    import zlib

    import numpy as np

    out = dict(_drawn_inputs(seed))
    spreads = {'L0_ffn_scale_param': (1.0, 0.552)}
    factors = {'L1_attn_Wq': 5.976,
     'L1_attn_bq': 8.0,
     'L1_attn_Wk': 5.961,
     'L1_attn_bk': 8.0,
     'L1_attn_Wv': 4.326,
     'L1_attn_bv': 8.0,
     'L1_attn_Wo': 4.302,
     'L1_attn_bo': 8.0,
     'L1_ffn_route_w': 5.101,
     'L1_ffn_A': 4.473,
     'L1_ffn_Bw': 4.341,
     'L1_c': 2.974,
     'L1_wmod': 2.99}
    for name, (base, spread) in spreads.items():
        noise = np.random.default_rng([zlib.crc32(name.encode()), seed]).standard_normal(out[name].shape)
        drawn = base * np.exp(spread * noise) if base else spread * noise
        out[name] = jnp.asarray(drawn.astype(out[name].dtype))
    for name, factor in factors.items():
        out[name] = (out[name] * factor).astype(out[name].dtype)
    return out
```

```python
from contextlib import ExitStack

import numpy as np
import concourse.bass as bass
from concourse import mybir

F32 = mybir.dt.float32
F32R = mybir.dt.float32r
I32 = mybir.dt.int32
ALU = mybir.AluOpType
ACT = mybir.ActivationFunctionType
AX = mybir.AxisListType

P = 128
B, T, D = 4, 512, 512
KT = D // P
HB = 2
NT = HB * T // P
TT = T // P
G, R0, HD = 8, 4, 128
H1, D1 = 32, 16
THRESH = 0.001
NE, R1 = 8, 16
EPS = 1e-5
MASKED = -1e30
MAGIC = 0x5F3759DF
LIMIT = 1000000.0
FIRST_SEM = 160


def tables():
    inv = 1.0 / 500000.0 ** (np.arange(0, HD, 2, dtype=np.float64) / HD)
    wave = 2.0 * np.pi / inv
    low, high = 1024 / 1.0, 1024 / 4.0
    smooth = (1024 / wave - 1.0) / (4.0 - 1.0)
    scaled = np.where(wave > low, inv / 8.0, inv)
    mid = (wave <= low) & (wave >= high)
    scaled = np.where(mid, (1 - smooth) * inv / 8.0 + smooth * inv, scaled).astype(np.float32)
    freqs = np.arange(T, dtype=np.float32)[:, None] * scaled[None, :]
    emb = np.concatenate([freqs, freqs], axis=-1)
    cos, sin = np.cos(emb).T, np.sin(emb).T
    sign = np.where(np.arange(HD) < HD // 2, -1.0, 1.0).astype(np.float32)[:, None]
    mask = np.where(np.arange(P)[None, :] <= np.arange(P)[:, None], 0.0, MASKED)
    ranks = np.broadcast_to(8.0 - np.arange(NE), (P, NE))
    parts = [cos, sin * sign, np.eye(P), mask, ranks]
    return np.ascontiguousarray(np.concatenate([p.astype(np.float32) for p in parts], axis=1))


class Stage:

    def __init__(self, nc, name):
        self.nc, self.name, self.ctx, self.sems = nc, name, ExitStack(), []

    def __enter__(self):
        return self

    def sb(self, name, shape, dt=F32):
        return self.ctx.enter_context(self.nc.sbuf_tensor(f"{self.name}_{name}", shape, dt))

    def ps(self, name, shape):
        return self.ctx.enter_context(self.nc.psum_tensor(f"{self.name}_{name}", shape, F32))

    def sem(self, name):
        s = self.ctx.enter_context(self.nc.semaphore(f"{self.name}_{name}", num=FIRST_SEM + len(self.sems)))
        self.sems.append(s.num)
        return s

    def __exit__(self, *e):
        if e[0] is None:
            self.nc.all_engine_barrier(sems_to_clear=range(self.sems[0], self.sems[-1] + 1))
        return self.ctx.__exit__(*e)


class Held:
    pass


def stage_modulation(nc, held, a):
    with Stage(nc, "mod") as st:
        consts = held.consts
        cT = st.sb("cT", [P, KT, 2 * B])
        ec = st.sb("ec", [P, KT, 2 * B])
        silu = st.sb("silu", [P, KT, 2 * B])
        wm = [st.sb(f"wm{l}", [P, KT, 6 * D]) for l in range(2)]
        gate = st.sb("gate", [B, 4, D])
        gabs = st.sb("gabs", [B, 4, D])
        gsgn = st.sb("gsgn", [B, 4, D])
        w = st.sb("w", [P, KT, D])
        sp = st.sb("sp", [P, KT])
        rs = st.sb("rs", [P, KT])
        pc = [st.ps(f"pc{l}", [P, 4, KT, B]) for l in range(2)]
        pg = [st.ps(f"pg{i}", [B, D]) for i in range(4)]
        const_in = st.sem("const_in")
        c_in = st.sem("c_in")
        wm_in = [st.sem(f"wm_in{l}") for l in range(2)]
        w_in = st.sem("w_in")
        c_exp = st.sem("c_exp")
        silu_step = st.sem("silu_step")
        silu_done = st.sem("silu_done")
        col_full = st.sem("col_full")
        gate_full = st.sem("gate_full")
        gate_step = st.sem("gate_step")
        held_done = st.sem("held_done")
        gate_copied = st.sem("gate_copied")
        rows_out = st.sem("rows_out")
        CH = [0, 1, 3, 4]
        GT = [2, 5]
        with nc.Block() as block:

            @block.sync
            def _(sp_):
                for l, c in enumerate((a["c0T"], a["c1T"])):
                    sp_.dma_start(cT[:, :, l * B:(l + 1) * B],
                                  c.rearrange("(k p) b -> p k b", p=P)).then_inc(c_in, 16)
                for l, m in enumerate((a["wmod0"], a["wmod1"])):
                    sp_.dma_start(wm[l][:], m.rearrange("(k p) n -> p k n", p=P)).then_inc(wm_in[l], 16)
                sp_.wait_ge(gate_step, 5)
                sp_.dma_start(a["gates"].rearrange("g b d -> b g d"), gate[:]).then_inc(rows_out, 16)
                sp_.wait_ge(rows_out, 32)

            @block.scalar
            def _(act):
                act.dma_start(held.consts[:], a["tables"]).then_inc(const_in, 16)
                act.dma_start(w[:], a["w_sign"].rearrange("(k p) n -> p k n", p=P)).then_inc(w_in, 16)
                act.dma_start(sp[:], a["scale_param"]).then_inc(w_in, 16)
                act.wait_ge(c_in, 32)
                nc.scalar.activation(ec[:], cT[:], ACT.Exp, scale=-1.0).then_inc(c_exp, 1)
                act.wait_ge(gate_step, 6)
                act.dma_start(a["row_scale"].rearrange("(k p) -> p k", p=P), rs[:], allow_slow_non_contiguous=True).then_inc(rows_out, 16)
                act.wait_ge(const_in, 16)

            @block.tensor
            def _(pe):
                pe.wait_ge(silu_done, 1)
                for l in range(2):
                    pe.wait_ge(wm_in[l], 16)
                    for ci, c in enumerate(CH):
                        for m in range(KT):
                            for k in range(KT):
                                mm = pe.matmul(pc[l][:, ci, m, :], wm[l][:, k, c * D + m * P:c * D + (m + 1) * P],
                                               silu[:, k, l * B:(l + 1) * B], start=(k == 0), stop=(k == KT - 1))
                    mm.then_inc(col_full, 1)
                    for gi, g in enumerate(GT):
                        for k in range(KT):
                            mm = pe.matmul(pg[2 * l + gi][:], silu[:, k, l * B:(l + 1) * B],
                                           wm[l][:, k, g * D:(g + 1) * D], start=(k == 0), stop=(k == KT - 1))
                        mm.then_inc(gate_full, 1)

            @block.vector
            def _(dve):
                dve.wait_ge(c_exp, 1)
                nc.vector.tensor_scalar_add(ec[:], ec[:], 1.0).then_inc(silu_step, 1)
                dve.wait_ge(silu_step, 1)
                nc.vector.reciprocal(ec[:], ec[:]).then_inc(silu_step, 1)
                dve.wait_ge(silu_step, 2)
                nc.vector.tensor_tensor(silu[:], cT[:], ec[:], ALU.mult).then_inc(silu_done, 1)
                dve.wait_ge(const_in, 16)
                nc.vector.tensor_copy(held.identr[:], held.ident).then_inc(held_done, 1)
                nc.vector.tensor_copy(held.maskr[:], held.mask).then_inc(held_done, 1)
                dve.wait_ge(w_in, 32)
                nc.vector.tensor_reduce(rs[:], w[:], AX.X, ALU.add, apply_absolute_value=True).then_inc(silu_step, 1)
                dve.wait_ge(silu_step, 3)
                nc.vector.tensor_scalar(rs[:], rs[:], 1.0 / D, 1e-8, ALU.mult, ALU.max).then_inc(silu_step, 1)
                dve.wait_ge(silu_step, 4)
                nc.vector.tensor_tensor(rs[:], rs[:], sp[:], ALU.mult).then_inc(silu_step, 1)
                for l in range(2):
                    dve.wait_ge(col_full, l + 1)
                    for ci in range(4):
                        nc.vector.tensor_scalar(held.modT[:, l, ci, :, :], pc[l][:, ci, :, :],
                                                float(ci % 2), None, ALU.add).then_inc(held_done, 1)
                for i in range(4):
                    dve.wait_ge(gate_full, i + 1)
                    nc.vector.tensor_copy(gate[:, i, :], pg[i][:]).then_inc(gate_copied, 1)
                dve.wait_ge(gate_copied, 4)
                nc.vector.scalar_tensor_tensor(gabs[:], gate[:], -1.0, gate[:], ALU.mult, ALU.max).then_inc(gate_step, 1)
                nc.vector.tensor_scalar(gsgn[:], gate[:], 0.0, 2.0, ALU.is_ge, ALU.mult).then_inc(gate_step, 1)
                dve.wait_ge(gate_step, 2)
                nc.vector.tensor_scalar_max(gabs[:], gabs[:], 0.25).then_inc(gate_step, 1)
                nc.vector.tensor_scalar_add(gsgn[:], gsgn[:], -1.0).then_inc(gate_step, 1)
                dve.wait_ge(gate_step, 4)
                nc.vector.tensor_tensor(gate[:], gabs[:], gsgn[:], ALU.mult).then_inc(gate_step, 1)
                dve.wait_ge(silu_step, 5)
                nc.vector.tensor_copy(sp[:], rs[:]).then_inc(gate_step, 1)


def stage_norm(nc, held, a, layer, which, half, residual=None, weights=None):
    with Stage(nc, f"ln{layer}{which}") as st:
        x, y, hh, hl = held.x, held.y, held.hh, held.hl
        xn = st.sb("xn", [P, NT, D])
        hf = st.sb("hf", [P, HB * KT, T])
        gate = st.sb("gate", [P, HB, D]) if residual is not None else None
        stats = st.sb("stats", [P, NT, 6])
        mv = st.sb("mv", [P, NT, 2])
        var = st.sb("var", [P, NT])
        rstd = st.sb("rstd", [P, NT])
        step = st.sb("step", [P, NT])
        pT = [st.ps(f"pT{i}", [P, T]) for i in range(HB * KT)]
        x_in = [st.sem(f"x_in{b}") for b in range(HB)]
        gate_in = st.sem("gate_in")
        gated = st.sem("gated")
        x_new = st.sem("x_new")
        stat_done = st.sem("stat_done")
        newton = st.sem("newton")
        xn_done = st.sem("xn_done")
        turned = st.sem("turned")
        scaled = st.sem("scaled")
        hi_done = st.sem("hi_done")
        lo_done = st.sem("lo_done")
        split_w = st.sem("split_w")
        w_in = st.sem("w_in")
        y_clear = st.sem("y_clear")
        ci = 2 * which
        with nc.Block() as block:

            @block.sync
            def _(sp):
                if residual is None:
                    for b in range(HB):
                        sp.dma_start(x[:, b * TT:(b + 1) * TT, :],
                                     a["x"][bass.ds(half * HB * T + b * T, T), :].rearrange("(j p) d -> p j d", p=P)
                                     ).then_inc(x_in[b], 16)
                else:
                    for b in range(HB):
                        sp.dma_start(gate[:, b, :], a["gates"][residual, bass.ds(half * HB + b, 1), :]
                                     .to_broadcast([P, D])).then_inc(gate_in, 16)
                if weights:
                    weights.load(sp, w_in, 0)

            @block.gpsimd
            def _(pool):
                if residual is not None:
                    pool.wait_ge(gate_in, 16 * HB)
                    for j in range(NT):
                        nc.gpsimd.tensor_tensor(y[:, j, :], y[:, j, :], gate[:, j // TT, :], ALU.mult).then_inc(gated, 1)
                if weights:
                    nc.gpsimd.memset(y[:], 0.0).then_inc(y_clear, 1)
                    pool.wait_ge(w_in, 48)
                    weights.split_all(pool, split_w)
                for i in range(HB * KT):
                    b, k = i // KT, i % KT
                    pool.wait_ge(hi_done, i + 1)
                    nc.gpsimd.tensor_tensor(hl[:, k, b * T:(b + 1) * T], hf[:, i, :], hh[:, k, b * T:(b + 1) * T],
                                            ALU.subtract).then_inc(lo_done, 1)

            @block.vector
            def _(dve):
                for j in range(NT):
                    if residual is None:
                        dve.wait_ge(x_in[j // TT], 16)
                    else:
                        dve.wait_ge(gated, j + 1)
                        nc.vector.tensor_tensor(x[:, j, :], x[:, j, :], y[:, j, :], ALU.add).then_inc(x_new, 1)
                for j in range(NT):
                    if residual is not None:
                        dve.wait_ge(x_new, j + 1)
                    nc.vector.bn_stats(stats[:, j, :], x[:, j, :]).then_inc(stat_done, 1)
                for j in range(NT):
                    dve.wait_ge(stat_done, j + 1)
                    nc.vector.bn_aggr(mv[:, j, :], stats[:, j, :]).then_inc(stat_done, 1)
                dve.wait_ge(stat_done, 2 * NT)
                n = [0]

                def link(ins):
                    n[0] += 1
                    ins.then_inc(newton, 1)
                    dve.wait_ge(newton, n[0])

                link(nc.vector.tensor_scalar(var[:], mv[:, :, 1], EPS, None, ALU.add))
                link(nc.vector.tensor_scalar(step[:].bitcast(I32), var[:].bitcast(I32), 1, None, ALU.logical_shift_right))
                link(nc.vector.tensor_scalar(rstd[:].bitcast(I32), step[:].bitcast(I32), -1.0, float(MAGIC), ALU.mult, ALU.add))
                for _ in range(4):
                    link(nc.vector.tensor_tensor(step[:], rstd[:], rstd[:], ALU.mult))
                    link(nc.vector.tensor_tensor(step[:], step[:], var[:], ALU.mult))
                    link(nc.vector.tensor_scalar(step[:], step[:], -0.5, 1.5, ALU.mult, ALU.add))
                    link(nc.vector.tensor_tensor(rstd[:], rstd[:], step[:], ALU.mult))
                for j in range(NT):
                    nc.vector.tensor_scalar(xn[:, j, :], x[:, j, :], mv[:, j, 0:1], rstd[:, j:j + 1],
                                            ALU.subtract, ALU.mult).then_inc(xn_done, 1)
                for i in range(HB * KT):
                    b, k = i // KT, i % KT
                    dve.wait_ge(scaled, i + 1)
                    nc.vector.tensor_copy(hh[:, k, b * T:(b + 1) * T], hf[:, i, :]).then_inc(hi_done, 1)

            @block.tensor
            def _(pe):
                for b in range(HB):
                    for j in range(TT):
                        pe.wait_ge(xn_done, b * TT + j + 1)
                        for k in range(KT):
                            mm = pe.transpose(pT[b * KT + k][:, j * P:(j + 1) * P], xn[:, b * TT + j, k * P:(k + 1) * P],
                                              held.ident)
                    mm.then_inc(turned, 1)

            @block.scalar
            def _(act):
                for i in range(HB * KT):
                    b, k = i // KT, i % KT
                    act.wait_ge(turned, b + 1)
                    nc.scalar.activation(hf[:, i, :], pT[i][:], ACT.Identity,
                                         bias=held.modh[:, layer, ci, k, b:b + 1],
                                         scale=held.modh[:, layer, ci + 1, k, b:b + 1]).then_inc(scaled, 1)


def stage_half_mod(nc, held, half):
    with Stage(nc, "hm") as st:
        done = st.sem("done")
        with nc.Block() as block:
            @block.vector
            def _(dve):
                nc.vector.tensor_copy(held.modh[:].rearrange("p l c k b -> p (l c k) b"),
                                      held.modT[:].rearrange("p l c k b -> p (l c k) b")[:, :, bass.ds(half * HB, HB)]
                                      ).then_inc(done, 1)


class GroupWeights:

    def __init__(self, ctx, nc, a):
        sb = lambda n, s, dt=F32: ctx.enter_context(nc.sbuf_tensor(n, s, dt))
        QW = R0 * HD
        self.nc, self.a = nc, a
        self.raw_q, self.raw_kv, self.raw_o = sb("raw_q", [P, KT, QW]), sb("raw_kv", [P, 2, KT, HD]), sb("raw_o", [P, R0, D])
        self.qh, self.ql = sb("wqh", [P, KT, QW], F32R), sb("wql", [P, KT, QW], F32R)
        self.kvh, self.kvl = sb("wkvh", [P, 2, KT, HD], F32R), sb("wkvl", [P, 2, KT, HD], F32R)
        self.oh, self.ol = sb("woh", [P, R0, D], F32R), sb("wol", [P, R0, D], F32R)

    def load(self, eng, sem, g):
        self.load_qkv(eng, sem, g)
        self.load_o(eng, sem, g)

    def load_qkv(self, eng, sem, g):
        QW = R0 * HD
        eng.dma_start(self.raw_q[:], self.a["wq"][:, bass.ds(g * QW, QW)].rearrange("(k p) n -> p k n", p=P)).then_inc(sem, 16)
        eng.dma_start(self.raw_kv[:], self.a["wkv"][:, :, bass.ds(g * HD, HD)].rearrange("w (k p) n -> p w k n", p=P)).then_inc(sem, 16)

    def load_o(self, eng, sem, g):
        QW = R0 * HD
        eng.dma_start(self.raw_o[:], self.a["wo"][bass.ds(g * QW, QW), :].rearrange("(h p) n -> p h n", p=P)).then_inc(sem, 16)

    def parts(self, what, i):
        if what == "q":
            s = slice(i * HD, (i + 1) * HD)
            return self.raw_q[:, :, s], self.qh[:, :, s], self.ql[:, :, s]
        if what == "kv":
            return self.raw_kv[:, i], self.kvh[:, i], self.kvl[:, i]
        return self.raw_o[:, 2 * i:2 * i + 2], self.oh[:, 2 * i:2 * i + 2], self.ol[:, 2 * i:2 * i + 2]

    def split(self, pool, sem, before, what, i):
        raw, hi, lo = self.parts(what, i)
        self.nc.gpsimd.tensor_copy(hi, raw).then_inc(sem, 1)
        pool.wait_ge(sem, before + 1)
        self.nc.gpsimd.tensor_tensor(lo, raw, hi, ALU.subtract).then_inc(sem, 1)

    def split_all(self, pool, sem):
        order = [("kv", 0), ("kv", 1)] + [("q", i) for i in range(R0)]
        for n, (what, i) in enumerate(order):
            self.split(pool, sem, 2 * n, what, i)


PROJ = [("K", 0), ("V", 0), ("Q", 0), ("Q", 1), ("Q", 2), ("Q", 3), ("K", 1), ("Q", 4), ("V", 1), ("Q", 5), ("Q", 6), ("Q", 7)]
STEP_PROJ = [[4], [5], [6, 7], [8, 9], [10], [11], [], []]
NH = HB * R0
ROPE = [e for e, (kind, _) in enumerate(PROJ) if kind != "V"]
S_AT = [(0, 0), (1, 0), (0, P), (2, 0)]
S_OF = [[0, 2], [1], [3]]
P_OFF = [P * i * (i + 1) // 2 for i in range(TT)]
PT_OFF = [0, 4 * P, 8 * P, 7 * P]


def stage_group(nc, held, a, wts, gnext):
    QS = HD ** -0.5
    with Stage(nc, "gqa") as st:
        hh, hl, y = held.hh, held.hl, held.y
        kh = [st.sb(f"kh{b}", [P, T], F32R) for b in range(HB)]
        kl = [st.sb(f"kl{b}", [P, T], F32R) for b in range(HB)]
        vh = [st.sb(f"vh{b}", [P, T], F32R) for b in range(HB)]
        vl = [st.sb(f"vl{b}", [P, T], F32R) for b in range(HB)]
        qh = [st.sb(f"qh{i}", [P, T], F32R) for i in range(2)]
        ql = [st.sb(f"ql{i}", [P, T], F32R) for i in range(2)]
        rot = [st.sb(f"rot{i}", [P, T]) for i in range(2)]
        full = [st.sb(f"full{i}", [P, T]) for i in range(2)]
        prob = [st.sb(f"prob{i}", [P, 10 * P]) for i in range(2)]
        pth, ptl = st.sb("pth", [P, 10 * P], F32R), st.sb("ptl", [P, 10 * P], F32R)
        oh = [st.sb(f"oh{i}", [P, T], F32R) for i in range(4)]
        ol = [st.sb(f"ol{i}", [P, T], F32R) for i in range(4)]
        nmax = [st.sb(f"nmax{i}", [P, TT]) for i in range(2)]
        den = [st.sb(f"den{i}", [P, TT]) for i in range(2)]
        rden = [st.sb(f"rden{i}", [P, TT]) for i in range(2)]
        pj = st.ps("pj", [P, T])
        pS = [st.ps(f"pS{i}", [P, T]) for i in range(3)]
        pT = [st.ps(f"pT{i}", [P, T]) for i in range(2)]
        pO, pW = st.ps("pO", [P, T]), st.ps("pW", [P, D])
        qkv_in, wo_in = st.sem("qkv_in"), st.sem("wo_in")
        proj_full = st.sem("proj_full")
        rotated, cosed = st.sem("rotated"), st.sem("cosed")
        v_hi, v_lo = st.sem("v_hi"), st.sem("v_lo")
        sined, roped, rope_hi, rope_lo = st.sem("sined"), st.sem("roped"), st.sem("rope_hi"), st.sem("rope_lo")
        s_full, max_done, exp_done = st.sem("s_full"), st.sem("max_done"), st.sem("exp_done")
        recip, normed = st.sem("recip"), st.sem("normed")
        pt_full, pt_hi, pt_lo = st.sem("pt_full"), st.sem("pt_hi"), st.sem("pt_lo")
        o_full, o_hi, o_lo = st.sem("o_full"), st.sem("o_hi"), st.sem("o_lo")
        w_full, w_added = st.sem("w_full"), st.sem("w_added")
        wo_split, next_split = st.sem("wo_split"), st.sem("next_split")
        bank = [pj] * len(PROJ)
        bank[1], bank[2] = pW, pO
        NTILES = NH // 2 * TT

        def wbank(d):
            return pO if d >= NTILES - TT and d % 2 else pW

        with nc.Block() as block:

            @block.sync
            def _(sp):
                wts.load_qkv(sp, qkv_in, gnext)
                sp.wait_ge(wo_split, 4)
                wts.load_o(sp, wo_in, gnext)
                sp.wait_ge(wo_in, 16)

            @block.tensor
            def _(pe):
                def free(e):
                    kind = PROJ[e][0]
                    if kind == "V":
                        pe.wait_ge(v_lo, 1 + PROJ[e][1])
                    else:
                        pe.wait_ge(cosed, ROPE.index(e) + 1)

                def project(e):
                    kind, i = PROJ[e]
                    if e == 3:
                        free(0)
                    elif e > 3:
                        free(e - 1)
                    out = bank[e]
                    if kind == "V":
                        for j in range(TT):
                            t = slice(i * T + j * P, i * T + (j + 1) * P)
                            n = 0
                            for k in range(KT):
                                for hp, wp in ((hh, wts.kvh), (hh, wts.kvl), (hl, wts.kvh)):
                                    mm = pe.matmul(out[:, j * P:(j + 1) * P], hp[:, k, t], wp[:, 1, k, :],
                                                   start=(n == 0), stop=(n == 3 * KT - 1))
                                    n += 1
                    else:
                        b = i if kind == "K" else i // R0
                        t = slice(b * T, (b + 1) * T)
                        n = 0
                        for k in range(KT):
                            if kind == "K":
                                wh, wl = wts.kvh[:, 0, k, :], wts.kvl[:, 0, k, :]
                            else:
                                c = slice((i % R0) * HD, (i % R0 + 1) * HD)
                                wh, wl = wts.qh[:, k, c], wts.ql[:, k, c]
                            for wp, hp in ((wh, hh), (wh, hl), (wl, hh)):
                                mm = pe.matmul(out[:], wp, hp[:, k, t], start=(n == 0), stop=(n == 3 * KT - 1))
                                n += 1
                    mm.then_inc(proj_full, 1)

                def scores(n):
                    b, r = n // R0, n % 2
                    pe.wait_ge(rope_lo, ROPE.index(PROJ.index(("Q", n))) + 1)
                    pe.wait_ge(rope_lo, ROPE.index(PROJ.index(("K", b))) + 1)
                    for s, tiles in enumerate(S_OF):
                        if n:
                            pe.wait_ge(exp_done, 3 * (n - 1) + s + 1)
                        for i in tiles:
                            w, c = (i + 1) * P, S_AT[i][1]
                            t = slice(i * P, (i + 1) * P)
                            out = pS[s][:, c:c + w]
                            pe.matmul(out, qh[r][:, t], kh[b][:, 0:w], start=True, stop=False)
                            pe.matmul(out, qh[r][:, t], kl[b][:, 0:w], start=False, stop=False)
                            pe.matmul(out, ql[r][:, t], kh[b][:, 0:w], start=False, stop=False)
                            mm = pe.matmul(pS[s][:, c + w - P:c + w], held.identr[:], held.maskr[:], start=False, stop=True)
                        mm.then_inc(s_full, 1)

                def turn(n, jobs):
                    for k, js in jobs:
                        if 3 * n + k >= 2:
                            pe.wait_ge(pt_lo, 3 * n + k - (1 if k == 0 else 2) if k < 2 else 3 * n + 1)
                        for j in js:
                            for i in range(j, TT):
                                c = (PT_OFF[j] + (i - j) * P) % T
                                mm = pe.transpose(pT[k % 2][:, c:c + P],
                                                  prob[n % 2][:, P_OFF[i] + j * P:P_OFF[i] + (j + 1) * P], held.ident)
                        mm.then_inc(pt_full, 1)

                def weigh(n, b):
                    if n == 0:
                        pe.wait_ge(cosed, 2)
                    else:
                        pe.wait_ge(o_lo, n)
                    pe.wait_ge(v_lo, b + 1)
                    m = 0
                    for j, k in ((0, 0), (1, 1), (3, 1), (2, 2)):
                        pe.wait_ge(pt_lo, 3 * n + k + 1)
                        w = (TT - j) * P
                        v = slice(j * P, (j + 1) * P)
                        pc = slice(PT_OFF[j], PT_OFF[j] + w)
                        for vp, pp in ((vh, pth), (vh, ptl), (vl, pth)):
                            mm = pe.matmul(pO[:, T - w:], vp[b][:, v], pp[:, pc], start=(m == 0), stop=(m == 11))
                            m += 1
                    mm.then_inc(o_full, 1)

                def out_proj(d):
                    pair, i = d // TT, d % TT
                    if d == 0:
                        pe.wait_ge(v_lo, 1)
                        pe.wait_ge(wo_split, 4)
                    if i == 0:
                        pe.wait_ge(o_lo, 2 * pair + 2)
                    if d:
                        pe.wait_ge(w_added, d if wbank(d) is wbank(d - 1) else d - 1)
                    t = slice(i * P, (i + 1) * P)
                    m = 0
                    for h in (2 * pair, 2 * pair + 1):
                        for op, wp in ((oh, wts.oh), (oh, wts.ol), (ol, wts.oh)):
                            mm = pe.matmul(wbank(d)[:], op[h % 4][:, t], wp[:, h % R0, :], start=(m == 0), stop=(m == 5))
                            m += 1
                    mm.then_inc(w_full, 1)

                for e in range(4):
                    project(e)
                scores(0)
                for n in range(NH):
                    pe.wait_ge(normed, n + 1)
                    turn(n, ((0, (0,)), (1, (1, 3))))
                    if n + 1 < NH:
                        scores(n + 1)
                    for e in STEP_PROJ[n]:
                        project(e)
                    turn(n, ((2, (2,)),))
                    weigh(n, n // R0)
                    if n >= 2:
                        out_proj(2 * (n - 2))
                        out_proj(2 * (n - 2) + 1)
                for d in range(NTILES - TT, NTILES):
                    out_proj(d)

            @block.scalar
            def _(act):
                def leave(e):
                    kind, i = PROJ[e]
                    act.wait_ge(proj_full, e + 1)
                    if kind == "V":
                        nc.scalar.copy(vh[i][:], bank[e][:]).then_inc(v_hi, 1)
                        return
                    r = ROPE.index(e)
                    if r >= 2:
                        act.wait_ge(rope_lo, r - 1)
                    scale = QS if kind == "Q" else 1.0
                    nc.scalar.mul(rot[r % 2][0:64, :], bank[e][64:128, :], scale).then_inc(rotated, 1)
                    nc.scalar.mul(rot[r % 2][64:128, :], bank[e][0:64, :], scale).then_inc(rotated, 1)

                def exps(n):
                    r = n % 2
                    for s, tiles in enumerate(S_OF):
                        act.wait_ge(max_done, 4 * n + (2, 3, 4)[s])
                        if n >= 2 and s == 0:
                            act.wait_ge(pt_full, 3 * (n - 1))
                            act.wait_ge(recip, n - 1)
                        for i in tiles:
                            w, c = (i + 1) * P, S_AT[i][1]
                            ins = nc.scalar.activation(prob[r][:, P_OFF[i]:P_OFF[i] + w], pS[s][:, c:c + w], ACT.Exp,
                                                       bias=nmax[r][:, i:i + 1], accum_out=den[r][:, i:i + 1])
                        ins.then_inc(exp_done, 1)

                def pt_his(n, ks):
                    for k in ks:
                        act.wait_ge(pt_full, 3 * n + k + 1)
                        if n:
                            act.wait_ge(o_full, n)
                        c, w = ((0, 4 * P), (4 * P, 4 * P), (8 * P, 2 * P))[k]
                        nc.scalar.copy(pth[:, c:c + w], pT[k % 2][:, 0:w]).then_inc(pt_hi, 1)

                for e in range(4):
                    leave(e)
                exps(0)
                for n in range(NH):
                    pt_his(n, (0, 1))
                    if n + 1 < NH:
                        exps(n + 1)
                    for e in STEP_PROJ[n]:
                        leave(e)
                    pt_his(n, (2,))
                    act.wait_ge(o_full, n + 1)
                    if n >= 4:
                        act.wait_ge(w_full, 4 * ((n - 4) // 2) + 4)
                    nc.scalar.copy(oh[n % 4][:], pO[:]).then_inc(o_hi, 1)

            @block.vector
            def _(dve):
                def leave(e):
                    kind, i = PROJ[e]
                    if kind == "V":
                        dve.wait_ge(v_hi, i + 1)
                        nc.vector.tensor_tensor(vl[i][:], bank[e][:], vh[i][:].bitcast(F32), ALU.subtract).then_inc(v_lo, 1)
                        return
                    r = ROPE.index(e)
                    dve.wait_ge(rotated, 2 * r + 2)
                    scale = QS if kind == "Q" else 1.0
                    nc.vector.scalar_tensor_tensor(full[r % 2][:], bank[e][:], scale, held.cosT, ALU.mult,
                                                   ALU.mult).then_inc(cosed, 1)

                def rope_parts(e):
                    kind, i = PROJ[e]
                    if kind == "V":
                        return
                    r = ROPE.index(e)
                    dve.wait_ge(roped, r + 1)
                    if kind == "Q" and i >= 2:
                        dve.wait_ge(s_full, 3 * (i - 1))
                    dst = kh[i] if kind == "K" else qh[i % 2]
                    nc.vector.tensor_copy(dst[:], full[r % 2][:]).then_inc(rope_hi, 1)

                def maxes(n):
                    r = n % 2
                    if n >= 2:
                        dve.wait_ge(exp_done, 3 * (n - 1))
                    for s, tiles in enumerate(S_OF):
                        dve.wait_ge(s_full, 3 * n + s + 1)
                        for i in tiles:
                            w, c = (i + 1) * P, S_AT[i][1]
                            nc.vector.tensor_reduce(nmax[r][:, i:i + 1], pS[s][:, c:c + w], AX.X, ALU.max,
                                                    negate=True).then_inc(max_done, 1)

                def pt_los(n, ks):
                    for k in ks:
                        dve.wait_ge(pt_hi, 3 * n + k + 1)
                        c, w = ((0, 4 * P), (4 * P, 4 * P), (8 * P, 2 * P))[k]
                        nc.vector.tensor_tensor(ptl[:, c:c + w], pT[k % 2][:, 0:w], pth[:, c:c + w].bitcast(F32),
                                                ALU.subtract).then_inc(pt_lo, 1)

                def recips(n):
                    dve.wait_ge(exp_done, 3 * n + 3)
                    if n >= 2:
                        dve.wait_ge(normed, n - 1)
                    nc.vector.reciprocal(rden[n % 2][:], den[n % 2][:]).then_inc(recip, 1)

                def add(d):
                    dve.wait_ge(w_full, d + 1)
                    if d >= TT:
                        dve.wait_ge(w_added, d - TT + 1)
                    j = (d // (2 * TT)) * TT + d % TT
                    nc.vector.tensor_tensor(y[:, j, :], wbank(d)[:], y[:, j, :], ALU.add).then_inc(w_added, 1)

                for e in range(4):
                    leave(e)
                    if e >= 2:
                        rope_parts(e - 2)
                rope_parts(2)
                rope_parts(3)
                maxes(0)
                recips(0)
                for n in range(NH):
                    pt_los(n, (0, 1))
                    if n + 1 < NH:
                        maxes(n + 1)
                    for e in STEP_PROJ[n]:
                        leave(e)
                        if len(STEP_PROJ[n]) > 1 and e == STEP_PROJ[n][0]:
                            rope_parts(e)
                    pt_los(n, (2,))
                    if n + 1 < NH:
                        recips(n + 1)
                    for e in STEP_PROJ[n][-1:]:
                        rope_parts(e)
                    dve.wait_ge(o_hi, n + 1)
                    nc.vector.tensor_tensor(ol[n % 4][:], pO[:], oh[n % 4][:].bitcast(F32), ALU.subtract).then_inc(o_lo, 1)
                    if n >= 2:
                        add(2 * (n - 2))
                        add(2 * (n - 2) + 1)
                for d in range(NTILES - TT, NTILES):
                    add(d)

            @block.gpsimd
            def _(pool):
                def rope(e):
                    kind, i = PROJ[e]
                    if kind == "V":
                        return
                    r = ROPE.index(e)
                    pool.wait_ge(rotated, 2 * r + 2)
                    nc.gpsimd.tensor_tensor(rot[r % 2][:], rot[r % 2][:], held.sinT, ALU.mult).then_inc(sined, 1)
                    pool.wait_ge(sined, r + 1)
                    pool.wait_ge(cosed, r + 1)
                    nc.gpsimd.tensor_tensor(full[r % 2][:], full[r % 2][:], rot[r % 2][:], ALU.add).then_inc(roped, 1)

                def rope_lo_part(e):
                    kind, i = PROJ[e]
                    if kind == "V":
                        return
                    r = ROPE.index(e)
                    pool.wait_ge(rope_hi, r + 1)
                    hi, lo = (kh[i], kl[i]) if kind == "K" else (qh[i % 2], ql[i % 2])
                    nc.gpsimd.tensor_tensor(lo[:], full[r % 2][:], hi[:].bitcast(F32), ALU.subtract).then_inc(rope_lo, 1)

                def norms(n):
                    pool.wait_ge(recip, n + 1)
                    for i in range(TT):
                        p = prob[n % 2][:, P_OFF[i]:P_OFF[i] + (i + 1) * P]
                        ins = nc.gpsimd.tensor_scalar(p, p, rden[n % 2][:, i:i + 1], 1.0, ALU.mult, ALU.mult)
                    ins.then_inc(normed, 1)

                rope(0)
                rope_lo_part(0)
                rope(2)
                rope_lo_part(2)
                rope(3)
                rope_lo_part(3)
                norms(0)
                for i in range(2):
                    wts.split(pool, wo_split, 2 * i, "o", i)
                pool.wait_ge(qkv_in, 32)
                done = 0
                for n in range(NH):
                    for e in STEP_PROJ[n]:
                        rope(e)
                        rope_lo_part(e)
                    if n + 1 < NH:
                        norms(n + 1)
                    for what, i, e in (("kv", 0, 6), ("q", 0, 7), ("kv", 1, 8), ("q", 1, 9), ("q", 2, 10), ("q", 3, 11)):
                        if e in (STEP_PROJ[n - 1] if n else []):
                            pool.wait_ge(proj_full, e + 1)
                            wts.split(pool, next_split, done, what, i)
                            done += 2


def stage_sign_ffn(nc, held, a):
    with Stage(nc, "ffn0") as st:
        wT = st.sb("wT", [P, KT, D])
        neg = st.sb("neg", [P, KT, D])
        sgn = st.sb("sgn", [P, KT, D], F32R)
        rs = st.sb("rs", [P, D])
        z = held.y
        clip = st.sb("clip", [P, NT, D])
        same = st.sb("same", [P, NT, D])
        wild = st.sb("wild", [P, NT, D], I32)
        ps = [st.ps(f"ps{i}", [P, D]) for i in range(NT)]
        w_in, rs_in = st.sem("w_in"), st.sem("rs_in")
        negs, signs = st.sem("negs"), st.sem("signs")
        full, scaled, clipped, equal, zeroed, marked, put = (st.sem(n) for n in
                                                             ("full", "scaled", "clipped", "equal", "zeroed", "marked", "put"))
        with nc.Block() as block:

            @block.sync
            def _(sp):
                sp.dma_start(wT[:], a["w_signT"].rearrange("(k p) n -> p k n", p=P)).then_inc(w_in, 16)
                sp.dma_start(rs[:], a["row_scale"].rearrange("(o d) -> o d", o=1).to_broadcast([P, D])).then_inc(rs_in, 16)

            @block.tensor
            def _(pe):
                for j in range(NT):
                    pe.wait_ge(signs, KT)
                    for k in range(KT):
                        for n, hp in enumerate((held.hh, held.hl)):
                            mm = pe.matmul(ps[j][:], hp[:, k, j * P:(j + 1) * P], sgn[:, k, :],
                                           start=(k == 0 and n == 0), stop=(k == KT - 1 and n == 1))
                    mm.then_inc(full, 1)

            @block.vector
            def _(dve):
                dve.wait_ge(w_in, 16)
                for k in range(KT):
                    nc.vector.tensor_scalar(neg[:, k], wT[:, k], 0.0, None, ALU.is_lt).then_inc(negs, 1)
                for k in range(KT):
                    dve.wait_ge(negs, k + 1)
                    nc.vector.scalar_tensor_tensor(sgn[:, k], wT[:, k], 0.0, neg[:, k], ALU.is_gt, ALU.subtract).then_inc(signs, 1)
                dve.wait_ge(rs_in, 16)
                for j in range(NT):
                    dve.wait_ge(full, j + 1)
                    nc.vector.tensor_tensor(z[:, j], ps[j][:], rs[:], ALU.mult).then_inc(scaled, 1)
                    dve.wait_ge(scaled, j + 1)
                    nc.vector.tensor_tensor(same[:, j], z[:, j], z[:, j], ALU.is_equal).then_inc(equal, 1)
                    nc.vector.tensor_scalar(wild[:, j], z[:, j], 0.0, 0.0, ALU.mult, ALU.not_equal).then_inc(marked, 1)
                for j in range(NT):
                    dve.wait_ge(marked, j + 1)
                    dve.wait_ge(zeroed, j + 1)
                    nc.vector.copy_predicated(z[:, j], wild[:, j], clip[:, j]).then_inc(put, 1)

            @block.gpsimd
            def _(pool):
                for j in range(NT):
                    pool.wait_ge(scaled, j + 1)
                    nc.gpsimd.tensor_scalar(clip[:, j], z[:, j], LIMIT, -LIMIT, ALU.min, ALU.max).then_inc(clipped, 1)
                    pool.wait_ge(clipped, j + 1)
                    pool.wait_ge(equal, j + 1)
                    nc.gpsimd.tensor_tensor(clip[:, j], clip[:, j], same[:, j], ALU.mult).then_inc(zeroed, 1)


def split_weight(nc, pool, raw, hi, lo, step, before):
    nc.gpsimd.tensor_copy(hi, raw).then_inc(step, 1)
    pool.wait_ge(step, before + 1)
    nc.gpsimd.tensor_tensor(lo, raw, hi, ALU.subtract).then_inc(step, 1)


def stage_qkv(nc, held, a):
    with Stage(nc, "qkv") as st:
        hh, hl = held.hh, held.hl
        raw = st.sb("raw", [P, 3, KT, D])
        wh, wl = st.sb("wh", [P, 3, KT, D], F32R), st.sb("wl", [P, 3, KT, D], F32R)
        bias = st.sb("bias", [P, 3, KT])
        NB = 4
        qf = [st.sb(f"qf{i}", [P, T]) for i in range(NB)]
        qh = [st.sb(f"qh{i}", [P, T], F32R) for i in range(NB)]
        ql = [st.sb(f"ql{i}", [P, T], F32R) for i in range(NB)]
        ps = [st.ps(f"ps{i}", [P, T]) for i in range(4)]
        w_in = [st.sem(f"w_in{i}") for i in range(3)]
        b_in = st.sem("b_in")
        w_split, b_scaled, full, left, hi, lo = (st.sem(n) for n in ("w_split", "b_scaled", "full", "left", "hi", "lo"))
        stored = [st.sem(f"stored{i}") for i in range(NB)]
        items = [(w, b, m) for w in range(3) for b in range(HB) for m in range(KT)]
        dests = [[("qs", 0, 0), ("qs", 1, 1)],
                 [("k1", 0, 0), ("k1", 1, 0), ("k2", 0, 1), ("k2", 1, 1)],
                 [("vs", 0, 0), ("vs", 1, 1)]]
        total, stored_by = [0] * NB, []
        for n, (w, b, m) in enumerate(items):
            total[n % NB] += 16 * len(dests[w])
            stored_by.append(total[n % NB])
        with nc.Block() as block:

            @block.sync
            def _(sp):
                for i, n in enumerate(("w1q", "w1k", "w1v")):
                    sp.dma_start(raw[:, i], a[n].rearrange("(k p) n -> p k n", p=P)).then_inc(w_in[i], 16)
                    sp.dma_start(bias[:, i], a[("b1q", "b1k", "b1v")[i]]).then_inc(b_in, 16)
                for n, (w, b, m) in enumerate(items):
                    sp.wait_ge(lo, n + 1)
                    for name, part, low in dests[w]:
                        src = (ql if low else qh)[n % NB]
                        sp.dma_start(a[name][b, :, part, m * P:(m + 1) * P, :].rearrange("q p t -> p q t"),
                                     src[:].bitcast(F32).rearrange("p (q t) -> p q t", q=4)).then_inc(stored[n % NB], 16)
                for i in range(NB):
                    sp.wait_ge(stored[i], total[i])

            @block.gpsimd
            def _(pool):
                for w in range(3):
                    pool.wait_ge(w_in[w], 16)
                    for k in range(KT):
                        split_weight(nc, pool, raw[:, w, k], wh[:, w, k], wl[:, w, k], w_split, 2 * (w * KT + k))

            @block.tensor
            def _(pe):
                for n, (w, b, m) in enumerate(items):
                    if n >= 4:
                        pe.wait_ge(left, n - 3)
                    for k in range(KT):
                        if b == 0 and m == 0:
                            pe.wait_ge(w_split, 2 * (w * KT + k + 1))
                        t, c = slice(b * T, (b + 1) * T), slice(m * P, (m + 1) * P)
                        for i, (wp, hp) in enumerate(((wh, hh), (wh, hl), (wl, hh))):
                            mm = pe.matmul(ps[n % 4][:], wp[:, w, k, c], hp[:, k, t],
                                           start=(k == 0 and i == 0), stop=(k == KT - 1 and i == 2))
                    mm.then_inc(full, 1)

            @block.scalar
            def _(act):
                act.wait_ge(b_scaled, 1)
                for n, (w, b, m) in enumerate(items):
                    act.wait_ge(full, n + 1)
                    if n >= NB:
                        act.wait_ge(lo, n - NB + 1)
                    nc.scalar.activation(qf[n % NB][:], ps[n % 4][:], ACT.Identity, bias=bias[:, w, m:m + 1],
                                         scale=D1 ** -0.5 if w == 0 else 1.0).then_inc(left, 1)

            @block.vector
            def _(dve):
                dve.wait_ge(b_in, 48)
                nc.vector.tensor_scalar(bias[:, 0], bias[:, 0], D1 ** -0.5, None, ALU.mult).then_inc(b_scaled, 1)
                for n in range(len(items)):
                    dve.wait_ge(left, n + 1)
                    if n >= NB:
                        dve.wait_ge(stored[n % NB], stored_by[n - NB])
                    nc.vector.tensor_copy(qh[n % NB][:], qf[n % NB][:]).then_inc(hi, 1)
                    dve.wait_ge(hi, n + 1)
                    nc.vector.tensor_tensor(ql[n % NB][:], qf[n % NB][:], qh[n % NB][:].bitcast(F32), ALU.subtract).then_inc(lo, 1)


TQ = T // 4
NC_ = 8
TC = TQ // NC_


def stage_zero_diagonal(nc, bd):
    with Stage(nc, "zero") as st:
        zeroed = st.sem("zeroed")
        with nc.Block() as block:
            @block.vector
            def _(dve):
                nc.vector.memset(bd[:, 0:64, :].bitcast(F32), 0.0).then_inc(zeroed, 1)

            @block.gpsimd
            def _(pool):
                nc.gpsimd.memset(bd[:, 64:P, :].bitcast(F32), 0.0).then_inc(zeroed, 1)


def stage_head_attention(nc, a, bd, b):
    with Stage(nc, "heads") as st:
        kk = st.sb("kk", [P, 2, H1, TQ], F32R)
        prob = st.sb("prob", [P, TQ, H1])
        pt = st.sb("pt", [P, TQ, H1])
        pth, ptl = st.sb("pth", [P, TQ, H1], F32R), st.sb("ptl", [P, TQ, H1], F32R)
        o = st.sb("o", [P, H1, TQ])
        top = st.sb("top", [P, TQ, 1])
        den = st.sb("den", [P, TQ, 1])
        rden = st.sb("rden", [P, TQ, 1])
        pS = [st.ps(f"pS{i}", [P, TC, H1]) for i in range(6)]
        pO = [st.ps(f"pO{i}", [P, TC, H1]) for i in range(2)]
        q_in, k_in, v_in = st.sem("q_in"), st.sem("k_in"), st.sem("v_in")
        s_full, top_done, shifted, exp_done, masked, summed, recip, normed, turned, hi, lo = (st.sem(n) for n in (
            "s_full", "top_done", "shifted", "exp_done", "masked", "summed", "recip", "normed", "turned", "hi", "lo"))
        o_full, o_left, o_out = st.sem("o_full"), st.sem("o_left"), st.sem("o_out")
        ch = [slice(c * TC, (c + 1) * TC) for c in range(NC_)]

        def load_queries(eng, q):
            eng.dma_start(bd[32 * q:32 * q + 32, 32 * q:32 * q + 32, :].bitcast(F32),
                          a["qs"][bass.ds(b, 1), q].rearrange("o u (d h) t -> (o u d) h t", h=H1)).then_inc(q_in, 16)

        def load_values(eng, q):
            for u in range(2):
                c = 32 * q + D1 * u
                eng.dma_start(bd[32 * q:32 * q + 32, c:c + D1, :].bitcast(F32),
                              a["vs"][bass.ds(b, 1), q, u].rearrange("o (g d) t -> (o g) d t", d=D1)).then_inc(v_in, 16)

        with nc.Block() as block:

            @block.sync
            def _(sp):
                for u, n in enumerate(("k1", "k2")):
                    sp.dma_start(kk[:, u].bitcast(F32), a[n][bass.ds(b, 1)].rearrange("o q u (d h) t -> (o q u d) h t", h=H1)
                                 ).then_inc(k_in, 16)
                for q in (0, 2):
                    load_queries(sp, q)
                sp.wait_ge(s_full, NC_)
                for q in (0, 2):
                    load_values(sp, q)
                sp.wait_ge(o_left, NC_)
                sp.dma_start(a["attn"][bass.ds(b, 1)].rearrange("o q u (d h) t -> (o q u d) h t", h=H1), o[:]).then_inc(o_out, 16)
                sp.wait_ge(o_out, 16)

            @block.tensor
            def _(pe):
                pe.wait_ge(q_in, 64)
                pe.wait_ge(k_in, 32)
                for c in range(NC_):
                    if c >= 6:
                        pe.wait_ge(masked, c - 5)
                    for i in range(TC):
                        t = c * TC + i
                        for u in range(2):
                            mm = pe.matmul(pS[c % 6][:, i, :], bd[:, :, t], kk[:, u, :, t], start=(u == 0), stop=(u == 1))
                    mm.then_inc(s_full, 1)
                pe.wait_ge(v_in, 128)
                for c in range(NC_):
                    pe.wait_ge(lo, c + 1)
                    if c >= 2:
                        pe.wait_ge(o_left, c - 1)
                    for i in range(TC):
                        t = c * TC + i
                        for m, pp in enumerate((pth, ptl)):
                            mm = pe.matmul(pO[c % 2][:, i, :], bd[:, :, t], pp[:, t, :], start=(m == 0), stop=(m == 1))
                    mm.then_inc(o_full, 1)

            @block.scalar
            def _(act):
                for q in (1, 3):
                    load_queries(act, q)
                for c in range(NC_):
                    act.wait_ge(shifted, c + 1)
                    nc.scalar.activation(prob[:, ch[c], :], prob[:, ch[c], :], ACT.Exp).then_inc(exp_done, 1)
                    if c == 5:
                        act.wait_ge(s_full, NC_)
                        for q in (1, 3):
                            load_values(act, q)
                    if c >= 2:
                        act.wait_ge(turned, c - 1)
                        nc.scalar.copy(pth[:, ch[c - 2], :], pt[:, ch[c - 2], :]).then_inc(hi, 1)
                for c in (NC_ - 2, NC_ - 1):
                    act.wait_ge(turned, c + 1)
                    nc.scalar.copy(pth[:, ch[c], :], pt[:, ch[c], :]).then_inc(hi, 1)
                for c in range(NC_):
                    act.wait_ge(o_full, c + 1)
                    nc.scalar.copy(o[:, :, ch[c]], pO[c % 2][:].rearrange("p t h -> p h t")).then_inc(o_left, 1)

            @block.vector
            def _(dve):
                wide = [P, TC, H1]

                def first(c):
                    dve.wait_ge(s_full, c + 1)
                    nc.vector.tensor_reduce(top[:, ch[c], :], pS[c % 6][:], AX.X, ALU.max).then_inc(top_done, 1)
                    dve.wait_ge(top_done, c + 1)
                    nc.vector.tensor_tensor(prob[:, ch[c], :], pS[c % 6][:], top[:, ch[c], :].to_broadcast(wide),
                                            ALU.subtract).then_inc(shifted, 1)

                def second(c):
                    dve.wait_ge(exp_done, c + 1)
                    nc.vector.scalar_tensor_tensor(prob[:, ch[c], :], pS[c % 6][:], THRESH, prob[:, ch[c], :],
                                                   ALU.is_gt, ALU.mult).then_inc(masked, 1)
                    dve.wait_ge(masked, c + 1)
                    nc.vector.tensor_reduce(den[:, ch[c], :], prob[:, ch[c], :], AX.X, ALU.add).then_inc(summed, 1)
                    dve.wait_ge(summed, c + 1)
                    nc.vector.reciprocal(rden[:, ch[c], :], den[:, ch[c], :]).then_inc(recip, 1)

                def third(c):
                    dve.wait_ge(normed, c + 1)
                    nc.vector.transpose(pt[:, ch[c], :].rearrange("p t h -> p (t h)"),
                                        prob[:, ch[c], :].rearrange("p t h -> p (t h)")).then_inc(turned, 1)

                for c in range(NC_ + 2):
                    if c < NC_:
                        first(c)
                    if 1 <= c <= NC_:
                        second(c - 1)
                    if c >= 2:
                        third(c - 2)

            @block.gpsimd
            def _(pool):
                for c in range(NC_ + 1):
                    if c < NC_:
                        pool.wait_ge(recip, c + 1)
                        nc.gpsimd.tensor_tensor(prob[:, ch[c], :], prob[:, ch[c], :], rden[:, ch[c], :].to_broadcast([P, TC, H1]),
                                                ALU.mult).then_inc(normed, 1)
                    if c:
                        pool.wait_ge(hi, c)
                        nc.gpsimd.tensor_tensor(ptl[:, ch[c - 1], :], pt[:, ch[c - 1], :], pth[:, ch[c - 1], :].bitcast(F32),
                                                ALU.subtract).then_inc(lo, 1)


def stage_attention_out(nc, held, a):
    with Stage(nc, "wo1") as st:
        y, hh, hl = held.y, held.hh, held.hl
        raw = st.sb("raw", [P, KT, D])
        at = st.sb("at", [P, 2, KT, HB * T])
        wh, wl = st.sb("wh", [P, KT, D], F32R), st.sb("wl", [P, KT, D], F32R)
        bo = st.sb("bo", [P, D])
        ps = [st.ps(f"ps{i}", [P, D]) for i in range(8)]
        w_in, b_in, w_split, summed, hi, lo, full, biased = (st.sem(n) for n in (
            "w_in", "b_in", "w_split", "summed", "hi", "lo", "full", "biased"))
        a_in = [st.sem(f"a_in{b}") for b in range(HB)]
        with nc.Block() as block:

            @block.sync
            def _(sp):
                sp.dma_start(raw[:], a["w1o"].rearrange("(k p) n -> p k n", p=P)).then_inc(w_in, 16)
                for b in range(HB):
                    for k in range(KT):
                        for u in range(2):
                            sp.dma_start(at[:, u, k, b * T:(b + 1) * T].rearrange("p (q t) -> p q t", q=4),
                                         a["attn"][b, :, u, k * P:(k + 1) * P, :].rearrange("q p t -> p q t")).then_inc(a_in[b], 16)
                sp.dma_start(bo[:], a["b1o"].rearrange("(o d) -> o d", o=1).to_broadcast([P, D])).then_inc(b_in, 16)

            @block.gpsimd
            def _(pool):
                pool.wait_ge(w_in, 16)
                for k in range(KT):
                    split_weight(nc, pool, raw[:, k], wh[:, k], wl[:, k], w_split, 2 * k)

            @block.tensor
            def _(pe):
                pe.wait_ge(w_split, 2 * KT)
                for j in range(NT):
                    pe.wait_ge(lo, (j // TT + 1) * KT)
                    for k in range(KT):
                        for i, (hp, wp) in enumerate(((hh, wh), (hh, wl), (hl, wh))):
                            mm = pe.matmul(ps[j][:], hp[:, k, j * P:(j + 1) * P], wp[:, k, :],
                                           start=(k == 0 and i == 0), stop=(k == KT - 1 and i == 2))
                    mm.then_inc(full, 1)

            @block.scalar
            def _(act):
                for i in range(HB * KT):
                    b, k = i // KT, i % KT
                    act.wait_ge(summed, i + 1)
                    nc.scalar.copy(hh[:, k, b * T:(b + 1) * T], at[:, 0, k, b * T:(b + 1) * T]).then_inc(hi, 1)

            @block.vector
            def _(dve):
                for i in range(HB * KT + 1):
                    if i < HB * KT:
                        b, k = i // KT, i % KT
                        dve.wait_ge(a_in[b], 32 * KT)
                        nc.vector.tensor_tensor(at[:, 0, k, b * T:(b + 1) * T], at[:, 0, k, b * T:(b + 1) * T],
                                                at[:, 1, k, b * T:(b + 1) * T], ALU.add).then_inc(summed, 1)
                    if i:
                        b, k = (i - 1) // KT, (i - 1) % KT
                        dve.wait_ge(hi, i)
                        nc.vector.tensor_tensor(hl[:, k, b * T:(b + 1) * T], at[:, 0, k, b * T:(b + 1) * T],
                                                hh[:, k, b * T:(b + 1) * T].bitcast(F32), ALU.subtract).then_inc(lo, 1)
                dve.wait_ge(b_in, 16)
                for j in range(NT):
                    dve.wait_ge(full, j + 1)
                    nc.vector.tensor_tensor(y[:, j, :], ps[j][:], bo[:], ALU.add).then_inc(biased, 1)


def stage_lora(nc, held, a, half):
    with Stage(nc, "ffn1") as st:
        x, hh, hl = held.x, held.hh, held.hl
        NA = NE * R1 + NE
        rawA, rawB = st.sb("rawA", [P, KT, NA]), st.sb("rawB", [P, D])
        ah, al = st.sb("ah", [P, KT, NA], F32R), st.sb("al", [P, KT, NA], F32R)
        bh, bl = st.sb("bh", [P, D], F32R), st.sb("bl", [P, D], F32R)
        gate = st.sb("gate", [P, HB, D])
        hs = st.sb("hs", [P, NT, NA])
        top = st.sb("top", [P, NT, 1])
        rank = st.sb("rank", [P, NT, NE])
        best = st.sb("best", [P, NT, 1])
        route = st.sb("route", [P, NT, NE])
        wt = st.sb("wt", [P, NT, NE * R1])
        wth, wtl = st.sb("wth", [P, NT * P], F32R), st.sb("wtl", [P, NT * P], F32R)
        yg = [st.sb(f"yg{i}", [P, D]) for i in range(2)]
        ps = [st.ps(f"ps{i}", [P, D]) for i in range(4)]
        pT = [st.ps(f"pT{i}", [P, T]) for i in range(2)]
        a_in, b_in, gate_in = st.sem("a_in"), st.sem("b_in"), st.sem("gate_in")
        w_split, h_full, h_left, pick, routed = (st.sem(n) for n in ("w_split", "h_full", "h_left", "pick", "routed"))
        turned, hi, lo, full, gated, added, stored = (st.sem(n) for n in ("turned", "hi", "lo", "full", "gated", "added", "stored"))
        with nc.Block() as block:

            @block.sync
            def _(sp):
                sp.dma_start(rawA[:, :, 0:NE * R1], a["loraAT"].rearrange("(k p) n -> p k n", p=P)).then_inc(a_in, 16)
                sp.dma_start(rawA[:, :, NE * R1:], a["routeT"].rearrange("(k p) n -> p k n", p=P)).then_inc(a_in, 16)
                sp.dma_start(rawB[:], a["loraBT"]).then_inc(b_in, 16)
                for b in range(HB):
                    sp.dma_start(gate[:, b, :], a["gates"][3, bass.ds(half * HB + b, 1), :].to_broadcast([P, D])).then_inc(gate_in, 16)
                for j in range(NT):
                    sp.wait_ge(added, j + 1)
                    sp.dma_start(a["out"][bass.ds(half * HB * T + j * P, P), :], x[:, j, :]).then_inc(stored, 16)
                sp.wait_ge(stored, 16 * NT)

            @block.gpsimd
            def _(pool):
                pool.wait_ge(a_in, 32)
                split_weight(nc, pool, rawA[:], ah[:], al[:], w_split, 0)
                pool.wait_ge(b_in, 16)
                split_weight(nc, pool, rawB[:], bh[:], bl[:], w_split, 2)
                for j in range(NT):
                    pool.wait_ge(gated, j + 1)
                    nc.gpsimd.tensor_tensor(x[:, j, :], x[:, j, :], yg[j % 2][:], ALU.add).then_inc(added, 1)

            @block.tensor
            def _(pe):
                pe.wait_ge(w_split, 2)
                for j in range(NT):
                    if j >= 4:
                        pe.wait_ge(h_left, j - 3)
                    for k in range(KT):
                        for i, (hp, wp) in enumerate(((hh, ah), (hh, al), (hl, ah))):
                            mm = pe.matmul(ps[j % 4][:, 0:NA], hp[:, k, j * P:(j + 1) * P], wp[:, k, :],
                                           start=(k == 0 and i == 0), stop=(k == KT - 1 and i == 2))
                    mm.then_inc(h_full, 1)
                pe.wait_ge(routed, 1)
                for b in range(HB):
                    for j in range(TT):
                        mm = pe.transpose(pT[b][:, j * P:(j + 1) * P], wt[:, b * TT + j, :], held.ident)
                    mm.then_inc(turned, 1)
                pe.wait_ge(w_split, 4)
                for j in range(NT):
                    pe.wait_ge(lo, j // TT + 1)
                    if j < 4:
                        pe.wait_ge(h_left, NT)
                    else:
                        pe.wait_ge(gated, j - 3)
                    for i, (wp, bp) in enumerate(((wth, bh), (wth, bl), (wtl, bh))):
                        mm = pe.matmul(ps[j % 4][:], wp[:, j * P:(j + 1) * P], bp[:], start=(i == 0), stop=(i == 2))
                    mm.then_inc(full, 1)

            @block.scalar
            def _(act):
                for j in range(NT):
                    act.wait_ge(h_full, j + 1)
                    nc.scalar.copy(hs[:, j, :], ps[j % 4][:, 0:NA]).then_inc(h_left, 1)
                for b in range(HB):
                    act.wait_ge(turned, b + 1)
                    nc.scalar.copy(wth[:, b * T:(b + 1) * T], pT[b][:]).then_inc(hi, 1)

            @block.vector
            def _(dve):
                n = [0]

                def link(ins):
                    n[0] += 1
                    ins.then_inc(pick, 1)
                    dve.wait_ge(pick, n[0])

                dve.wait_ge(h_left, NT)
                logits = hs[:, :, NE * R1:]
                wide = [P, NT, NE]
                link(nc.vector.tensor_reduce(top[:], logits, AX.X, ALU.max))
                link(nc.vector.tensor_tensor(rank[:], logits, top[:].to_broadcast(wide), ALU.is_ge))
                for j in range(NT):
                    ins = nc.vector.tensor_tensor(route[:, j, :], rank[:, j, :], held.ranks, ALU.mult)
                link(ins)
                link(nc.vector.tensor_reduce(best[:], route[:], AX.X, ALU.max))
                link(nc.vector.tensor_tensor(rank[:], route[:], best[:].to_broadcast(wide), ALU.is_equal))
                link(nc.vector.tensor_tensor(route[:], rank[:], top[:].to_broadcast(wide), ALU.mult))
                for j in range(NT):
                    ins = nc.vector.tensor_tensor(wt[:, j, :].rearrange("p (e r) -> p e r", e=NE),
                                                  hs[:, j, 0:NE * R1].rearrange("p (e r) -> p e r", e=NE),
                                                  route[:, j, :].rearrange("p (e o) -> p e o", o=1).to_broadcast([P, NE, R1]), ALU.mult)
                ins.then_inc(routed, 1)
                for b in range(HB):
                    dve.wait_ge(hi, b + 1)
                    nc.vector.tensor_tensor(wtl[:, b * T:(b + 1) * T], pT[b][:], wth[:, b * T:(b + 1) * T].bitcast(F32),
                                            ALU.subtract).then_inc(lo, 1)
                dve.wait_ge(gate_in, 16 * HB)
                for j in range(NT):
                    dve.wait_ge(full, j + 1)
                    if j >= 2:
                        dve.wait_ge(added, j - 1)
                    nc.vector.tensor_tensor(yg[j % 2][:], ps[j % 4][:], gate[:, j // TT, :], ALU.mult).then_inc(gated, 1)


def build(nc, a):
    with ExitStack() as ctx:
        sb = lambda n, s, dt=F32: ctx.enter_context(nc.sbuf_tensor(n, s, dt))
        held = Held()
        W = 2 * T + 2 * P + NE
        held.consts = sb("consts", [P, W])
        held.cosT, held.sinT = held.consts[:, 0:T], held.consts[:, T:2 * T]
        held.ident = held.consts[:, 2 * T:2 * T + P]
        held.mask = held.consts[:, 2 * T + P:2 * T + 2 * P]
        held.ranks = held.consts[:, 2 * T + 2 * P:]
        held.identr, held.maskr = sb("identr", [P, P], F32R), sb("maskr", [P, P], F32R)
        held.modT = sb("modT", [P, 2, 4, KT, B])
        held.modh = sb("modh", [P, 2, 4, KT, HB])
        stage_modulation(nc, held, a)
        held.x = sb("x", [P, NT, D])

        def working(wctx, name):
            wsb = lambda n, s, dt=F32: wctx.enter_context(nc.sbuf_tensor(f"{name}_{n}", s, dt))
            held.y = wsb("y", [P, NT, D])
            held.hh, held.hl = wsb("hh", [P, KT, HB * T], F32R), wsb("hl", [P, KT, HB * T], F32R)

        with nc.Fori(0, B // HB) as half:
            stage_half_mod(nc, held, half)
            with ExitStack() as wctx:
                working(wctx, "first")
                with ExitStack() as gctx:
                    wts = GroupWeights(gctx, nc, a)
                    stage_norm(nc, held, a, 0, 0, half, weights=wts)
                    with nc.Fori(0, G) as g:
                        stage_group(nc, held, a, wts, (g + 1) % G)
                stage_norm(nc, held, a, 0, 1, half, residual=0)
                stage_sign_ffn(nc, held, a)
                stage_norm(nc, held, a, 1, 0, half, residual=1)
                stage_qkv(nc, held, a)
            with nc.sbuf_tensor("bd", [P, P, TQ], F32R) as bd:
                stage_zero_diagonal(nc, bd)
                with nc.Fori(0, HB) as b:
                    stage_head_attention(nc, a, bd, b)
            with ExitStack() as wctx:
                working(wctx, "second")
                stage_attention_out(nc, held, a)
                stage_norm(nc, held, a, 1, 1, half, residual=2)
                stage_lora(nc, held, a, half)


def kernel(**inputs):
    import numpy as _np
    import concourse.bacc as _bacc
    from concourse import mybir as _mybir
    from concourse.bass_utils import run_bass_kernel_spmd as _run

    i = {k: _np.asarray(v) for k, v in inputs.items()}
    wq = i["L0_attn_wq"]
    dim_head = _np.arange(D).reshape(H1, D1).T.reshape(-1)
    arrays = {
        "x": i["L0_attn_x"].reshape(B * T, D), "wq": wq, "wkv": _np.stack([i["L0_attn_wk"], i["L0_attn_wv"]]),
        "wo": i["L0_attn_wo"], "w_sign": i["L0_ffn_weight"], "w_signT": i["L0_ffn_weight"].T,
        "scale_param": i["L0_ffn_scale_param"].reshape(KT, P).T, "c0T": i["L0_c"].T, "c1T": i["L1_c"].T,
        "wmod0": i["L0_wmod"], "wmod1": i["L1_wmod"],
        "w1q": i["L1_attn_Wq"][dim_head].T, "w1k": i["L1_attn_Wk"][dim_head].T, "w1v": i["L1_attn_Wv"].T,
        "w1o": i["L1_attn_Wo"].T[dim_head],
        "b1q": i["L1_attn_bq"][dim_head].reshape(KT, P).T, "b1k": i["L1_attn_bk"][dim_head].reshape(KT, P).T,
        "b1v": i["L1_attn_bv"].reshape(KT, P).T, "b1o": i["L1_attn_bo"],
        "routeT": i["L1_ffn_route_w"].T, "loraAT": i["L1_ffn_A"].reshape(NE * R1, D).T,
        "loraBT": i["L1_ffn_Bw"].transpose(0, 2, 1).reshape(NE * R1, D), "tables": tables(),
    }
    arrays = {f"in_{k}": _np.ascontiguousarray(v) for k, v in arrays.items()}
    nc = _bacc.Bacc("TRN2", target_bir_lowering=False, num_devices=1)
    a = {k[3:]: nc.dram_tensor(k, v.shape, _mybir.dt.from_np(v.dtype), kind="ExternalInput").ap() for k, v in arrays.items()}
    a["out"] = nc.dram_tensor("out", (B * T, D), F32, kind="ExternalOutput").ap()
    a["gates"] = nc.dram_tensor("gates", (4, B, D), F32).ap()
    a["row_scale"] = nc.dram_tensor("row_scale", (D,), F32).ap()
    for n in ("qs", "k1", "k2", "vs"):
        a[n] = nc.dram_tensor(n, (HB, 4, 2, D, TQ), F32).ap()
    a["attn"] = nc.dram_tensor("attn", (HB, 4, 2, D, TQ), F32).ap()
    build(nc, a)
    r = _run(nc, [arrays], core_ids=[0])
    return r.results[0]["out"].reshape(B, T, D)
```

```python
from contextlib import ExitStack

import numpy as np
import concourse.bass as bass
from concourse import mybir

F32 = mybir.dt.float32
F32R = mybir.dt.float32r
BF16 = mybir.dt.bfloat16
I32 = mybir.dt.int32
ALU = mybir.AluOpType
ACT = mybir.ActivationFunctionType
AX = mybir.AxisListType

P = 128
B, T, D = 4, 512, 512
KT = D // P
HB = 2
NT = HB * T // P
TT = T // P
G, R0, HD = 8, 4, 128
H1, D1 = 32, 16
THRESH = 0.001
NE, R1 = 8, 16
EPS = 1e-5
MASKED = -1e30
MAGIC = 0x5F3759DF
LIMIT = 1000000.0
FIRST_SEM = 160


def tables():
    inv = 1.0 / 500000.0 ** (np.arange(0, HD, 2, dtype=np.float64) / HD)
    wave = 2.0 * np.pi / inv
    low, high = 1024 / 1.0, 1024 / 4.0
    smooth = (1024 / wave - 1.0) / (4.0 - 1.0)
    scaled = np.where(wave > low, inv / 8.0, inv)
    mid = (wave <= low) & (wave >= high)
    scaled = np.where(mid, (1 - smooth) * inv / 8.0 + smooth * inv, scaled).astype(np.float32)
    freqs = np.arange(T, dtype=np.float32)[:, None] * scaled[None, :]
    emb = np.concatenate([freqs, freqs], axis=-1)
    cos, sin = np.cos(emb).T, np.sin(emb).T
    sign = np.where(np.arange(HD) < HD // 2, -1.0, 1.0).astype(np.float32)[:, None]
    mask = np.where(np.arange(P)[None, :] <= np.arange(P)[:, None], 0.0, MASKED)
    ranks = np.broadcast_to(8.0 - np.arange(NE), (P, NE))
    parts = [cos, sin * sign, np.eye(P), mask, ranks]
    return np.ascontiguousarray(np.concatenate([p.astype(np.float32) for p in parts], axis=1))


class Stage:

    def __init__(self, nc, name):
        self.nc, self.name, self.ctx, self.sems = nc, name, ExitStack(), []

    def __enter__(self):
        return self

    def sb(self, name, shape, dt=F32):
        return self.ctx.enter_context(self.nc.sbuf_tensor(f"{self.name}_{name}", shape, dt))

    def ps(self, name, shape):
        return self.ctx.enter_context(self.nc.psum_tensor(f"{self.name}_{name}", shape, F32))

    def sem(self, name):
        s = self.ctx.enter_context(self.nc.semaphore(f"{self.name}_{name}", num=FIRST_SEM + len(self.sems)))
        self.sems.append(s.num)
        return s

    def __exit__(self, *e):
        if e[0] is None:
            self.nc.all_engine_barrier(sems_to_clear=range(self.sems[0], self.sems[-1] + 1))
        return self.ctx.__exit__(*e)


class Held:
    pass


def stage_modulation(nc, held, a):
    with Stage(nc, "mod") as st:
        consts = held.consts
        cT = st.sb("cT", [P, KT, 2 * B])
        ec = st.sb("ec", [P, KT, 2 * B])
        silu = st.sb("silu", [P, KT, 2 * B])
        wm = [st.sb(f"wm{l}", [P, KT, 6 * D]) for l in range(2)]
        gate = st.sb("gate", [B, 4, D])
        gabs = st.sb("gabs", [B, 4, D])
        gsgn = st.sb("gsgn", [B, 4, D])
        w = st.sb("w", [P, KT, D])
        sp = st.sb("sp", [P, KT])
        rs = st.sb("rs", [P, KT])
        pc = [st.ps(f"pc{l}", [P, 4, KT, B]) for l in range(2)]
        pg = [st.ps(f"pg{i}", [B, D]) for i in range(4)]
        const_in = st.sem("const_in")
        c_in = st.sem("c_in")
        wm_in = [st.sem(f"wm_in{l}") for l in range(2)]
        w_in = st.sem("w_in")
        c_exp = st.sem("c_exp")
        silu_step = st.sem("silu_step")
        silu_done = st.sem("silu_done")
        col_full = st.sem("col_full")
        gate_full = st.sem("gate_full")
        gate_step = st.sem("gate_step")
        held_done = st.sem("held_done")
        gate_copied = st.sem("gate_copied")
        rows_out = st.sem("rows_out")
        CH = [0, 1, 3, 4]
        GT = [2, 5]
        with nc.Block() as block:

            @block.sync
            def _(sp_):
                for l, c in enumerate((a["c0T"], a["c1T"])):
                    sp_.dma_start(cT[:, :, l * B:(l + 1) * B],
                                  c.rearrange("(k p) b -> p k b", p=P)).then_inc(c_in, 16)
                for l, m in enumerate((a["wmod0"], a["wmod1"])):
                    sp_.dma_start(wm[l][:], m.rearrange("(k p) n -> p k n", p=P)).then_inc(wm_in[l], 16)
                sp_.wait_ge(gate_step, 5)
                sp_.dma_start(a["gates"].rearrange("g b d -> b g d"), gate[:]).then_inc(rows_out, 16)
                sp_.wait_ge(rows_out, 32)

            @block.scalar
            def _(act):
                act.dma_start(held.consts[:], a["tables"]).then_inc(const_in, 16)
                act.dma_start(w[:], a["w_sign"].rearrange("(k p) n -> p k n", p=P)).then_inc(w_in, 16)
                act.dma_start(sp[:], a["scale_param"]).then_inc(w_in, 16)
                act.wait_ge(c_in, 32)
                nc.scalar.activation(ec[:], cT[:], ACT.Exp, scale=-1.0).then_inc(c_exp, 1)
                act.wait_ge(gate_step, 6)
                act.dma_start(a["row_scale"].rearrange("(k p) -> p k", p=P), rs[:], allow_slow_non_contiguous=True).then_inc(rows_out, 16)
                act.wait_ge(const_in, 16)

            @block.tensor
            def _(pe):
                pe.wait_ge(silu_done, 1)
                for l in range(2):
                    pe.wait_ge(wm_in[l], 16)
                    for ci, c in enumerate(CH):
                        for m in range(KT):
                            for k in range(KT):
                                mm = pe.matmul(pc[l][:, ci, m, :], wm[l][:, k, c * D + m * P:c * D + (m + 1) * P],
                                               silu[:, k, l * B:(l + 1) * B], start=(k == 0), stop=(k == KT - 1))
                    mm.then_inc(col_full, 1)
                    for gi, g in enumerate(GT):
                        for k in range(KT):
                            mm = pe.matmul(pg[2 * l + gi][:], silu[:, k, l * B:(l + 1) * B],
                                           wm[l][:, k, g * D:(g + 1) * D], start=(k == 0), stop=(k == KT - 1))
                        mm.then_inc(gate_full, 1)

            @block.vector
            def _(dve):
                dve.wait_ge(c_exp, 1)
                nc.vector.tensor_scalar_add(ec[:], ec[:], 1.0).then_inc(silu_step, 1)
                dve.wait_ge(silu_step, 1)
                nc.vector.reciprocal(ec[:], ec[:]).then_inc(silu_step, 1)
                dve.wait_ge(silu_step, 2)
                nc.vector.tensor_tensor(silu[:], cT[:], ec[:], ALU.mult).then_inc(silu_done, 1)
                dve.wait_ge(const_in, 16)
                nc.vector.tensor_copy(held.identb[:], held.ident).then_inc(held_done, 1)
                nc.vector.tensor_copy(held.maskb[:], held.mask).then_inc(held_done, 1)
                dve.wait_ge(w_in, 32)
                nc.vector.tensor_reduce(rs[:], w[:], AX.X, ALU.add, apply_absolute_value=True).then_inc(silu_step, 1)
                dve.wait_ge(silu_step, 3)
                nc.vector.tensor_scalar(rs[:], rs[:], 1.0 / D, 1e-8, ALU.mult, ALU.max).then_inc(silu_step, 1)
                dve.wait_ge(silu_step, 4)
                nc.vector.tensor_tensor(rs[:], rs[:], sp[:], ALU.mult).then_inc(silu_step, 1)
                for l in range(2):
                    dve.wait_ge(col_full, l + 1)
                    for ci in range(4):
                        nc.vector.tensor_scalar(held.modT[:, l, ci, :, :], pc[l][:, ci, :, :],
                                                float(ci % 2), None, ALU.add).then_inc(held_done, 1)
                for i in range(4):
                    dve.wait_ge(gate_full, i + 1)
                    nc.vector.tensor_copy(gate[:, i, :], pg[i][:]).then_inc(gate_copied, 1)
                dve.wait_ge(gate_copied, 4)
                nc.vector.scalar_tensor_tensor(gabs[:], gate[:], -1.0, gate[:], ALU.mult, ALU.max).then_inc(gate_step, 1)
                nc.vector.tensor_scalar(gsgn[:], gate[:], 0.0, 2.0, ALU.is_ge, ALU.mult).then_inc(gate_step, 1)
                dve.wait_ge(gate_step, 2)
                nc.vector.tensor_scalar_max(gabs[:], gabs[:], 0.25).then_inc(gate_step, 1)
                nc.vector.tensor_scalar_add(gsgn[:], gsgn[:], -1.0).then_inc(gate_step, 1)
                dve.wait_ge(gate_step, 4)
                nc.vector.tensor_tensor(gate[:], gabs[:], gsgn[:], ALU.mult).then_inc(gate_step, 1)
                dve.wait_ge(silu_step, 5)
                nc.vector.tensor_copy(sp[:], rs[:]).then_inc(gate_step, 1)


def stage_norm(nc, held, a, layer, which, half, residual=None, weights=None):
    with Stage(nc, f"ln{layer}{which}") as st:
        x, y, hh, hl = held.x, held.y, held.hh, held.hl
        xn = st.sb("xn", [P, NT, D])
        hf = st.sb("hf", [P, HB * KT, T])
        gate = st.sb("gate", [P, HB, D]) if residual is not None else None
        stats = st.sb("stats", [P, NT, 6])
        mv = st.sb("mv", [P, NT, 2])
        var = st.sb("var", [P, NT])
        rstd = st.sb("rstd", [P, NT])
        step = st.sb("step", [P, NT])
        pT = [st.ps(f"pT{i}", [P, T]) for i in range(HB * KT)]
        x_in = [st.sem(f"x_in{b}") for b in range(HB)]
        gate_in = st.sem("gate_in")
        gated = st.sem("gated")
        x_new = st.sem("x_new")
        stat_done = st.sem("stat_done")
        newton = st.sem("newton")
        xn_done = st.sem("xn_done")
        turned = st.sem("turned")
        scaled = st.sem("scaled")
        hi_done = st.sem("hi_done")
        lo_done = st.sem("lo_done")
        split_hi, split_lo = st.sem("split_hi"), st.sem("split_lo")
        w_in = st.sem("w_in")
        y_clear = st.sem("y_clear")
        ci = 2 * which
        with nc.Block() as block:

            @block.sync
            def _(sp):
                if residual is None:
                    for b in range(HB):
                        sp.dma_start(x[:, b * TT:(b + 1) * TT, :],
                                     a["x"][bass.ds(half * HB * T + b * T, T), :].rearrange("(j p) d -> p j d", p=P)
                                     ).then_inc(x_in[b], 16)
                else:
                    for b in range(HB):
                        sp.dma_start(gate[:, b, :], a["gates"][residual, bass.ds(half * HB + b, 1), :]
                                     .to_broadcast([P, D])).then_inc(gate_in, 16)
                if weights:
                    weights.load_qkv(sp, w_in, 0)
                    weights.load_o(sp, w_in, 0)

            @block.gpsimd
            def _(pool):
                if residual is not None:
                    pool.wait_ge(gate_in, 16 * HB)
                    for j in range(NT):
                        nc.gpsimd.tensor_tensor(y[:, j, :], y[:, j, :], gate[:, j // TT, :], ALU.mult).then_inc(gated, 1)
                if weights:
                    nc.gpsimd.memset(y[:], 0.0).then_inc(y_clear, 1)
                    for n, (what, i) in enumerate(FIRST_PARTS):
                        pool.wait_ge(split_hi, n + 1)
                        weights.split_lo(what, i).then_inc(split_lo, 1)
                for i in range(HB * KT):
                    b, k = i // KT, i % KT
                    pool.wait_ge(hi_done, i + 1)
                    nc.gpsimd.tensor_tensor(hl[:, k, b * T:(b + 1) * T], hf[:, i, :], hh[:, k, b * T:(b + 1) * T],
                                            ALU.subtract).then_inc(lo_done, 1)

            @block.vector
            def _(dve):
                for j in range(NT):
                    if residual is None:
                        dve.wait_ge(x_in[j // TT], 16)
                    else:
                        dve.wait_ge(gated, j + 1)
                        nc.vector.tensor_tensor(x[:, j, :], x[:, j, :], y[:, j, :], ALU.add).then_inc(x_new, 1)
                for j in range(NT):
                    if residual is not None:
                        dve.wait_ge(x_new, j + 1)
                    nc.vector.bn_stats(stats[:, j, :], x[:, j, :]).then_inc(stat_done, 1)
                for j in range(NT):
                    dve.wait_ge(stat_done, j + 1)
                    nc.vector.bn_aggr(mv[:, j, :], stats[:, j, :]).then_inc(stat_done, 1)
                dve.wait_ge(stat_done, 2 * NT)
                n = [0]

                def link(ins):
                    n[0] += 1
                    ins.then_inc(newton, 1)
                    dve.wait_ge(newton, n[0])

                link(nc.vector.tensor_scalar(var[:], mv[:, :, 1], EPS, None, ALU.add))
                link(nc.vector.tensor_scalar(step[:].bitcast(I32), var[:].bitcast(I32), 1, None, ALU.logical_shift_right))
                link(nc.vector.tensor_scalar(rstd[:].bitcast(I32), step[:].bitcast(I32), -1.0, float(MAGIC), ALU.mult, ALU.add))
                for _ in range(4):
                    link(nc.vector.tensor_tensor(step[:], rstd[:], rstd[:], ALU.mult))
                    link(nc.vector.tensor_tensor(step[:], step[:], var[:], ALU.mult))
                    link(nc.vector.tensor_scalar(step[:], step[:], -0.5, 1.5, ALU.mult, ALU.add))
                    link(nc.vector.tensor_tensor(rstd[:], rstd[:], step[:], ALU.mult))
                for j in range(NT):
                    nc.vector.tensor_scalar(xn[:, j, :], x[:, j, :], mv[:, j, 0:1], rstd[:, j:j + 1],
                                            ALU.subtract, ALU.mult).then_inc(xn_done, 1)
                for i in range(HB * KT):
                    b, k = i // KT, i % KT
                    dve.wait_ge(scaled, i + 1)
                    nc.vector.tensor_copy(hh[:, k, b * T:(b + 1) * T], hf[:, i, :]).then_inc(hi_done, 1)

            @block.tensor
            def _(pe):
                for b in range(HB):
                    for j in range(TT):
                        pe.wait_ge(xn_done, b * TT + j + 1)
                        for k in range(KT):
                            mm = pe.transpose(pT[b * KT + k][:, j * P:(j + 1) * P], xn[:, b * TT + j, k * P:(k + 1) * P],
                                              held.ident)
                    mm.then_inc(turned, 1)

            @block.scalar
            def _(act):
                if weights:
                    act.wait_ge(w_in, 48)
                    for what, i in FIRST_PARTS:
                        weights.split_hi(what, i).then_inc(split_hi, 1)
                for i in range(HB * KT):
                    b, k = i // KT, i % KT
                    act.wait_ge(turned, b + 1)
                    nc.scalar.activation(hf[:, i, :], pT[i][:], ACT.Identity,
                                         bias=held.modh[:, layer, ci, k, b:b + 1],
                                         scale=held.modh[:, layer, ci + 1, k, b:b + 1]).then_inc(scaled, 1)


def stage_half_mod(nc, held, half):
    with Stage(nc, "hm") as st:
        done = st.sem("done")
        with nc.Block() as block:
            @block.vector
            def _(dve):
                nc.vector.tensor_copy(held.modh[:].rearrange("p l c k b -> p (l c k) b"),
                                      held.modT[:].rearrange("p l c k b -> p (l c k) b")[:, :, bass.ds(half * HB, HB)]
                                      ).then_inc(done, 1)


class GroupWeights:

    def __init__(self, ctx, nc, a):
        sb = lambda n, s, dt=F32: ctx.enter_context(nc.sbuf_tensor(n, s, dt))
        QW = R0 * HD
        self.nc, self.a = nc, a
        self.raw_q, self.raw_kv, self.raw_o = sb("raw_q", [P, KT, QW]), sb("raw_kv", [P, 2, KT, HD]), sb("raw_o", [P, R0, D])
        self.qh, self.ql = sb("wqh", [P, KT, QW], F32R), sb("wql", [P, KT, QW], F32R)
        self.kvh, self.kvl = sb("wkvh", [P, 2, KT, HD], F32R), sb("wkvl", [P, 2, KT, HD], F32R)
        self.oh, self.ol = sb("woh", [P, R0, D], F32R), sb("wol", [P, R0, D], F32R)

    def load_qkv(self, eng, sem, g):
        QW = R0 * HD
        eng.dma_start(self.raw_q[:], self.a["wq"][:, bass.ds(g * QW, QW)].rearrange("(k p) n -> p k n", p=P)).then_inc(sem, 16)
        eng.dma_start(self.raw_kv[:], self.a["wkv"][:, :, bass.ds(g * HD, HD)].rearrange("w (k p) n -> p w k n", p=P)).then_inc(sem, 16)

    def load_o(self, eng, sem, g):
        QW = R0 * HD
        eng.dma_start(self.raw_o[:], self.a["wo"][bass.ds(g * QW, QW), :].rearrange("(h p) n -> p h n", p=P)).then_inc(sem, 16)

    def parts(self, what, i):
        if what == "q":
            s = slice(i * HD, (i + 1) * HD)
            return self.raw_q[:, :, s], self.qh[:, :, s], self.ql[:, :, s]
        if what == "kv":
            return self.raw_kv[:, i], self.kvh[:, i], self.kvl[:, i]
        return self.raw_o[:, i], self.oh[:, i], self.ol[:, i]

    def split_hi(self, what, i):
        raw, hi, lo = self.parts(what, i)
        return self.nc.scalar.copy(hi, raw)

    def split_lo(self, what, i):
        raw, hi, lo = self.parts(what, i)
        return self.nc.gpsimd.tensor_tensor(lo, raw, hi.bitcast(F32), ALU.subtract)


FIRST_PARTS = [("kv", 0), ("q", 0), ("kv", 1), ("q", 1), ("q", 2), ("q", 3)]

GB = 2
UNITS = GB * HB
NH = UNITS * R0
STEP_KINDS = [[("Q", n + 2)] * (n + 2 < NH)
              + [(kind, n // R0 + 1) for at, kind in ((1, "K"), (2, "V")) if n % R0 == at and n // R0 + 1 < UNITS]
              for n in range(NH)]
PROJ = [("K", 0), ("Q", 0), ("V", 0), ("Q", 1)] + [p for step in STEP_KINDS for p in step]
STEP_PROJ = [[PROJ.index(p) for p in step] for step in STEP_KINDS]
ROPE = [e for e, (kind, _) in enumerate(PROJ) if kind != "V"]
S_AT = [(0, 0), (1, 0), (0, P), (2, 0)]
S_OF = [[0, 2], [1], [3]]
P_OFF = [P * i * (i + 1) // 2 for i in range(TT)]
PT_OFF = [0, 4 * P, 8 * P, 7 * P]
PT_CHUNK = ((0, 4 * P), (4 * P, 4 * P), (8 * P, 2 * P))
NARROW = 192


def weight_splits():
    at = [[] for _ in range(NH)]
    for i in range(R0):
        at[i // 2].append(("o", i, 0, None))
    for gr in range(GB):
        n0 = 2 * R0 * gr
        used = lambda kind, i: PROJ.index((kind, i))
        at[n0 + 2].append(("kv", 0, gr + 1, used("K", 2 * gr + 1)))
        at[n0 + 3].append(("kv", 1, gr + 1, used("V", 2 * gr + 1)))
        for i in range(R0):
            at[n0 + 3 + i if i < 3 else n0 + 6].append(("q", i, gr + 1, used("Q", n0 + R0 + i)))
        if gr + 1 < GB:
            for i in range(R0):
                at[n0 + 8 + i].append(("o", i, gr + 1, 4 * (4 * gr + 2 + i // 2) + 3))
    return at


SPLITS = weight_splits()
SPLIT_LIST = [s for step in SPLITS for s in step]


def stage_groups(nc, held, a, wts, g):
    QS = HD ** -0.5
    with Stage(nc, "gqa") as st:
        hh, hl, y = held.hh, held.hl, held.y
        kh = [st.sb(f"kh{b}", [P, T], F32R) for b in range(2)]
        kl = [st.sb(f"kl{b}", [P, T], F32R) for b in range(2)]
        vt = st.sb("vt", [P, T])
        vh = [st.sb(f"vh{b}", [P, T], F32R) for b in range(2)]
        vl = [st.sb(f"vl{b}", [P, T], F32R) for b in range(2)]
        qh = [st.sb(f"qh{i}", [P, T], F32R) for i in range(2)]
        ql = [st.sb(f"ql{i}", [P, T], F32R) for i in range(2)]
        rot = [st.sb(f"rot{i}", [P, T]) for i in range(2)]
        full = [st.sb(f"full{i}", [P, T]) for i in range(2)]
        prob = [st.sb(f"prob{i}", [P, 10 * P]) for i in range(2)]
        pth, ptl = st.sb("pth", [P, 10 * P], F32R), st.sb("ptl", [P, 10 * P], F32R)
        oh = [st.sb(f"oh{i}", [P, T], F32R) for i in range(4)]
        ol = [st.sb(f"ol{i}", [P, T], F32R) for i in range(4)]
        nmax = [st.sb(f"nmax{i}", [P, TT]) for i in range(2)]
        den = [st.sb(f"den{i}", [P, TT]) for i in range(2)]
        rden = [st.sb(f"rden{i}", [P, TT]) for i in range(2)]
        pj = st.ps("pj", [P, T])
        pS = [st.ps(f"pS{i}", [P, T]) for i in range(3)]
        pT = [st.ps(f"pT{i}", [P, T]) for i in range(2)]
        pO, pW = st.ps("pO", [P, T]), st.ps("pW", [P, D])
        qkv_in, wo_in = st.sem("qkv_in"), st.sem("wo_in")
        proj_full = st.sem("proj_full")
        rotated, cosed = st.sem("rotated"), st.sem("cosed")
        v_out, v_turned, v_hi, v_lo = st.sem("v_out"), st.sem("v_turned"), st.sem("v_hi"), st.sem("v_lo")
        sined, roped, rope_hi, rope_lo = st.sem("sined"), st.sem("roped"), st.sem("rope_hi"), st.sem("rope_lo")
        s_full, max_done, exp_done = st.sem("s_full"), st.sem("max_done"), st.sem("exp_done")
        recip, normed = st.sem("recip"), st.sem("normed")
        pt_full, pt_hi, pt_lo = st.sem("pt_full"), st.sem("pt_hi"), st.sem("pt_lo")
        o_full, o_hi, o_lo = st.sem("o_full"), st.sem("o_hi"), st.sem("o_lo")
        w_full, w_added = st.sem("w_full"), st.sem("w_added")
        w_hi, w_lo = st.sem("w_hi"), st.sem("w_lo")
        bank = [pj] * len(PROJ)
        bank[1], bank[2] = pO, pW
        NTILES = NH // 2 * TT

        def wbank(d):
            return pO if d >= NTILES - TT and d % 2 else pW

        def split_no(what, i, group):
            return next(n for n, s in enumerate(SPLIT_LIST) if s[:3] == (what, i, group)) + 1

        def last_split(kinds, group):
            return max(n for n, s in enumerate(SPLIT_LIST) if s[0] in kinds and s[2] == group) + 1

        def step_e(n, slot):
            return [e for e in STEP_PROJ[n] if (PROJ[e][0] == "Q") == (slot == 0)]

        with nc.Block() as block:

            @block.sync
            def _(sp):
                after = [g + 1, (g + 2) % G]
                for i in range(GB):
                    if i:
                        sp.wait_ge(w_lo, last_split(("q", "kv"), i))
                    wts.load_qkv(sp, qkv_in, after[i])
                    sp.wait_ge(w_lo, last_split(("o",), i))
                    wts.load_o(sp, wo_in, after[i])
                sp.wait_ge(wo_in, 16 * GB)

            @block.tensor
            def _(pe):
                def free(e):
                    kind, i = PROJ[e]
                    if kind == "V":
                        pe.wait_ge(v_out, i + 1)
                    else:
                        pe.wait_ge(cosed, ROPE.index(e) + 1)

                def project(e):
                    kind, i = PROJ[e]
                    if e >= 3:
                        free(0 if e == 3 else e - 1)
                    u = i // R0 if kind == "Q" else i
                    b, group = u % HB, u // HB
                    if group:
                        pe.wait_ge(w_lo, split_no(*(("q", i % R0) if kind == "Q" else ("kv", int(kind == "V"))), group))
                    t = slice(b * T, (b + 1) * T)
                    n = 0
                    for k in range(KT):
                        if kind == "Q":
                            c = slice((i % R0) * HD, (i % R0 + 1) * HD)
                            wh, wl = wts.qh[:, k, c], wts.ql[:, k, c]
                        else:
                            w = int(kind == "V")
                            wh, wl = wts.kvh[:, w, k, :], wts.kvl[:, w, k, :]
                        for wp, hp in ((wh, hh), (wh, hl), (wl, hh)):
                            mm = pe.matmul(bank[e][:], wp, hp[:, k, t], start=(n == 0), stop=(n == 3 * KT - 1))
                            n += 1
                    mm.then_inc(proj_full, 1)

                def turn_values(u):
                    pe.wait_ge(v_out, u + 1)
                    if u:
                        pe.wait_ge(pt_lo, 3 * (R0 * u - 2) + 2)
                    for j in range(TT):
                        mm = pe.transpose(pT[1][:, j * P:(j + 1) * P], vt[:, j * P:(j + 1) * P], held.ident)
                    mm.then_inc(v_turned, 1)

                def scores(n):
                    u, r = n // R0, n % 2
                    pe.wait_ge(rope_lo, ROPE.index(PROJ.index(("Q", n))) + 1)
                    pe.wait_ge(rope_lo, ROPE.index(PROJ.index(("K", u))) + 1)
                    for s, tiles in enumerate(S_OF):
                        if n:
                            pe.wait_ge(exp_done, 3 * (n - 1) + s + 1)
                        for i in tiles:
                            w, c = (i + 1) * P, S_AT[i][1]
                            t = slice(i * P, (i + 1) * P)
                            wide = max(w, NARROW)
                            out = pS[s][:, c:c + wide]
                            pe.matmul(out, qh[r][:, t], kh[u % 2][:, 0:wide], start=True, stop=False)
                            pe.matmul(out, qh[r][:, t], kl[u % 2][:, 0:wide], start=False, stop=False)
                            pe.matmul(out, ql[r][:, t], kh[u % 2][:, 0:wide], start=False, stop=False)
                            mm = pe.matmul(pS[s][:, c + w - P:c + w], held.identb[:], held.maskb[:], start=False, stop=True)
                        mm.then_inc(s_full, 1)

                def turn(n, jobs):
                    for k, js in jobs:
                        if 3 * n + k >= 2:
                            pe.wait_ge(pt_lo, 3 * n + k - (1 if k == 0 else 2) if k < 2 else 3 * n + 1)
                        if k == 1 and n % R0 == R0 - 1 and n + 1 < NH:
                            pe.wait_ge(v_lo, n // R0 + 2)
                        if k == 1 and n == 0:
                            pe.wait_ge(v_lo, 1)
                        for j in js:
                            for i in range(j, TT):
                                c = (PT_OFF[j] + (i - j) * P) % T
                                mm = pe.transpose(pT[k % 2][:, c:c + P],
                                                  prob[n % 2][:, P_OFF[i] + j * P:P_OFF[i] + (j + 1) * P], held.ident)
                        mm.then_inc(pt_full, 1)

                def weigh(n):
                    u = n // R0
                    if n == 0:
                        pe.wait_ge(cosed, 2)
                    else:
                        pe.wait_ge(o_lo, n)
                    pe.wait_ge(v_lo, u + 1)
                    m = 0
                    for j, k in ((0, 0), (1, 1), (3, 1), (2, 2)):
                        pe.wait_ge(pt_lo, 3 * n + k + 1)
                        w = (TT - j) * P
                        v = slice(j * P, (j + 1) * P)
                        pc = slice(PT_OFF[j], PT_OFF[j] + w)
                        for vp, pp in ((vh, pth), (vh, ptl), (vl, pth)):
                            mm = pe.matmul(pO[:, T - w:], vp[u % 2][:, v], pp[:, pc], start=(m == 0), stop=(m == 11))
                            m += 1
                    mm.then_inc(o_full, 1)

                def out_proj(d):
                    pair, i = d // TT, d % TT
                    if d == 0:
                        pe.wait_ge(v_out, 1)
                    if i == 0:
                        pe.wait_ge(o_lo, 2 * pair + 2)
                        pe.wait_ge(w_lo, split_no("o", (2 * pair + 1) % R0, pair // (R0 * HB // 2)))
                    if d:
                        pe.wait_ge(w_added, d if wbank(d) is wbank(d - 1) else d - 1)
                    t = slice(i * P, (i + 1) * P)
                    m = 0
                    for h in (2 * pair, 2 * pair + 1):
                        for op, wp in ((oh, wts.oh), (oh, wts.ol), (ol, wts.oh)):
                            mm = pe.matmul(wbank(d)[:], op[h % 4][:, t], wp[:, h % R0, :], start=(m == 0), stop=(m == 5))
                            m += 1
                    mm.then_inc(w_full, 1)

                for e in range(4):
                    project(e)
                turn_values(0)
                scores(0)
                for n in range(NH):
                    if n == 0:
                        project(4)
                    pe.wait_ge(normed, n + 1)
                    turn(n, ((0, (0,)), (1, (1, 3))))
                    if n:
                        for e in step_e(n, 0):
                            project(e)
                    if n + 1 < NH:
                        scores(n + 1)
                    if n >= 2:
                        out_proj(2 * (n - 2))
                    for e in step_e(n, 1):
                        project(e)
                    turn(n, ((2, (2,)),))
                    if n >= 2:
                        out_proj(2 * (n - 2) + 1)
                    if n % R0 == 2 and n // R0 + 1 < UNITS:
                        turn_values(n // R0 + 1)
                    weigh(n)
                for d in range(NTILES - TT, NTILES):
                    out_proj(d)

            @block.scalar
            def _(act):
                def leave(e):
                    kind, i = PROJ[e]
                    act.wait_ge(proj_full, e + 1)
                    if kind == "V":
                        if i:
                            act.wait_ge(v_turned, i)
                        nc.scalar.copy(vt[:], bank[e][:]).then_inc(v_out, 1)
                        return
                    r = ROPE.index(e)
                    if r >= 2:
                        act.wait_ge(rope_lo, r - 1)
                    scale = QS if kind == "Q" else 1.0
                    nc.scalar.mul(rot[r % 2][0:64, :], bank[e][64:128, :], scale).then_inc(rotated, 1)
                    nc.scalar.mul(rot[r % 2][64:128, :], bank[e][0:64, :], scale).then_inc(rotated, 1)

                def value_his(u):
                    act.wait_ge(v_turned, u + 1)
                    if u >= 2:
                        act.wait_ge(o_full, R0 * (u - 1))
                    nc.scalar.copy(vh[u % 2][:], pT[1][:]).then_inc(v_hi, 1)

                def exps(n):
                    r = n % 2
                    for s, tiles in enumerate(S_OF):
                        act.wait_ge(max_done, 4 * n + (2, 3, 4)[s])
                        if n >= 2 and s == 0:
                            act.wait_ge(pt_full, 3 * (n - 1))
                            act.wait_ge(recip, n - 1)
                        for i in tiles:
                            w, c = (i + 1) * P, S_AT[i][1]
                            ins = nc.scalar.activation(prob[r][:, P_OFF[i]:P_OFF[i] + w], pS[s][:, c:c + w], ACT.Exp,
                                                       bias=nmax[r][:, i:i + 1], accum_out=den[r][:, i:i + 1])
                        ins.then_inc(exp_done, 1)

                def pt_his(n, ks):
                    for k in ks:
                        act.wait_ge(pt_full, 3 * n + k + 1)
                        if n:
                            act.wait_ge(o_full, n)
                        c, w = PT_CHUNK[k]
                        nc.scalar.copy(pth[:, c:c + w], pT[k % 2][:, 0:w]).then_inc(pt_hi, 1)

                def weight_his(n):
                    for what, i, group, user in SPLITS[n]:
                        if what != "o":
                            act.wait_ge(qkv_in, 32 * group)
                            act.wait_ge(proj_full, user + 1)
                        elif user is not None:
                            act.wait_ge(wo_in, 16 * group)
                            act.wait_ge(w_full, user + 1)
                        wts.split_hi(what, i).then_inc(w_hi, 1)

                for e in range(4):
                    leave(e)
                value_his(0)
                exps(0)
                for n in range(NH):
                    if n == 0:
                        leave(4)
                    pt_his(n, (0, 1))
                    if n:
                        for e in step_e(n, 0):
                            leave(e)
                    if n + 1 < NH:
                        exps(n + 1)
                    for e in step_e(n, 1):
                        leave(e)
                    pt_his(n, (2,))
                    if n % R0 == 2 and n // R0 + 1 < UNITS:
                        value_his(n // R0 + 1)
                    weight_his(n)
                    act.wait_ge(o_full, n + 1)
                    if n >= 4:
                        act.wait_ge(w_full, 4 * ((n - 4) // 2) + 4)
                    nc.scalar.copy(oh[n % 4][:], pO[:]).then_inc(o_hi, 1)

            @block.vector
            def _(dve):
                def leave(e):
                    kind, i = PROJ[e]
                    if kind == "V":
                        return
                    r = ROPE.index(e)
                    dve.wait_ge(rotated, 2 * r + 2)
                    scale = QS if kind == "Q" else 1.0
                    nc.vector.scalar_tensor_tensor(full[r % 2][:], bank[e][:], scale, held.cosT, ALU.mult,
                                                   ALU.mult).then_inc(cosed, 1)

                def value_los(u):
                    dve.wait_ge(v_hi, u + 1)
                    nc.vector.tensor_tensor(vl[u % 2][:], pT[1][:], vh[u % 2][:].bitcast(F32), ALU.subtract).then_inc(v_lo, 1)

                def rope_parts(e):
                    kind, i = PROJ[e]
                    if kind == "V":
                        return
                    r = ROPE.index(e)
                    dve.wait_ge(roped, r + 1)
                    if kind == "Q" and i >= 2:
                        dve.wait_ge(s_full, 3 * (i - 1))
                    if kind == "K" and i >= 2:
                        dve.wait_ge(s_full, 3 * R0 * (i - 1))
                    dst = kh[i % 2] if kind == "K" else qh[i % 2]
                    nc.vector.tensor_copy(dst[:], full[r % 2][:]).then_inc(rope_hi, 1)

                def maxes(n):
                    r = n % 2
                    if n >= 2:
                        dve.wait_ge(exp_done, 3 * (n - 1))
                    for s, tiles in enumerate(S_OF):
                        dve.wait_ge(s_full, 3 * n + s + 1)
                        for i in tiles:
                            w, c = (i + 1) * P, S_AT[i][1]
                            nc.vector.tensor_reduce(nmax[r][:, i:i + 1], pS[s][:, c:c + w], AX.X, ALU.max,
                                                    negate=True).then_inc(max_done, 1)

                def pt_los(n, ks):
                    for k in ks:
                        dve.wait_ge(pt_hi, 3 * n + k + 1)
                        c, w = PT_CHUNK[k]
                        nc.vector.tensor_tensor(ptl[:, c:c + w], pT[k % 2][:, 0:w], pth[:, c:c + w].bitcast(F32),
                                                ALU.subtract).then_inc(pt_lo, 1)

                def norms(n):
                    dve.wait_ge(exp_done, 3 * n + 3)
                    nc.vector.reciprocal(rden[n % 2][:], den[n % 2][:]).then_inc(recip, 1)
                    dve.wait_ge(recip, n + 1)
                    for i in range(TT):
                        p = prob[n % 2][:, P_OFF[i]:P_OFF[i] + (i + 1) * P]
                        ins = nc.vector.tensor_scalar(p, p, rden[n % 2][:, i:i + 1], None, ALU.mult)
                    ins.then_inc(normed, 1)

                def add(d):
                    dve.wait_ge(w_full, d + 1)
                    if d >= TT:
                        dve.wait_ge(w_added, d - TT + 1)
                    j = (d // (2 * TT)) % HB * TT + d % TT
                    nc.vector.tensor_tensor(y[:, j, :], wbank(d)[:], y[:, j, :], ALU.add).then_inc(w_added, 1)

                leave(0)
                leave(1)
                rope_parts(0)
                rope_parts(1)
                leave(3)
                value_los(0)
                rope_parts(3)
                maxes(0)
                norms(0)
                for n in range(NH):
                    if n == 0:
                        leave(4)
                    pt_los(n, (0, 1))
                    if n:
                        for e in step_e(n, 0):
                            leave(e)
                    if n + 1 < NH:
                        maxes(n + 1)
                    if n >= 2:
                        add(2 * (n - 2))
                    for e in step_e(n, 0):
                        rope_parts(e)
                    for e in step_e(n, 1):
                        leave(e)
                    pt_los(n, (2,))
                    if n + 1 < NH:
                        norms(n + 1)
                    if n >= 2:
                        add(2 * (n - 2) + 1)
                    if n % R0 == 2 and n // R0 + 1 < UNITS:
                        value_los(n // R0 + 1)
                    for e in step_e(n, 1):
                        rope_parts(e)
                    dve.wait_ge(o_hi, n + 1)
                    nc.vector.tensor_tensor(ol[n % 4][:], pO[:], oh[n % 4][:].bitcast(F32), ALU.subtract).then_inc(o_lo, 1)
                for d in range(NTILES - TT, NTILES):
                    add(d)

            @block.gpsimd
            def _(pool):
                def rope(e):
                    kind, i = PROJ[e]
                    if kind == "V":
                        return
                    r = ROPE.index(e)
                    pool.wait_ge(rotated, 2 * r + 2)
                    nc.gpsimd.tensor_tensor(rot[r % 2][:], rot[r % 2][:], held.sinT, ALU.mult).then_inc(sined, 1)
                    pool.wait_ge(sined, r + 1)
                    pool.wait_ge(cosed, r + 1)
                    nc.gpsimd.tensor_tensor(full[r % 2][:], full[r % 2][:], rot[r % 2][:], ALU.add).then_inc(roped, 1)

                def rope_lo_part(e):
                    kind, i = PROJ[e]
                    if kind == "V":
                        return
                    r = ROPE.index(e)
                    pool.wait_ge(rope_hi, r + 1)
                    hi, lo = (kh[i % 2], kl[i % 2]) if kind == "K" else (qh[i % 2], ql[i % 2])
                    nc.gpsimd.tensor_tensor(lo[:], full[r % 2][:], hi[:].bitcast(F32), ALU.subtract).then_inc(rope_lo, 1)

                rope(0)
                rope(1)
                rope_lo_part(0)
                rope_lo_part(1)
                rope(3)
                rope_lo_part(3)
                done = 0
                for n in range(NH):
                    for e in STEP_PROJ[n]:
                        rope(e)
                        rope_lo_part(e)
                    for what, i, group, user in SPLITS[n]:
                        done += 1
                        pool.wait_ge(w_hi, done)
                        wts.split_lo(what, i).then_inc(w_lo, 1)


def stage_sign_ffn(nc, held, a):
    with Stage(nc, "ffn0") as st:
        wT = st.sb("wT", [P, KT, D])
        neg = st.sb("neg", [P, KT, D])
        sgn = st.sb("sgn", [P, KT, D], F32R)
        rs = st.sb("rs", [P, D])
        z = held.y
        clip = st.sb("clip", [P, NT, D])
        same = st.sb("same", [P, NT, D])
        wild = st.sb("wild", [P, NT, D], I32)
        ps = [st.ps(f"ps{i}", [P, D]) for i in range(NT)]
        w_in, rs_in = st.sem("w_in"), st.sem("rs_in")
        negs, signs = st.sem("negs"), st.sem("signs")
        full, scaled, clipped, equal, zeroed, marked, put = (st.sem(n) for n in
                                                             ("full", "scaled", "clipped", "equal", "zeroed", "marked", "put"))
        with nc.Block() as block:

            @block.sync
            def _(sp):
                sp.dma_start(wT[:], a["w_signT"].rearrange("(k p) n -> p k n", p=P)).then_inc(w_in, 16)
                sp.dma_start(rs[:], a["row_scale"].rearrange("(o d) -> o d", o=1).to_broadcast([P, D])).then_inc(rs_in, 16)

            @block.tensor
            def _(pe):
                for j in range(NT):
                    pe.wait_ge(signs, KT)
                    for k in range(KT):
                        for n, hp in enumerate((held.hh, held.hl)):
                            mm = pe.matmul(ps[j][:], hp[:, k, j * P:(j + 1) * P], sgn[:, k, :],
                                           start=(k == 0 and n == 0), stop=(k == KT - 1 and n == 1))
                    mm.then_inc(full, 1)

            @block.vector
            def _(dve):
                dve.wait_ge(w_in, 16)
                for k in range(KT):
                    nc.vector.tensor_scalar(neg[:, k], wT[:, k], 0.0, None, ALU.is_lt).then_inc(negs, 1)
                for k in range(KT):
                    dve.wait_ge(negs, k + 1)
                    nc.vector.scalar_tensor_tensor(sgn[:, k], wT[:, k], 0.0, neg[:, k], ALU.is_gt, ALU.subtract).then_inc(signs, 1)
                dve.wait_ge(rs_in, 16)
                for j in range(NT):
                    dve.wait_ge(full, j + 1)
                    nc.vector.tensor_tensor(z[:, j], ps[j][:], rs[:], ALU.mult).then_inc(scaled, 1)
                    dve.wait_ge(scaled, j + 1)
                    nc.vector.tensor_tensor(same[:, j], z[:, j], z[:, j], ALU.is_equal).then_inc(equal, 1)
                    nc.vector.tensor_scalar(wild[:, j], z[:, j], 0.0, 0.0, ALU.mult, ALU.not_equal).then_inc(marked, 1)
                for j in range(NT):
                    dve.wait_ge(marked, j + 1)
                    dve.wait_ge(zeroed, j + 1)
                    nc.vector.copy_predicated(z[:, j], wild[:, j], clip[:, j]).then_inc(put, 1)

            @block.gpsimd
            def _(pool):
                for j in range(NT):
                    pool.wait_ge(scaled, j + 1)
                    nc.gpsimd.tensor_scalar(clip[:, j], z[:, j], LIMIT, -LIMIT, ALU.min, ALU.max).then_inc(clipped, 1)
                    pool.wait_ge(clipped, j + 1)
                    pool.wait_ge(equal, j + 1)
                    nc.gpsimd.tensor_tensor(clip[:, j], clip[:, j], same[:, j], ALU.mult).then_inc(zeroed, 1)


def split_weight(nc, pool, raw, hi, lo, step, before):
    nc.gpsimd.tensor_copy(hi, raw).then_inc(step, 1)
    pool.wait_ge(step, before + 1)
    nc.gpsimd.tensor_tensor(lo, raw, hi, ALU.subtract).then_inc(step, 1)


def stage_qkv(nc, held, a):
    with Stage(nc, "qkv") as st:
        hh, hl = held.hh, held.hl
        raw = st.sb("raw", [P, 3, KT, D])
        wh, wl = st.sb("wh", [P, 3, KT, D], F32R), st.sb("wl", [P, 3, KT, D], F32R)
        bias = st.sb("bias", [P, 3, KT])
        NB = 4
        qf = [st.sb(f"qf{i}", [P, T]) for i in range(NB)]
        qh = [st.sb(f"qh{i}", [P, T], F32R) for i in range(NB)]
        ql = [st.sb(f"ql{i}", [P, T], F32R) for i in range(NB)]
        ps = [st.ps(f"ps{i}", [P, T]) for i in range(4)]
        w_in = [st.sem(f"w_in{i}") for i in range(3)]
        b_in = st.sem("b_in")
        w_split, b_scaled, full, left, hi, lo = (st.sem(n) for n in ("w_split", "b_scaled", "full", "left", "hi", "lo"))
        stored = [st.sem(f"stored{i}") for i in range(NB)]
        items = [(w, b, m) for w in range(3) for b in range(HB) for m in range(KT)]
        dests = [[("qs", 0, 0), ("qs", 1, 1)],
                 [("k1", 0, 0), ("k1", 1, 0), ("k2", 0, 1), ("k2", 1, 1)],
                 [("vs", 0, 0), ("vs", 1, 1)]]
        total, stored_by = [0] * NB, []
        for n, (w, b, m) in enumerate(items):
            total[n % NB] += 16 * len(dests[w])
            stored_by.append(total[n % NB])
        with nc.Block() as block:

            @block.sync
            def _(sp):
                for i, n in enumerate(("w1q", "w1k", "w1v")):
                    sp.dma_start(raw[:, i], a[n].rearrange("(k p) n -> p k n", p=P)).then_inc(w_in[i], 16)
                    sp.dma_start(bias[:, i], a[("b1q", "b1k", "b1v")[i]]).then_inc(b_in, 16)
                for n, (w, b, m) in enumerate(items):
                    sp.wait_ge(lo, n + 1)
                    for name, part, low in dests[w]:
                        src = (ql if low else qh)[n % NB]
                        sp.dma_start(a[name][b, :, part, m * P:(m + 1) * P, :].rearrange("q p t -> p q t"),
                                     src[:].bitcast(F32).rearrange("p (q t) -> p q t", q=4)).then_inc(stored[n % NB], 16)
                for i in range(NB):
                    sp.wait_ge(stored[i], total[i])

            @block.gpsimd
            def _(pool):
                for w in range(3):
                    pool.wait_ge(w_in[w], 16)
                    for k in range(KT):
                        split_weight(nc, pool, raw[:, w, k], wh[:, w, k], wl[:, w, k], w_split, 2 * (w * KT + k))

            @block.tensor
            def _(pe):
                for n, (w, b, m) in enumerate(items):
                    if n >= 4:
                        pe.wait_ge(left, n - 3)
                    for k in range(KT):
                        if b == 0 and m == 0:
                            pe.wait_ge(w_split, 2 * (w * KT + k + 1))
                        t, c = slice(b * T, (b + 1) * T), slice(m * P, (m + 1) * P)
                        for i, (wp, hp) in enumerate(((wh, hh), (wh, hl), (wl, hh))):
                            mm = pe.matmul(ps[n % 4][:], wp[:, w, k, c], hp[:, k, t],
                                           start=(k == 0 and i == 0), stop=(k == KT - 1 and i == 2))
                    mm.then_inc(full, 1)

            @block.scalar
            def _(act):
                act.wait_ge(b_scaled, 1)
                for n, (w, b, m) in enumerate(items):
                    act.wait_ge(full, n + 1)
                    if n >= NB:
                        act.wait_ge(lo, n - NB + 1)
                    nc.scalar.activation(qf[n % NB][:], ps[n % 4][:], ACT.Identity, bias=bias[:, w, m:m + 1],
                                         scale=D1 ** -0.5 if w == 0 else 1.0).then_inc(left, 1)

            @block.vector
            def _(dve):
                dve.wait_ge(b_in, 48)
                nc.vector.tensor_scalar(bias[:, 0], bias[:, 0], D1 ** -0.5, None, ALU.mult).then_inc(b_scaled, 1)
                for n in range(len(items)):
                    dve.wait_ge(left, n + 1)
                    if n >= NB:
                        dve.wait_ge(stored[n % NB], stored_by[n - NB])
                    nc.vector.tensor_copy(qh[n % NB][:], qf[n % NB][:]).then_inc(hi, 1)
                    dve.wait_ge(hi, n + 1)
                    nc.vector.tensor_tensor(ql[n % NB][:], qf[n % NB][:], qh[n % NB][:].bitcast(F32), ALU.subtract).then_inc(lo, 1)


TQ = T // 4
NC_ = 8
TC = TQ // NC_


def stage_zero_diagonal(nc, bd):
    with Stage(nc, "zero") as st:
        zeroed = st.sem("zeroed")
        with nc.Block() as block:
            @block.vector
            def _(dve):
                nc.vector.memset(bd[:, 0:64, :].bitcast(F32), 0.0).then_inc(zeroed, 1)

            @block.gpsimd
            def _(pool):
                nc.gpsimd.memset(bd[:, 64:P, :].bitcast(F32), 0.0).then_inc(zeroed, 1)


def stage_head_attention(nc, a, bd, b):
    with Stage(nc, "heads") as st:
        kk = st.sb("kk", [P, 2, H1, TQ], F32R)
        prob = st.sb("prob", [P, TQ, H1])
        pt = st.sb("pt", [P, TQ, H1])
        pth, ptl = st.sb("pth", [P, TQ, H1], F32R), st.sb("ptl", [P, TQ, H1], F32R)
        o = st.sb("o", [P, H1, TQ])
        top = st.sb("top", [P, TQ, 1])
        den = st.sb("den", [P, TQ, 1])
        rden = st.sb("rden", [P, TQ, 1])
        pS = [st.ps(f"pS{i}", [P, TC, H1]) for i in range(6)]
        pO = [st.ps(f"pO{i}", [P, TC, H1]) for i in range(2)]
        q_in, k_in, v_in = st.sem("q_in"), st.sem("k_in"), st.sem("v_in")
        s_full, top_done, shifted, exp_done, masked, summed, recip, normed, turned, hi, lo = (st.sem(n) for n in (
            "s_full", "top_done", "shifted", "exp_done", "masked", "summed", "recip", "normed", "turned", "hi", "lo"))
        o_full, o_left, o_out = st.sem("o_full"), st.sem("o_left"), st.sem("o_out")
        ch = [slice(c * TC, (c + 1) * TC) for c in range(NC_)]

        def load_queries(eng, q):
            eng.dma_start(bd[32 * q:32 * q + 32, 32 * q:32 * q + 32, :].bitcast(F32),
                          a["qs"][bass.ds(b, 1), q].rearrange("o u (d h) t -> (o u d) h t", h=H1)).then_inc(q_in, 16)

        def load_values(eng, q):
            for u in range(2):
                c = 32 * q + D1 * u
                eng.dma_start(bd[32 * q:32 * q + 32, c:c + D1, :].bitcast(F32),
                              a["vs"][bass.ds(b, 1), q, u].rearrange("o (g d) t -> (o g) d t", d=D1)).then_inc(v_in, 16)

        with nc.Block() as block:

            @block.sync
            def _(sp):
                for u, n in enumerate(("k1", "k2")):
                    sp.dma_start(kk[:, u].bitcast(F32), a[n][bass.ds(b, 1)].rearrange("o q u (d h) t -> (o q u d) h t", h=H1)
                                 ).then_inc(k_in, 16)
                for q in (0, 2):
                    load_queries(sp, q)
                sp.wait_ge(s_full, NC_)
                for q in (0, 2):
                    load_values(sp, q)
                sp.wait_ge(o_left, NC_)
                sp.dma_start(a["attn"][bass.ds(b, 1)].rearrange("o q u (d h) t -> (o q u d) h t", h=H1), o[:]).then_inc(o_out, 16)
                sp.wait_ge(o_out, 16)

            @block.tensor
            def _(pe):
                pe.wait_ge(q_in, 64)
                pe.wait_ge(k_in, 32)
                for c in range(NC_):
                    if c >= 6:
                        pe.wait_ge(masked, c - 5)
                    for i in range(TC):
                        t = c * TC + i
                        for u in range(2):
                            mm = pe.matmul(pS[c % 6][:, i, :], bd[:, :, t], kk[:, u, :, t], start=(u == 0), stop=(u == 1))
                    mm.then_inc(s_full, 1)
                pe.wait_ge(v_in, 128)
                for c in range(NC_):
                    pe.wait_ge(lo, c + 1)
                    if c >= 2:
                        pe.wait_ge(o_left, c - 1)
                    for i in range(TC):
                        t = c * TC + i
                        for m, pp in enumerate((pth, ptl)):
                            mm = pe.matmul(pO[c % 2][:, i, :], bd[:, :, t], pp[:, t, :], start=(m == 0), stop=(m == 1))
                    mm.then_inc(o_full, 1)

            @block.scalar
            def _(act):
                for q in (1, 3):
                    load_queries(act, q)
                for c in range(NC_):
                    act.wait_ge(shifted, c + 1)
                    nc.scalar.activation(prob[:, ch[c], :], prob[:, ch[c], :], ACT.Exp).then_inc(exp_done, 1)
                    if c == 5:
                        act.wait_ge(s_full, NC_)
                        for q in (1, 3):
                            load_values(act, q)
                    if c >= 2:
                        act.wait_ge(turned, c - 1)
                        nc.scalar.copy(pth[:, ch[c - 2], :], pt[:, ch[c - 2], :]).then_inc(hi, 1)
                for c in (NC_ - 2, NC_ - 1):
                    act.wait_ge(turned, c + 1)
                    nc.scalar.copy(pth[:, ch[c], :], pt[:, ch[c], :]).then_inc(hi, 1)
                for c in range(NC_):
                    act.wait_ge(o_full, c + 1)
                    nc.scalar.copy(o[:, :, ch[c]], pO[c % 2][:].rearrange("p t h -> p h t")).then_inc(o_left, 1)

            @block.vector
            def _(dve):
                wide = [P, TC, H1]

                def first(c):
                    dve.wait_ge(s_full, c + 1)
                    nc.vector.tensor_reduce(top[:, ch[c], :], pS[c % 6][:], AX.X, ALU.max).then_inc(top_done, 1)
                    dve.wait_ge(top_done, c + 1)
                    nc.vector.tensor_tensor(prob[:, ch[c], :], pS[c % 6][:], top[:, ch[c], :].to_broadcast(wide),
                                            ALU.subtract).then_inc(shifted, 1)

                def second(c):
                    dve.wait_ge(exp_done, c + 1)
                    nc.vector.scalar_tensor_tensor(prob[:, ch[c], :], pS[c % 6][:], THRESH, prob[:, ch[c], :],
                                                   ALU.is_gt, ALU.mult).then_inc(masked, 1)
                    dve.wait_ge(masked, c + 1)
                    nc.vector.tensor_reduce(den[:, ch[c], :], prob[:, ch[c], :], AX.X, ALU.add).then_inc(summed, 1)
                    dve.wait_ge(summed, c + 1)
                    nc.vector.reciprocal(rden[:, ch[c], :], den[:, ch[c], :]).then_inc(recip, 1)

                def third(c):
                    dve.wait_ge(normed, c + 1)
                    nc.vector.transpose(pt[:, ch[c], :].rearrange("p t h -> p (t h)"),
                                        prob[:, ch[c], :].rearrange("p t h -> p (t h)")).then_inc(turned, 1)

                for c in range(NC_ + 2):
                    if c < NC_:
                        first(c)
                    if 1 <= c <= NC_:
                        second(c - 1)
                    if c >= 2:
                        third(c - 2)

            @block.gpsimd
            def _(pool):
                for c in range(NC_ + 1):
                    if c < NC_:
                        pool.wait_ge(recip, c + 1)
                        nc.gpsimd.tensor_tensor(prob[:, ch[c], :], prob[:, ch[c], :], rden[:, ch[c], :].to_broadcast([P, TC, H1]),
                                                ALU.mult).then_inc(normed, 1)
                    if c:
                        pool.wait_ge(hi, c)
                        nc.gpsimd.tensor_tensor(ptl[:, ch[c - 1], :], pt[:, ch[c - 1], :], pth[:, ch[c - 1], :].bitcast(F32),
                                                ALU.subtract).then_inc(lo, 1)


def stage_attention_out(nc, held, a):
    with Stage(nc, "wo1") as st:
        y, hh, hl = held.y, held.hh, held.hl
        raw = st.sb("raw", [P, KT, D])
        at = st.sb("at", [P, 2, KT, HB * T])
        wh, wl = st.sb("wh", [P, KT, D], F32R), st.sb("wl", [P, KT, D], F32R)
        bo = st.sb("bo", [P, D])
        ps = [st.ps(f"ps{i}", [P, D]) for i in range(8)]
        w_in, b_in, w_split, summed, hi, lo, full, biased = (st.sem(n) for n in (
            "w_in", "b_in", "w_split", "summed", "hi", "lo", "full", "biased"))
        a_in = [st.sem(f"a_in{b}") for b in range(HB)]
        with nc.Block() as block:

            @block.sync
            def _(sp):
                sp.dma_start(raw[:], a["w1o"].rearrange("(k p) n -> p k n", p=P)).then_inc(w_in, 16)
                for b in range(HB):
                    for k in range(KT):
                        for u in range(2):
                            sp.dma_start(at[:, u, k, b * T:(b + 1) * T].rearrange("p (q t) -> p q t", q=4),
                                         a["attn"][b, :, u, k * P:(k + 1) * P, :].rearrange("q p t -> p q t")).then_inc(a_in[b], 16)
                sp.dma_start(bo[:], a["b1o"].rearrange("(o d) -> o d", o=1).to_broadcast([P, D])).then_inc(b_in, 16)

            @block.gpsimd
            def _(pool):
                pool.wait_ge(w_in, 16)
                for k in range(KT):
                    split_weight(nc, pool, raw[:, k], wh[:, k], wl[:, k], w_split, 2 * k)

            @block.tensor
            def _(pe):
                pe.wait_ge(w_split, 2 * KT)
                for j in range(NT):
                    pe.wait_ge(lo, (j // TT + 1) * KT)
                    for k in range(KT):
                        for i, (hp, wp) in enumerate(((hh, wh), (hh, wl), (hl, wh))):
                            mm = pe.matmul(ps[j][:], hp[:, k, j * P:(j + 1) * P], wp[:, k, :],
                                           start=(k == 0 and i == 0), stop=(k == KT - 1 and i == 2))
                    mm.then_inc(full, 1)

            @block.scalar
            def _(act):
                for i in range(HB * KT):
                    b, k = i // KT, i % KT
                    act.wait_ge(summed, i + 1)
                    nc.scalar.copy(hh[:, k, b * T:(b + 1) * T], at[:, 0, k, b * T:(b + 1) * T]).then_inc(hi, 1)

            @block.vector
            def _(dve):
                for i in range(HB * KT + 1):
                    if i < HB * KT:
                        b, k = i // KT, i % KT
                        dve.wait_ge(a_in[b], 32 * KT)
                        nc.vector.tensor_tensor(at[:, 0, k, b * T:(b + 1) * T], at[:, 0, k, b * T:(b + 1) * T],
                                                at[:, 1, k, b * T:(b + 1) * T], ALU.add).then_inc(summed, 1)
                    if i:
                        b, k = (i - 1) // KT, (i - 1) % KT
                        dve.wait_ge(hi, i)
                        nc.vector.tensor_tensor(hl[:, k, b * T:(b + 1) * T], at[:, 0, k, b * T:(b + 1) * T],
                                                hh[:, k, b * T:(b + 1) * T].bitcast(F32), ALU.subtract).then_inc(lo, 1)
                dve.wait_ge(b_in, 16)
                for j in range(NT):
                    dve.wait_ge(full, j + 1)
                    nc.vector.tensor_tensor(y[:, j, :], ps[j][:], bo[:], ALU.add).then_inc(biased, 1)


def stage_lora(nc, held, a, half):
    with Stage(nc, "ffn1") as st:
        x, hh, hl = held.x, held.hh, held.hl
        NA = NE * R1 + NE
        rawA, rawB = st.sb("rawA", [P, KT, NA]), st.sb("rawB", [P, D])
        ah, al = st.sb("ah", [P, KT, NA], F32R), st.sb("al", [P, KT, NA], F32R)
        bh, bl = st.sb("bh", [P, D], F32R), st.sb("bl", [P, D], F32R)
        gate = st.sb("gate", [P, HB, D])
        hs = st.sb("hs", [P, NT, NA])
        top = st.sb("top", [P, NT, 1])
        rank = st.sb("rank", [P, NT, NE])
        best = st.sb("best", [P, NT, 1])
        route = st.sb("route", [P, NT, NE])
        wt = st.sb("wt", [P, NT, NE * R1])
        wth, wtl = st.sb("wth", [P, NT * P], F32R), st.sb("wtl", [P, NT * P], F32R)
        yg = [st.sb(f"yg{i}", [P, D]) for i in range(2)]
        ps = [st.ps(f"ps{i}", [P, D]) for i in range(4)]
        pT = [st.ps(f"pT{i}", [P, T]) for i in range(2)]
        a_in, b_in, gate_in = st.sem("a_in"), st.sem("b_in"), st.sem("gate_in")
        w_split, h_full, h_left, pick, routed = (st.sem(n) for n in ("w_split", "h_full", "h_left", "pick", "routed"))
        turned, hi, lo, full, gated, added, stored = (st.sem(n) for n in ("turned", "hi", "lo", "full", "gated", "added", "stored"))
        with nc.Block() as block:

            @block.sync
            def _(sp):
                sp.dma_start(rawA[:, :, 0:NE * R1], a["loraAT"].rearrange("(k p) n -> p k n", p=P)).then_inc(a_in, 16)
                sp.dma_start(rawA[:, :, NE * R1:], a["routeT"].rearrange("(k p) n -> p k n", p=P)).then_inc(a_in, 16)
                sp.dma_start(rawB[:], a["loraBT"]).then_inc(b_in, 16)
                for b in range(HB):
                    sp.dma_start(gate[:, b, :], a["gates"][3, bass.ds(half * HB + b, 1), :].to_broadcast([P, D])).then_inc(gate_in, 16)
                for j in range(NT):
                    sp.wait_ge(added, j + 1)
                    sp.dma_start(a["out"][bass.ds(half * HB * T + j * P, P), :], x[:, j, :]).then_inc(stored, 16)
                sp.wait_ge(stored, 16 * NT)

            @block.gpsimd
            def _(pool):
                pool.wait_ge(a_in, 32)
                split_weight(nc, pool, rawA[:], ah[:], al[:], w_split, 0)
                pool.wait_ge(b_in, 16)
                split_weight(nc, pool, rawB[:], bh[:], bl[:], w_split, 2)
                for j in range(NT):
                    pool.wait_ge(gated, j + 1)
                    nc.gpsimd.tensor_tensor(x[:, j, :], x[:, j, :], yg[j % 2][:], ALU.add).then_inc(added, 1)

            @block.tensor
            def _(pe):
                pe.wait_ge(w_split, 2)
                for j in range(NT):
                    if j >= 4:
                        pe.wait_ge(h_left, j - 3)
                    for k in range(KT):
                        for i, (hp, wp) in enumerate(((hh, ah), (hh, al), (hl, ah))):
                            mm = pe.matmul(ps[j % 4][:, 0:NA], hp[:, k, j * P:(j + 1) * P], wp[:, k, :],
                                           start=(k == 0 and i == 0), stop=(k == KT - 1 and i == 2))
                    mm.then_inc(h_full, 1)
                pe.wait_ge(routed, 1)
                for b in range(HB):
                    for j in range(TT):
                        mm = pe.transpose(pT[b][:, j * P:(j + 1) * P], wt[:, b * TT + j, :], held.ident)
                    mm.then_inc(turned, 1)
                pe.wait_ge(w_split, 4)
                for j in range(NT):
                    pe.wait_ge(lo, j // TT + 1)
                    if j < 4:
                        pe.wait_ge(h_left, NT)
                    else:
                        pe.wait_ge(gated, j - 3)
                    for i, (wp, bp) in enumerate(((wth, bh), (wth, bl), (wtl, bh))):
                        mm = pe.matmul(ps[j % 4][:], wp[:, j * P:(j + 1) * P], bp[:], start=(i == 0), stop=(i == 2))
                    mm.then_inc(full, 1)

            @block.scalar
            def _(act):
                for j in range(NT):
                    act.wait_ge(h_full, j + 1)
                    nc.scalar.copy(hs[:, j, :], ps[j % 4][:, 0:NA]).then_inc(h_left, 1)
                for b in range(HB):
                    act.wait_ge(turned, b + 1)
                    nc.scalar.copy(wth[:, b * T:(b + 1) * T], pT[b][:]).then_inc(hi, 1)

            @block.vector
            def _(dve):
                n = [0]

                def link(ins):
                    n[0] += 1
                    ins.then_inc(pick, 1)
                    dve.wait_ge(pick, n[0])

                dve.wait_ge(h_left, NT)
                logits = hs[:, :, NE * R1:]
                wide = [P, NT, NE]
                link(nc.vector.tensor_reduce(top[:], logits, AX.X, ALU.max))
                link(nc.vector.tensor_tensor(rank[:], logits, top[:].to_broadcast(wide), ALU.is_ge))
                for j in range(NT):
                    ins = nc.vector.tensor_tensor(route[:, j, :], rank[:, j, :], held.ranks, ALU.mult)
                link(ins)
                link(nc.vector.tensor_reduce(best[:], route[:], AX.X, ALU.max))
                link(nc.vector.tensor_tensor(rank[:], route[:], best[:].to_broadcast(wide), ALU.is_equal))
                link(nc.vector.tensor_tensor(route[:], rank[:], top[:].to_broadcast(wide), ALU.mult))
                for j in range(NT):
                    ins = nc.vector.tensor_tensor(wt[:, j, :].rearrange("p (e r) -> p e r", e=NE),
                                                  hs[:, j, 0:NE * R1].rearrange("p (e r) -> p e r", e=NE),
                                                  route[:, j, :].rearrange("p (e o) -> p e o", o=1).to_broadcast([P, NE, R1]), ALU.mult)
                ins.then_inc(routed, 1)
                for b in range(HB):
                    dve.wait_ge(hi, b + 1)
                    nc.vector.tensor_tensor(wtl[:, b * T:(b + 1) * T], pT[b][:], wth[:, b * T:(b + 1) * T].bitcast(F32),
                                            ALU.subtract).then_inc(lo, 1)
                dve.wait_ge(gate_in, 16 * HB)
                for j in range(NT):
                    dve.wait_ge(full, j + 1)
                    if j >= 2:
                        dve.wait_ge(added, j - 1)
                    nc.vector.tensor_tensor(yg[j % 2][:], ps[j % 4][:], gate[:, j // TT, :], ALU.mult).then_inc(gated, 1)


def build(nc, a):
    with ExitStack() as ctx:
        sb = lambda n, s, dt=F32: ctx.enter_context(nc.sbuf_tensor(n, s, dt))
        held = Held()
        W = 2 * T + 2 * P + NE
        held.consts = sb("consts", [P, W])
        held.cosT, held.sinT = held.consts[:, 0:T], held.consts[:, T:2 * T]
        held.ident = held.consts[:, 2 * T:2 * T + P]
        held.mask = held.consts[:, 2 * T + P:2 * T + 2 * P]
        held.ranks = held.consts[:, 2 * T + 2 * P:]
        held.identb, held.maskb = sb("identb", [P, P], BF16), sb("maskb", [P, P], BF16)
        held.modT = sb("modT", [P, 2, 4, KT, B])
        held.modh = sb("modh", [P, 2, 4, KT, HB])
        stage_modulation(nc, held, a)
        held.x = sb("x", [P, NT, D])

        def working(wctx, name):
            wsb = lambda n, s, dt=F32: wctx.enter_context(nc.sbuf_tensor(f"{name}_{n}", s, dt))
            held.y = wsb("y", [P, NT, D])
            held.hh, held.hl = wsb("hh", [P, KT, HB * T], F32R), wsb("hl", [P, KT, HB * T], F32R)

        with nc.Fori(0, B // HB) as half:
            stage_half_mod(nc, held, half)
            with ExitStack() as wctx:
                working(wctx, "first")
                with ExitStack() as gctx:
                    wts = GroupWeights(gctx, nc, a)
                    stage_norm(nc, held, a, 0, 0, half, weights=wts)
                    with nc.Fori(0, G // GB) as g:
                        stage_groups(nc, held, a, wts, g * GB)
                stage_norm(nc, held, a, 0, 1, half, residual=0)
                stage_sign_ffn(nc, held, a)
                stage_norm(nc, held, a, 1, 0, half, residual=1)
                stage_qkv(nc, held, a)
            with nc.sbuf_tensor("bd", [P, P, TQ], F32R) as bd:
                stage_zero_diagonal(nc, bd)
                with nc.Fori(0, HB) as b:
                    stage_head_attention(nc, a, bd, b)
            with ExitStack() as wctx:
                working(wctx, "second")
                stage_attention_out(nc, held, a)
                stage_norm(nc, held, a, 1, 1, half, residual=2)
                stage_lora(nc, held, a, half)


def kernel(**inputs):
    import numpy as _np
    import concourse.bacc as _bacc
    from concourse import mybir as _mybir
    from concourse.bass_utils import run_bass_kernel_spmd as _run

    i = {k: _np.asarray(v) for k, v in inputs.items()}
    wq = i["L0_attn_wq"]
    dim_head = _np.arange(D).reshape(H1, D1).T.reshape(-1)
    arrays = {
        "x": i["L0_attn_x"].reshape(B * T, D), "wq": wq, "wkv": _np.stack([i["L0_attn_wk"], i["L0_attn_wv"]]),
        "wo": i["L0_attn_wo"], "w_sign": i["L0_ffn_weight"], "w_signT": i["L0_ffn_weight"].T,
        "scale_param": i["L0_ffn_scale_param"].reshape(KT, P).T, "c0T": i["L0_c"].T, "c1T": i["L1_c"].T,
        "wmod0": i["L0_wmod"], "wmod1": i["L1_wmod"],
        "w1q": i["L1_attn_Wq"][dim_head].T, "w1k": i["L1_attn_Wk"][dim_head].T, "w1v": i["L1_attn_Wv"].T,
        "w1o": i["L1_attn_Wo"].T[dim_head],
        "b1q": i["L1_attn_bq"][dim_head].reshape(KT, P).T, "b1k": i["L1_attn_bk"][dim_head].reshape(KT, P).T,
        "b1v": i["L1_attn_bv"].reshape(KT, P).T, "b1o": i["L1_attn_bo"],
        "routeT": i["L1_ffn_route_w"].T, "loraAT": i["L1_ffn_A"].reshape(NE * R1, D).T,
        "loraBT": i["L1_ffn_Bw"].transpose(0, 2, 1).reshape(NE * R1, D), "tables": tables(),
    }
    arrays = {f"in_{k}": _np.ascontiguousarray(v) for k, v in arrays.items()}
    nc = _bacc.Bacc("TRN2", target_bir_lowering=False, num_devices=1)
    a = {k[3:]: nc.dram_tensor(k, v.shape, _mybir.dt.from_np(v.dtype), kind="ExternalInput").ap() for k, v in arrays.items()}
    a["out"] = nc.dram_tensor("out", (B * T, D), F32, kind="ExternalOutput").ap()
    a["gates"] = nc.dram_tensor("gates", (4, B, D), F32).ap()
    a["row_scale"] = nc.dram_tensor("row_scale", (D,), F32).ap()
    for n in ("qs", "k1", "k2", "vs"):
        a[n] = nc.dram_tensor(n, (HB, 4, 2, D, TQ), F32).ap()
    a["attn"] = nc.dram_tensor("attn", (HB, 4, 2, D, TQ), F32).ap()
    build(nc, a)
    r = _run(nc, [arrays], core_ids=[0])
    return r.results[0]["out"].reshape(B, T, D)
```

```python
from contextlib import ExitStack

import numpy as np
import concourse.bass as bass
from concourse import mybir

F32 = mybir.dt.float32
F32R = mybir.dt.float32r
BF16 = mybir.dt.bfloat16
I32 = mybir.dt.int32
ALU = mybir.AluOpType
ACT = mybir.ActivationFunctionType
AX = mybir.AxisListType

P = 128
B, T, D = 4, 512, 512
KT = D // P
HB = 2
NT = HB * T // P
TT = T // P
G, R0, HD = 8, 4, 128
H1, D1 = 32, 16
THRESH = 0.001
NE, R1 = 8, 16
EPS = 1e-5
MASKED = -1e30
MAGIC = 0x5F3759DF
LIMIT = 1000000.0
FIRST_SEM = 160


def tables():
    inv = 1.0 / 500000.0 ** (np.arange(0, HD, 2, dtype=np.float64) / HD)
    wave = 2.0 * np.pi / inv
    low, high = 1024 / 1.0, 1024 / 4.0
    smooth = (1024 / wave - 1.0) / (4.0 - 1.0)
    scaled = np.where(wave > low, inv / 8.0, inv)
    mid = (wave <= low) & (wave >= high)
    scaled = np.where(mid, (1 - smooth) * inv / 8.0 + smooth * inv, scaled).astype(np.float32)
    freqs = np.arange(T, dtype=np.float32)[:, None] * scaled[None, :]
    emb = np.concatenate([freqs, freqs], axis=-1)
    cos, sin = np.cos(emb).T, np.sin(emb).T
    sign = np.where(np.arange(HD) < HD // 2, -1.0, 1.0).astype(np.float32)[:, None]
    mask = np.where(np.arange(P)[None, :] <= np.arange(P)[:, None], 0.0, MASKED)
    ranks = np.broadcast_to(8.0 - np.arange(NE), (P, NE))
    parts = [cos, sin * sign, np.eye(P), mask, ranks]
    return np.ascontiguousarray(np.concatenate([p.astype(np.float32) for p in parts], axis=1))


class Stage:

    def __init__(self, nc, name):
        self.nc, self.name, self.ctx, self.sems = nc, name, ExitStack(), []

    def __enter__(self):
        return self

    def sb(self, name, shape, dt=F32):
        return self.ctx.enter_context(self.nc.sbuf_tensor(f"{self.name}_{name}", shape, dt))

    def ps(self, name, shape):
        return self.ctx.enter_context(self.nc.psum_tensor(f"{self.name}_{name}", shape, F32))

    def sem(self, name):
        s = self.ctx.enter_context(self.nc.semaphore(f"{self.name}_{name}", num=FIRST_SEM + len(self.sems)))
        self.sems.append(s.num)
        return s

    def __exit__(self, *e):
        if e[0] is None:
            self.nc.all_engine_barrier(sems_to_clear=range(self.sems[0], self.sems[-1] + 1))
        return self.ctx.__exit__(*e)


class Held:
    pass


def stage_modulation(nc, held, a):
    with Stage(nc, "mod") as st:
        NCH = 6
        cT = st.sb("cT", [P, KT, 2 * B])
        ec = st.sb("ec", [P, KT, 2 * B])
        silu = st.sb("silu", [P, KT, 2 * B])
        wm = [st.sb(f"wm{l}", [P, KT, NCH * D]) for l in range(2)]
        row = st.sb("row", [B, 2, NCH, D])
        gate = st.sb("gate", [B, 4, D])
        gabs = st.sb("gabs", [B, 4, D])
        gsgn = st.sb("gsgn", [B, 4, D])
        w = st.sb("w", [P, KT, D])
        sp = st.sb("sp", [P, KT])
        rs = st.sb("rs", [P, KT])
        pr = [st.ps(f"pr{i}", [B, D]) for i in range(NCH)]
        pc = [st.ps(f"pc{l}", [P, 4, KT, B]) for l in range(2)]
        const_in = st.sem("const_in")
        c_in = st.sem("c_in")
        wm_in = [[st.sem(f"wm_in{l}{k}") for k in range(KT)] for l in range(2)]
        w_in = st.sem("w_in")
        c_exp = st.sem("c_exp")
        silu_step = st.sem("silu_step")
        silu_done = st.sem("silu_done")
        row_full, row_out, col_full, gate_step = (st.sem(n) for n in ("row_full", "row_out", "col_full", "gate_step"))
        held_done = st.sem("held_done")
        rows_out = st.sem("rows_out")
        COLS = [0, 1, 3, 4]
        with nc.Block() as block:

            @block.sync
            def _(sp_):
                for l, c in enumerate((a["c0T"], a["c1T"])):
                    sp_.dma_start(cT[:, :, l * B:(l + 1) * B],
                                  c.rearrange("(k p) b -> p k b", p=P)).then_inc(c_in, 16)
                for l, m in enumerate((a["wmod0"], a["wmod1"])):
                    for k in range(KT):
                        sp_.dma_start(wm[l][:, k], m[k * P:(k + 1) * P, :]).then_inc(wm_in[l][k], 16)
                sp_.wait_ge(gate_step, 5)
                sp_.dma_start(a["gates"].rearrange("g b d -> b g d"), gate[:]).then_inc(rows_out, 16)
                sp_.wait_ge(rows_out, 32)

            @block.scalar
            def _(act):
                act.dma_start(held.consts[:], a["tables"]).then_inc(const_in, 16)
                act.wait_ge(c_in, 32)
                nc.scalar.activation(ec[:], cT[:], ACT.Exp, scale=-1.0).then_inc(c_exp, 1)
                act.wait_ge(wm_in[0][2], 16)
                act.dma_start(w[:], a["w_sign"].rearrange("(k p) n -> p k n", p=P)).then_inc(w_in, 16)
                act.dma_start(sp[:], a["scale_param"]).then_inc(w_in, 16)
                for i in range(2 * NCH):
                    act.wait_ge(row_full, i + 1)
                    nc.scalar.copy(row[:, i // NCH, i % NCH], pr[i % NCH][:]).then_inc(row_out, 1)
                act.wait_ge(silu_step, 5)
                act.dma_start(a["row_scale"].rearrange("(k p) -> p k", p=P), rs[:], allow_slow_non_contiguous=True).then_inc(rows_out, 16)

            @block.tensor
            def _(pe):
                pe.wait_ge(silu_done, 1)
                for l in range(2):
                    for k in range(KT):
                        pe.wait_ge(wm_in[l][k], 16)
                        for i in range(NCH):
                            if l and k == 0:
                                pe.wait_ge(row_out, i + 1)
                            mm = pe.matmul(pr[i][:], silu[:, k, l * B:(l + 1) * B], wm[l][:, k, i * D:(i + 1) * D],
                                           start=(k == 0), stop=(k == KT - 1))
                            if k == KT - 1:
                                mm.then_inc(row_full, 1)
                pe.wait_ge(const_in, 16)
                for l in range(2):
                    pe.wait_ge(row_out, (l + 1) * NCH)
                    for ci, c in enumerate(COLS):
                        for m in range(KT):
                            mm = pe.transpose(pc[l][:, ci, m, :], row[:, l, c, m * P:(m + 1) * P], held.ident[0:B, 0:B])
                    mm.then_inc(col_full, 1)

            @block.vector
            def _(dve):
                dve.wait_ge(c_exp, 1)
                nc.vector.tensor_scalar_add(ec[:], ec[:], 1.0).then_inc(silu_step, 1)
                dve.wait_ge(silu_step, 1)
                nc.vector.reciprocal(ec[:], ec[:]).then_inc(silu_step, 1)
                dve.wait_ge(silu_step, 2)
                nc.vector.tensor_tensor(silu[:], cT[:], ec[:], ALU.mult).then_inc(silu_done, 1)
                dve.wait_ge(const_in, 16)
                nc.vector.tensor_copy(held.identb[:], held.ident).then_inc(held_done, 1)
                nc.vector.tensor_copy(held.maskb[:], held.mask).then_inc(held_done, 1)
                nc.vector.memset(held.zerob[:], 0.0).then_inc(held_done, 1)
                dve.wait_ge(w_in, 32)
                nc.vector.tensor_reduce(rs[:], w[:], AX.X, ALU.add, apply_absolute_value=True).then_inc(silu_step, 1)
                dve.wait_ge(silu_step, 3)
                nc.vector.tensor_scalar(rs[:], rs[:], 1.0 / D, 1e-8, ALU.mult, ALU.max).then_inc(silu_step, 1)
                dve.wait_ge(silu_step, 4)
                nc.vector.tensor_tensor(rs[:], rs[:], sp[:], ALU.mult).then_inc(silu_step, 1)
                dve.wait_ge(row_out, 2 * NCH)
                g = row[:].rearrange("b l (w c) d -> b (l w) c d", c=3)[:, :, 2, :]
                nc.vector.scalar_tensor_tensor(gabs[:], g, -1.0, g, ALU.mult, ALU.max).then_inc(gate_step, 1)
                nc.vector.tensor_scalar(gsgn[:], g, 0.0, 2.0, ALU.is_ge, ALU.mult).then_inc(gate_step, 1)
                dve.wait_ge(gate_step, 2)
                nc.vector.tensor_scalar_max(gabs[:], gabs[:], 0.25).then_inc(gate_step, 1)
                nc.vector.tensor_scalar_add(gsgn[:], gsgn[:], -1.0).then_inc(gate_step, 1)
                dve.wait_ge(gate_step, 4)
                nc.vector.tensor_tensor(gate[:], gabs[:], gsgn[:], ALU.mult).then_inc(gate_step, 1)
                for l in range(2):
                    dve.wait_ge(col_full, l + 1)
                    for ci in range(4):
                        nc.vector.tensor_scalar(held.modT[:, l, ci, :, :], pc[l][:, ci, :, :],
                                                float(ci % 2), None, ALU.add).then_inc(held_done, 1)


class SignWeights:

    def __init__(self, ctx, nc, a):
        sb = lambda n, s, dt=F32: ctx.enter_context(nc.sbuf_tensor(n, s, dt))
        self.nc, self.a = nc, a
        self.wT, self.sgn, self.rs = sb("sign_raw", [P, KT, D]), sb("sgn", [P, KT, D], F32R), sb("rs", [P, D])

    def sems(self, st):
        self.came, self.signed = st.sem("came"), st.sem("signed")

    def load(self, act):
        act.dma_start(self.wT[:], self.a["w_signT"].rearrange("(k p) n -> p k n", p=P)).then_inc(self.came, 16)
        act.dma_start(self.rs[:], self.a["row_scale"].rearrange("(o d) -> o d", o=1).to_broadcast([P, D])).then_inc(self.came, 16)

    def his(self, act):
        act.wait_ge(self.came, 32)
        for k in range(KT):
            self.nc.scalar.activation(self.sgn[:, k], self.wT[:, k], ACT.Sign).then_inc(self.signed, 1)

    def los(self, pool):
        pass


QKV_ORDER = (1, 0, 2)


class QkvWeights:

    def __init__(self, ctx, nc, a):
        sb = lambda n, s, dt=F32: ctx.enter_context(nc.sbuf_tensor(n, s, dt))
        self.nc, self.a = nc, a
        self.raw, self.bias = sb("qkv_raw", [P, 3, KT, D]), sb("qkv_bias", [P, 3, KT])
        self.wh, self.wl = sb("qkv_wh", [P, 3, KT, D], F32R), sb("qkv_wl", [P, 3, KT, D], F32R)

    def sems(self, st):
        self.b_came, self.hi, self.lo = st.sem("b_came"), st.sem("ahead_hi"), st.sem("ahead_lo")
        self.came = [st.sem(f"came{i}") for i in range(3)]

    def load(self, act):
        for i in range(3):
            act.dma_start(self.bias[:, i], self.a[("b1q", "b1k", "b1v")[i]]).then_inc(self.b_came, 16)
        for i in QKV_ORDER:
            act.dma_start(self.raw[:, i], self.a[("w1q", "w1k", "w1v")[i]].rearrange("(k p) n -> p k n", p=P)).then_inc(self.came[i], 16)

    def his(self, act):
        act.wait_ge(self.b_came, 48)
        for i in QKV_ORDER:
            act.wait_ge(self.came[i], 16)
            for k in range(KT):
                self.nc.scalar.copy(self.wh[:, i, k], self.raw[:, i, k]).then_inc(self.hi, 1)

    def lo_part(self, i, k):
        return self.nc.gpsimd.tensor_tensor(self.wl[:, i, k], self.raw[:, i, k], self.wh[:, i, k].bitcast(F32), ALU.subtract)

    def los(self, pool):
        for k in range(KT):
            pool.wait_ge(self.hi, k + 1)
            self.lo_part(QKV_ORDER[0], k).then_inc(self.lo, 1)


class LoraWeights:

    def __init__(self, ctx, nc, a):
        sb = lambda n, s, dt=F32: ctx.enter_context(nc.sbuf_tensor(n, s, dt))
        self.nc, self.a = nc, a
        self.NA = NE * R1 + NE
        self.rawA, self.rawB = sb("rawA", [P, KT, self.NA]), sb("rawB", [P, D])
        self.ah, self.al = sb("lora_ah", [P, KT, NARROW], F32R), sb("lora_al", [P, KT, NARROW], F32R)
        self.bh, self.bl = sb("lora_bh", [P, D], F32R), sb("lora_bl", [P, D], F32R)

    def sems(self, st):
        self.came, self.padded, self.hi, self.lo = (st.sem(n) for n in ("came", "padded", "ahead_hi", "ahead_lo"))

    def load(self, act):
        act.dma_start(self.rawA[:, :, 0:NE * R1], self.a["loraAT"].rearrange("(k p) n -> p k n", p=P)).then_inc(self.came, 16)
        act.dma_start(self.rawA[:, :, NE * R1:], self.a["routeT"].rearrange("(k p) n -> p k n", p=P)).then_inc(self.came, 16)
        act.dma_start(self.rawB[:], self.a["loraBT"]).then_inc(self.came, 16)

    def his(self, act):
        act.wait_ge(self.came, 48)
        self.nc.scalar.copy(self.ah[:, :, 0:self.NA], self.rawA[:]).then_inc(self.hi, 1)
        self.nc.scalar.copy(self.bh[:], self.rawB[:]).then_inc(self.hi, 1)

    def los(self, pool):
        NA = self.NA
        self.nc.gpsimd.memset(self.ah[:, :, NA:].bitcast(F32), 0.0).then_inc(self.padded, 1)
        self.nc.gpsimd.memset(self.al[:, :, NA:].bitcast(F32), 0.0).then_inc(self.padded, 1)
        pool.wait_ge(self.hi, 2)
        self.nc.gpsimd.tensor_tensor(self.al[:, :, 0:NA], self.rawA[:], self.ah[:, :, 0:NA].bitcast(F32), ALU.subtract).then_inc(self.lo, 1)
        self.nc.gpsimd.tensor_tensor(self.bl[:], self.rawB[:], self.bh[:].bitcast(F32), ALU.subtract).then_inc(self.lo, 1)


def load_gates(eng, held, a, which, half, sem):
    for b in range(HB):
        eng.dma_start(held.gate[:, b, :], a["gates"][which, bass.ds(half * HB + b, 1), :].to_broadcast([P, D])).then_inc(sem, 16)
    eng.wait_ge(sem, 16 * HB)


def stage_norm(nc, held, a, layer, which, half, residual=None, weights=None, ahead=None):
    with Stage(nc, f"ln{layer}{which}") as st:
        x, y, hh, hl = held.x, held.y, held.hh, held.hl
        xn = st.sb("xn", [P, NT, D])
        hf = st.sb("hf", [P, HB * KT, T])
        gate = held.gate
        stats = st.sb("stats", [P, NT, 6])
        mv = st.sb("mv", [P, NT, 2])
        var = st.sb("var", [P, NT])
        rstd = st.sb("rstd", [P, NT])
        step = st.sb("step", [P, NT])
        pT = [st.ps(f"pT{i}", [P, T]) for i in range(HB * KT)]
        x_in = [st.sem(f"x_in{b}") for b in range(HB)]
        gate_in = st.sem("gate_in")
        own_gated, gated, x_new, stat_done, newton = (st.sem(n) for n in ("own_gated", "gated", "x_new", "stat_done", "newton"))
        xn_done, turned, scaled = (st.sem(n) for n in ("xn_done", "turned", "scaled"))
        act_hi, dve_hi, dve_lo, pool_lo = (st.sem(n) for n in ("act_hi", "dve_hi", "dve_lo", "pool_lo"))
        split_hi, split_lo = st.sem("split_hi"), st.sem("split_lo")
        w_in = st.sem("w_in")
        y_clear = st.sem("y_clear")
        ci = 2 * which
        if ahead:
            ahead.sems(st)
        NEWTON = 3
        with nc.Block() as block:

            @block.sync
            def _(sp):
                for b in range(HB):
                    if residual is None:
                        sp.dma_start(x[:, b * TT:(b + 1) * TT, :],
                                     a["x"][bass.ds(half * HB * T + b * T, T), :].rearrange("(j p) d -> p j d", p=P)
                                     ).then_inc(x_in[b], 16)
                if residual is None:
                    load_gates(sp, held, a, 0, half, gate_in)

            @block.gpsimd
            def _(pool):
                if residual is not None:
                    for j in range(NT):
                        if j % TT:
                            nc.gpsimd.tensor_tensor(y[:, j, :], y[:, j, :], gate[:, j // TT, :], ALU.mult).then_inc(gated, 1)
                if weights:
                    for n, (what, i) in enumerate(FIRST_PARTS):
                        pool.wait_ge(split_hi, n + 1)
                        weights.split_lo(what, i).then_inc(split_lo, 1)
                if ahead:
                    ahead.los(pool)
                for k in range(KT):
                    pool.wait_ge(act_hi, k + 1)
                    nc.gpsimd.tensor_tensor(hl[:, k, 0:T], hf[:, k, :], hh[:, k, 0:T].bitcast(F32), ALU.subtract).then_inc(pool_lo, 1)
                for k in range(2):
                    pool.wait_ge(dve_hi, k + 1)
                    nc.gpsimd.tensor_tensor(hl[:, k, T:2 * T], hf[:, KT + k, :], hh[:, k, T:2 * T].bitcast(F32),
                                            ALU.subtract).then_inc(pool_lo, 1)

            @block.vector
            def _(dve):
                n = [0]

                def link(ins):
                    n[0] += 1
                    ins.then_inc(newton, 1)
                    dve.wait_ge(newton, n[0])

                def normalise(b):
                    tiles, s = range(b * TT, (b + 1) * TT), slice(b * TT, (b + 1) * TT)
                    for j in tiles:
                        if residual is None:
                            dve.wait_ge(x_in[b], 16)
                            nc.vector.bn_stats(stats[:, j, :], x[:, j, :]).then_inc(stat_done, 1)
                            continue
                        if j % TT == 0:
                            nc.vector.tensor_tensor(y[:, j, :], y[:, j, :], gate[:, b, :], ALU.mult).then_inc(own_gated, 1)
                            dve.wait_ge(own_gated, b + 1)
                        else:
                            dve.wait_ge(gated, j - b)
                        nc.vector.tensor_tensor(x[:, j, :], x[:, j, :], y[:, j, :], ALU.add).then_inc(x_new, 1)
                        dve.wait_ge(x_new, j + 1)
                        nc.vector.bn_stats(stats[:, j, :], x[:, j, :]).then_inc(stat_done, 1)
                    for j in tiles:
                        dve.wait_ge(stat_done, b * TT + j + 1)
                        nc.vector.bn_aggr(mv[:, j, :], stats[:, j, :]).then_inc(stat_done, 1)
                    dve.wait_ge(stat_done, 2 * TT * (b + 1))
                    v, r, t = var[:, s], rstd[:, s], step[:, s]
                    link(nc.vector.tensor_scalar(v, mv[:, s, 1], EPS, None, ALU.add))
                    link(nc.vector.tensor_scalar(t.bitcast(I32), v.bitcast(I32), 1, None, ALU.logical_shift_right))
                    link(nc.vector.tensor_scalar(r.bitcast(I32), t.bitcast(I32), -1.0, float(MAGIC), ALU.mult, ALU.add))
                    for _ in range(NEWTON):
                        link(nc.vector.tensor_tensor(t, r, r, ALU.mult))
                        link(nc.vector.tensor_tensor(t, t, v, ALU.mult))
                        link(nc.vector.tensor_scalar(t, t, -0.5, 1.5, ALU.mult, ALU.add))
                        link(nc.vector.tensor_tensor(r, r, t, ALU.mult))
                    for j in tiles:
                        nc.vector.tensor_scalar(xn[:, j, :], x[:, j, :], mv[:, j, 0:1], rstd[:, j:j + 1],
                                                ALU.subtract, ALU.mult).then_inc(xn_done, 1)

                if weights:
                    nc.vector.memset(y[:], 0.0).then_inc(y_clear, 1)
                for b in range(HB):
                    normalise(b)
                for k in range(KT):
                    dve.wait_ge(scaled, KT + k + 1)
                    nc.vector.tensor_copy(hh[:, k, T:2 * T], hf[:, KT + k, :]).then_inc(dve_hi, 1)
                for k in range(2, KT):
                    dve.wait_ge(dve_hi, k + 1)
                    nc.vector.tensor_tensor(hl[:, k, T:2 * T], hf[:, KT + k, :], hh[:, k, T:2 * T].bitcast(F32),
                                            ALU.subtract).then_inc(dve_lo, 1)

            @block.tensor
            def _(pe):
                for b in range(HB):
                    for j in range(TT):
                        pe.wait_ge(xn_done, b * TT + j + 1)
                        for k in range(KT):
                            mm = pe.transpose(pT[b * KT + k][:, j * P:(j + 1) * P], xn[:, b * TT + j, k * P:(k + 1) * P],
                                              held.ident)
                    mm.then_inc(turned, 1)

            @block.scalar
            def _(act):
                if weights:
                    act.wait_ge(x_in[HB - 1], 16)
                    weights.load_qkv(act, w_in, 0)
                    weights.load_o(act, w_in, 0)
                    act.wait_ge(w_in, 48)
                    for what, i in FIRST_PARTS:
                        weights.split_hi(what, i).then_inc(split_hi, 1)
                if ahead:
                    ahead.load(act)
                    ahead.his(act)
                for b in range(HB):
                    act.wait_ge(turned, b + 1)
                    for k in range(KT):
                        i = b * KT + k
                        nc.scalar.activation(hf[:, i, :], pT[i][:], ACT.Identity,
                                             bias=held.modh[:, layer, ci, k, b:b + 1],
                                             scale=held.modh[:, layer, ci + 1, k, b:b + 1]).then_inc(scaled, 1)
                    if b == 0:
                        for k in range(KT):
                            act.wait_ge(scaled, k + 1)
                            nc.scalar.copy(hh[:, k, 0:T], hf[:, k, :]).then_inc(act_hi, 1)


def stage_half_mod(nc, held, half):
    with Stage(nc, "hm") as st:
        done = st.sem("done")
        with nc.Block() as block:
            @block.vector
            def _(dve):
                nc.vector.tensor_copy(held.modh[:].rearrange("p l c k b -> p (l c k) b"),
                                      held.modT[:].rearrange("p l c k b -> p (l c k) b")[:, :, bass.ds(half * HB, HB)]
                                      ).then_inc(done, 1)


class GroupWeights:

    def __init__(self, ctx, nc, a):
        sb = lambda n, s, dt=F32: ctx.enter_context(nc.sbuf_tensor(n, s, dt))
        QW = R0 * HD
        self.nc, self.a = nc, a
        self.raw_q, self.raw_kv, self.raw_o = sb("raw_q", [P, KT, QW]), sb("raw_kv", [P, 2, KT, HD]), sb("raw_o", [P, R0, D])
        self.qh, self.ql = sb("wqh", [P, KT, QW], F32R), sb("wql", [P, KT, QW], F32R)
        self.kvh, self.kvl = sb("wkvh", [P, 2, KT, HD], F32R), sb("wkvl", [P, 2, KT, HD], F32R)
        self.oh, self.ol = sb("woh", [P, R0, D], F32R), sb("wol", [P, R0, D], F32R)

    def load_qkv(self, eng, sem, g):
        QW = R0 * HD
        eng.dma_start(self.raw_q[:], self.a["wq"][:, bass.ds(g * QW, QW)].rearrange("(k p) n -> p k n", p=P)).then_inc(sem, 16)
        eng.dma_start(self.raw_kv[:], self.a["wkv"][:, :, bass.ds(g * HD, HD)].rearrange("w (k p) n -> p w k n", p=P)).then_inc(sem, 16)

    def load_o(self, eng, sem, g):
        QW = R0 * HD
        eng.dma_start(self.raw_o[:], self.a["wo"][bass.ds(g * QW, QW), :].rearrange("(h p) n -> p h n", p=P)).then_inc(sem, 16)

    def parts(self, what, i):
        if what == "q":
            s = slice(i * HD, (i + 1) * HD)
            return self.raw_q[:, :, s], self.qh[:, :, s], self.ql[:, :, s]
        if what == "kv":
            return self.raw_kv[:, i], self.kvh[:, i], self.kvl[:, i]
        return self.raw_o[:, i], self.oh[:, i], self.ol[:, i]

    def split_hi(self, what, i):
        raw, hi, lo = self.parts(what, i)
        return self.nc.scalar.copy(hi, raw)

    def split_lo(self, what, i):
        raw, hi, lo = self.parts(what, i)
        return self.nc.gpsimd.tensor_tensor(lo, raw, hi.bitcast(F32), ALU.subtract)


FIRST_PARTS = [("kv", 0), ("q", 0), ("kv", 1), ("q", 1), ("q", 2), ("q", 3)]

GB = 4
UNITS = GB * HB
NH = UNITS * R0
KEYS_AT = [None] + [R0 * (u - 1) + (u > 1) for u in range(1, UNITS)]
VALUES_AT = [None] + [R0 * (u - 1) + 2 for u in range(1, UNITS)]
STEP_KINDS = [[(kind, at.index(n)) for kind, at in (("K", KEYS_AT), ("V", VALUES_AT)) if n in at]
              + [("Q", n + 2)] * (n + 2 < NH) for n in range(NH)]
STEP_KINDS[0].reverse()
PROJ = [("K", 0), ("Q", 0), ("V", 0), ("Q", 1)] + [p for step in STEP_KINDS for p in step]
STEP_PROJ = [[PROJ.index(p) for p in step] for step in STEP_KINDS]
ROPE = [e for e, (kind, _) in enumerate(PROJ) if kind != "V"]
S_AT = [(0, 0), (1, 0), (0, P), (2, 0)]
S_OF = [[0, 2], [1], [3]]
P_OFF = [P * i * (i + 1) // 2 for i in range(TT)]
NARROW = 192
PAD = NARROW - P
PT_OFF = [0, 4 * P, 7 * P, 9 * P + PAD]
PT_CHUNK = ((0, 4 * P), (4 * P, 3 * P), (7 * P, 3 * P + PAD))
PT_OF = (0, 1, 2, 2)


def weight_splits():
    at = [[] for _ in range(NH)]
    for i in range(R0):
        at[i // 2].append(("o", i, 0, None))
    for gr in range(GB):
        n0 = 2 * R0 * gr
        used = lambda kind, i: PROJ.index((kind, i))
        at[n0 + 2].append(("kv", 0, gr + 1, used("K", 2 * gr + 1)))
        at[n0 + 3].append(("kv", 1, gr + 1, used("V", 2 * gr + 1)))
        for i in range(R0):
            at[n0 + 3 + i if i < 3 else n0 + 6].append(("q", i, gr + 1, used("Q", n0 + R0 + i)))
        if gr + 1 < GB:
            for i in range(R0):
                at[n0 + 8 + i].append(("o", i, gr + 1, 4 * (4 * gr + 2 + i // 2) + 3))
    return at


SPLITS = weight_splits()
SPLIT_LIST = [s for step in SPLITS for s in step]


def stage_groups(nc, held, a, wts, g):
    QS = HD ** -0.5
    with Stage(nc, "gqa") as st:
        hh, hl, y = held.hh, held.hl, held.y
        kh = [st.sb(f"kh{b}", [P, T], F32R) for b in range(2)]
        kl = [st.sb(f"kl{b}", [P, T], F32R) for b in range(2)]
        vt = st.sb("vt", [P, T])
        vh = [st.sb(f"vh{b}", [P, T], F32R) for b in range(2)]
        vl = [st.sb(f"vl{b}", [P, T], F32R) for b in range(2)]
        qh = [st.sb(f"qh{i}", [P, T], F32R) for i in range(2)]
        ql = [st.sb(f"ql{i}", [P, T], F32R) for i in range(2)]
        rot = [st.sb(f"rot{i}", [P, T]) for i in range(2)]
        full = [st.sb(f"full{i}", [P, T]) for i in range(2)]
        prob = [st.sb(f"prob{i}", [P, 10 * P]) for i in range(2)]
        pth, ptl = st.sb("pth", [P, 10 * P + PAD], F32R), st.sb("ptl", [P, 10 * P + PAD], F32R)
        oh = [st.sb(f"oh{i}", [P, T], F32R) for i in range(4)]
        ol = [st.sb(f"ol{i}", [P, T], F32R) for i in range(4)]
        nmax = [st.sb(f"nmax{i}", [P, TT]) for i in range(2)]
        den = [st.sb(f"den{i}", [P, TT]) for i in range(2)]
        rden = [st.sb(f"rden{i}", [P, TT]) for i in range(2)]
        pj = st.ps("pj", [P, T])
        pS = [st.ps(f"pS{i}", [P, T]) for i in range(3)]
        pT = [st.ps(f"pT{i}", [P, T]) for i in range(2)]
        pO, pW = st.ps("pO", [P, T]), st.ps("pW", [P, D])
        qkv_in, wo_in = st.sem("qkv_in"), st.sem("wo_in")
        proj_full = st.sem("proj_full")
        rotated, cosed = st.sem("rotated"), st.sem("cosed")
        v_out, v_turned, v_hi, v_lo = st.sem("v_out"), st.sem("v_turned"), st.sem("v_hi"), st.sem("v_lo")
        sined, roped, rope_hi, rope_lo = st.sem("sined"), st.sem("roped"), st.sem("rope_hi"), st.sem("rope_lo")
        s_full, max_done, exp_done = st.sem("s_full"), st.sem("max_done"), st.sem("exp_done")
        recip, normed = st.sem("recip"), st.sem("normed")
        pt_full, pt_hi, pt_lo = st.sem("pt_full"), st.sem("pt_hi"), st.sem("pt_lo")
        o_full, o_hi, o_lo = st.sem("o_full"), st.sem("o_hi"), st.sem("o_lo")
        w_full, w_added = st.sem("w_full"), st.sem("w_added")
        w_hi, w_lo = st.sem("w_hi"), st.sem("w_lo")
        bank = [pj] * len(PROJ)
        bank[1], bank[2], bank[4] = pO, pW, pW
        NTILES = NH // 2 * TT

        def wbank(d):
            return pO if d >= NTILES - TT and d % 2 else pW

        def split_no(what, i, group):
            return next(n for n, s in enumerate(SPLIT_LIST) if s[:3] == (what, i, group)) + 1

        def last_split(kinds, group):
            return max(n for n, s in enumerate(SPLIT_LIST) if s[0] in kinds and s[2] == group) + 1

        def step_e(n, slot):
            return [e for e in STEP_PROJ[n] if n and (PROJ[e][0] == "Q") == (slot == 0)]

        with nc.Block() as block:

            @block.sync
            def _(sp):
                after = [g + i for i in range(1, GB)] + [(g + GB) % G]
                for i in range(GB):
                    if i:
                        sp.wait_ge(w_lo, last_split(("q", "kv"), i))
                    wts.load_qkv(sp, qkv_in, after[i])
                    sp.wait_ge(w_lo, last_split(("o",), i))
                    wts.load_o(sp, wo_in, after[i])
                sp.wait_ge(wo_in, 16 * GB)

            @block.tensor
            def _(pe):
                def free(e):
                    kind, i = PROJ[e]
                    if kind == "V":
                        pe.wait_ge(v_out, i + 1)
                    else:
                        pe.wait_ge(cosed, ROPE.index(e) + 1)

                def project(e):
                    kind, i = PROJ[e]
                    before = [f for f in range(e) if bank[f] is bank[e]]
                    if before:
                        free(before[-1])
                    u = i // R0 if kind == "Q" else i
                    b, group = u % HB, u // HB
                    if group:
                        pe.wait_ge(w_lo, split_no(*(("q", i % R0) if kind == "Q" else ("kv", int(kind == "V"))), group))
                    t = slice(b * T, (b + 1) * T)
                    n = 0
                    for k in range(KT):
                        if kind == "Q":
                            c = slice((i % R0) * HD, (i % R0 + 1) * HD)
                            wh, wl = wts.qh[:, k, c], wts.ql[:, k, c]
                        else:
                            w = int(kind == "V")
                            wh, wl = wts.kvh[:, w, k, :], wts.kvl[:, w, k, :]
                        for wp, hp in ((wh, hh), (wh, hl), (wl, hh)):
                            mm = pe.matmul(bank[e][:], wp, hp[:, k, t], start=(n == 0), stop=(n == 3 * KT - 1))
                            n += 1
                    mm.then_inc(proj_full, 1)

                def turn_values(u):
                    pe.wait_ge(v_out, u + 1)
                    if u:
                        pe.wait_ge(pt_lo, 3 * (R0 * u - 2) + 2)
                    for j in range(TT):
                        mm = pe.transpose(pT[1][:, j * P:(j + 1) * P], vt[:, j * P:(j + 1) * P], held.ident)
                    mm.then_inc(v_turned, 1)

                def scores(n):
                    u, r = n // R0, n % 2
                    pe.wait_ge(rope_lo, ROPE.index(PROJ.index(("Q", n))) + 1)
                    pe.wait_ge(rope_lo, ROPE.index(PROJ.index(("K", u))) + 1)
                    for s, tiles in enumerate(S_OF):
                        if n:
                            pe.wait_ge(exp_done, 3 * (n - 1) + s + 1)
                        for i in tiles:
                            w, c = (i + 1) * P, S_AT[i][1]
                            t = slice(i * P, (i + 1) * P)
                            wide = max(w, NARROW)
                            out = pS[s][:, c:c + wide]
                            pe.matmul(out, qh[r][:, t], kh[u % 2][:, 0:wide], start=True, stop=False)
                            pe.matmul(out, qh[r][:, t], kl[u % 2][:, 0:wide], start=False, stop=False)
                            pe.matmul(out, ql[r][:, t], kh[u % 2][:, 0:wide], start=False, stop=False)
                            mm = pe.matmul(pS[s][:, c + w - P:c + w], held.identb[:], held.maskb[:], start=False, stop=True)
                        mm.then_inc(s_full, 1)

                def turn(n, jobs):
                    for k, js in jobs:
                        if 3 * n + k >= 2:
                            pe.wait_ge(pt_lo, 3 * n + k - (1 if k == 0 else 2) if k < 2 else 3 * n + 1)
                        if k == 1 and n % R0 == R0 - 1 and n + 1 < NH:
                            pe.wait_ge(v_lo, n // R0 + 2)
                        if k == 1 and n == 0:
                            pe.wait_ge(v_lo, 1)
                        if k == 2:
                            c = PT_OFF[3] - PAD - PT_CHUNK[2][0]
                            pe.matmul(pT[0][:, c:c + PAD], held.identb[:], held.zerob[:], start=True, stop=True)
                        for j in js:
                            for i in range(j, TT):
                                c = PT_OFF[j] - PT_CHUNK[k][0] + (i - j) * P
                                mm = pe.transpose(pT[k % 2][:, c:c + P],
                                                  prob[n % 2][:, P_OFF[i] + j * P:P_OFF[i] + (j + 1) * P], held.ident)
                        mm.then_inc(pt_full, 1)

                def weigh(n):
                    u = n // R0
                    if n == 0:
                        pe.wait_ge(cosed, 2)
                    else:
                        pe.wait_ge(o_lo, n)
                    pe.wait_ge(v_lo, u + 1)
                    m = 0
                    for j in range(TT):
                        pe.wait_ge(pt_lo, 3 * n + PT_OF[j] + 1)
                        w = max((TT - j) * P, NARROW)
                        v = slice(j * P, (j + 1) * P)
                        end = PT_OFF[j] + (TT - j) * P
                        pc = slice(end - w, end)
                        for vp, pp in ((vh, pth), (vh, ptl), (vl, pth)):
                            mm = pe.matmul(pO[:, T - w:], vp[u % 2][:, v], pp[:, pc], start=(m == 0), stop=(m == 11))
                            m += 1
                    mm.then_inc(o_full, 1)

                def out_proj(d):
                    pair, i = d // TT, d % TT
                    if d == 0:
                        free(4)
                    if i == 0:
                        pe.wait_ge(o_lo, 2 * pair + 2)
                        pe.wait_ge(w_lo, split_no("o", (2 * pair + 1) % R0, pair // (R0 * HB // 2)))
                    if d:
                        pe.wait_ge(w_added, d if wbank(d) is wbank(d - 1) else d - 1)
                    t = slice(i * P, (i + 1) * P)
                    m = 0
                    for h in (2 * pair, 2 * pair + 1):
                        for op, wp in ((oh, wts.oh), (oh, wts.ol), (ol, wts.oh)):
                            mm = pe.matmul(wbank(d)[:], op[h % 4][:, t], wp[:, h % R0, :], start=(m == 0), stop=(m == 5))
                            m += 1
                    mm.then_inc(w_full, 1)

                for e in range(4):
                    project(e)
                turn_values(0)
                scores(0)
                for n in range(NH):
                    if n == 0:
                        for e in STEP_PROJ[0]:
                            project(e)
                    pe.wait_ge(normed, n + 1)
                    turn(n, ((0, (0,)), (1, (1,))))
                    for e in step_e(n, 1):
                        project(e)
                    if n + 1 < NH:
                        scores(n + 1)
                    for e in step_e(n, 0):
                        project(e)
                    turn(n, ((2, (2, 3)),))
                    if n >= 2:
                        out_proj(2 * (n - 2))
                    if n % R0 == 2 and n // R0 + 1 < UNITS:
                        turn_values(n // R0 + 1)
                    weigh(n)
                    if n >= 2:
                        out_proj(2 * (n - 2) + 1)
                for d in range(NTILES - TT, NTILES):
                    out_proj(d)

            @block.scalar
            def _(act):
                def leave(e):
                    kind, i = PROJ[e]
                    act.wait_ge(proj_full, e + 1)
                    if kind == "V":
                        if i:
                            act.wait_ge(v_turned, i)
                        nc.scalar.copy(vt[:], bank[e][:]).then_inc(v_out, 1)
                        return
                    r = ROPE.index(e)
                    if r >= 2:
                        act.wait_ge(rope_lo, r - 1)
                    scale = QS if kind == "Q" else 1.0
                    nc.scalar.mul(rot[r % 2][0:64, :], bank[e][64:128, :], scale).then_inc(rotated, 1)
                    nc.scalar.mul(rot[r % 2][64:128, :], bank[e][0:64, :], scale).then_inc(rotated, 1)

                def value_his(u):
                    act.wait_ge(v_turned, u + 1)
                    if u >= 2:
                        act.wait_ge(o_full, R0 * (u - 1))
                    nc.scalar.copy(vh[u % 2][:], pT[1][:]).then_inc(v_hi, 1)

                def exps(n):
                    r = n % 2
                    for s, tiles in enumerate(S_OF):
                        act.wait_ge(max_done, 4 * n + (2, 3, 4)[s])
                        if n >= 2 and s == 0:
                            act.wait_ge(pt_full, 3 * (n - 1))
                            act.wait_ge(recip, n - 1)
                        for i in tiles:
                            w, c = (i + 1) * P, S_AT[i][1]
                            ins = nc.scalar.activation(prob[r][:, P_OFF[i]:P_OFF[i] + w], pS[s][:, c:c + w], ACT.Exp,
                                                       bias=nmax[r][:, i:i + 1], accum_out=den[r][:, i:i + 1])
                        ins.then_inc(exp_done, 1)

                def pt_his(n, ks):
                    for k in ks:
                        act.wait_ge(pt_full, 3 * n + k + 1)
                        if n:
                            act.wait_ge(o_full, n)
                        c, w = PT_CHUNK[k]
                        nc.scalar.copy(pth[:, c:c + w], pT[k % 2][:, 0:w]).then_inc(pt_hi, 1)

                def weight_his(n):
                    for what, i, group, user in SPLITS[n]:
                        if what != "o":
                            act.wait_ge(qkv_in, 32 * group)
                            act.wait_ge(proj_full, user + 1)
                        elif user is not None:
                            act.wait_ge(wo_in, 16 * group)
                            act.wait_ge(w_full, user + 1)
                        wts.split_hi(what, i).then_inc(w_hi, 1)

                for e in range(4):
                    leave(e)
                value_his(0)
                exps(0)
                for n in range(NH):
                    if n == 0:
                        for e in STEP_PROJ[0]:
                            leave(e)
                    pt_his(n, (0, 1))
                    for e in step_e(n, 1):
                        leave(e)
                    if n == 0:
                        pt_his(n, (2,))
                    if n + 1 < NH:
                        exps(n + 1)
                    for e in step_e(n, 0):
                        leave(e)
                    if n:
                        pt_his(n, (2,))
                    if n % R0 == 2 and n // R0 + 1 < UNITS:
                        value_his(n // R0 + 1)
                    act.wait_ge(o_full, n + 1)
                    if n >= 4:
                        act.wait_ge(w_full, 4 * ((n - 4) // 2) + 4)
                    nc.scalar.copy(oh[n % 4][:], pO[:]).then_inc(o_hi, 1)
                    weight_his(n)

            @block.vector
            def _(dve):
                def leave(e):
                    kind, i = PROJ[e]
                    if kind == "V":
                        return
                    r = ROPE.index(e)
                    dve.wait_ge(rotated, 2 * r + 2)
                    scale = QS if kind == "Q" else 1.0
                    nc.vector.scalar_tensor_tensor(full[r % 2][:], bank[e][:], scale, held.cosT, ALU.mult,
                                                   ALU.mult).then_inc(cosed, 1)

                def value_los(u):
                    dve.wait_ge(v_hi, u + 1)
                    nc.vector.tensor_tensor(vl[u % 2][:], pT[1][:], vh[u % 2][:].bitcast(F32), ALU.subtract).then_inc(v_lo, 1)

                def rope_parts(e):
                    kind, i = PROJ[e]
                    if kind == "V":
                        return
                    r = ROPE.index(e)
                    dve.wait_ge(roped, r + 1)
                    if kind == "Q" and i >= 2:
                        dve.wait_ge(s_full, 3 * (i - 1))
                    if kind == "K" and i >= 2:
                        dve.wait_ge(s_full, 3 * R0 * (i - 1))
                    dst = kh[i % 2] if kind == "K" else qh[i % 2]
                    nc.vector.tensor_copy(dst[:], full[r % 2][:]).then_inc(rope_hi, 1)

                def maxes(n):
                    r = n % 2
                    if n >= 2:
                        dve.wait_ge(exp_done, 3 * (n - 1))
                    for s, tiles in enumerate(S_OF):
                        dve.wait_ge(s_full, 3 * n + s + 1)
                        for i in tiles:
                            w, c = (i + 1) * P, S_AT[i][1]
                            nc.vector.tensor_reduce(nmax[r][:, i:i + 1], pS[s][:, c:c + w], AX.X, ALU.max,
                                                    negate=True).then_inc(max_done, 1)

                def pt_los(n, ks):
                    for k in ks:
                        dve.wait_ge(pt_hi, 3 * n + k + 1)
                        c, w = PT_CHUNK[k]
                        nc.vector.tensor_tensor(ptl[:, c:c + w], pT[k % 2][:, 0:w], pth[:, c:c + w].bitcast(F32),
                                                ALU.subtract).then_inc(pt_lo, 1)

                def norms(n):
                    dve.wait_ge(exp_done, 3 * n + 3)
                    nc.vector.reciprocal(rden[n % 2][:], den[n % 2][:]).then_inc(recip, 1)
                    dve.wait_ge(recip, n + 1)
                    for i in range(TT):
                        p = prob[n % 2][:, P_OFF[i]:P_OFF[i] + (i + 1) * P]
                        ins = nc.vector.tensor_scalar(p, p, rden[n % 2][:, i:i + 1], None, ALU.mult)
                    ins.then_inc(normed, 1)

                def add(d):
                    dve.wait_ge(w_full, d + 1)
                    if d >= TT:
                        dve.wait_ge(w_added, d - TT + 1)
                    j = (d // (2 * TT)) % HB * TT + d % TT
                    nc.vector.tensor_tensor(y[:, j, :], wbank(d)[:], y[:, j, :], ALU.add).then_inc(w_added, 1)

                leave(0)
                leave(1)
                rope_parts(0)
                rope_parts(1)
                leave(3)
                value_los(0)
                rope_parts(3)
                maxes(0)
                norms(0)
                for n in range(NH):
                    if n == 0:
                        for e in STEP_PROJ[0]:
                            leave(e)
                    pt_los(n, (0, 1))
                    for e in step_e(n, 1):
                        leave(e)
                    if n + 1 < NH:
                        maxes(n + 1)
                    for e in step_e(n, 1):
                        rope_parts(e)
                    if n == 0:
                        pt_los(n, (2,))
                        rope_parts(STEP_PROJ[0][0])
                    if n + 1 < NH:
                        norms(n + 1)
                    for e in step_e(n, 0):
                        leave(e)
                    if n:
                        pt_los(n, (2,))
                    if n >= 2:
                        add(2 * (n - 2))
                    if n % R0 == 2 and n // R0 + 1 < UNITS:
                        value_los(n // R0 + 1)
                    for e in step_e(n, 0) if n else STEP_PROJ[0][1:]:
                        rope_parts(e)
                    dve.wait_ge(o_hi, n + 1)
                    nc.vector.tensor_tensor(ol[n % 4][:], pO[:], oh[n % 4][:].bitcast(F32), ALU.subtract).then_inc(o_lo, 1)
                    if n >= 2:
                        add(2 * (n - 2) + 1)
                for d in range(NTILES - TT, NTILES):
                    add(d)

            @block.gpsimd
            def _(pool):
                def rope(e):
                    kind, i = PROJ[e]
                    if kind == "V":
                        return
                    r = ROPE.index(e)
                    pool.wait_ge(rotated, 2 * r + 2)
                    nc.gpsimd.tensor_tensor(rot[r % 2][:], rot[r % 2][:], held.sinT, ALU.mult).then_inc(sined, 1)
                    pool.wait_ge(sined, r + 1)
                    pool.wait_ge(cosed, r + 1)
                    nc.gpsimd.tensor_tensor(full[r % 2][:], full[r % 2][:], rot[r % 2][:], ALU.add).then_inc(roped, 1)

                def rope_lo_part(e):
                    kind, i = PROJ[e]
                    if kind == "V":
                        return
                    r = ROPE.index(e)
                    pool.wait_ge(rope_hi, r + 1)
                    hi, lo = (kh[i % 2], kl[i % 2]) if kind == "K" else (qh[i % 2], ql[i % 2])
                    nc.gpsimd.tensor_tensor(lo[:], full[r % 2][:], hi[:].bitcast(F32), ALU.subtract).then_inc(rope_lo, 1)

                rope(0)
                rope(1)
                rope_lo_part(0)
                rope_lo_part(1)
                rope(3)
                rope_lo_part(3)
                done = 0
                for n in range(NH):
                    for e in STEP_PROJ[n]:
                        rope(e)
                        rope_lo_part(e)
                    for what, i, group, user in SPLITS[n]:
                        done += 1
                        pool.wait_ge(w_hi, done)
                        wts.split_lo(what, i).then_inc(w_lo, 1)


def stage_sign_ffn(nc, held, a, signs, half):
    with Stage(nc, "ffn0") as st:
        sgn, rs = signs.sgn, signs.rs
        z = held.y
        clip = st.sb("clip", [P, NT, D])
        same = st.sb("same", [P, NT, D])
        wild = st.sb("wild", [P, NT, D], I32)
        ps = [st.ps(f"ps{i}", [P, D]) for i in range(NT)]
        full, scaled, clipped, equal, zeroed, marked, put = (st.sem(n) for n in (
            "full", "scaled", "clipped", "equal", "zeroed", "marked", "put"))
        gate_in = st.sem("gate_in")
        with nc.Block() as block:

            @block.sync
            def _(sp):
                load_gates(sp, held, a, 1, half, gate_in)

            @block.tensor
            def _(pe):
                for j in range(NT):
                    for k in range(KT):
                        for n, hp in enumerate((held.hh, held.hl)):
                            mm = pe.matmul(ps[j][:], hp[:, k, j * P:(j + 1) * P], sgn[:, k, :],
                                           start=(k == 0 and n == 0), stop=(k == KT - 1 and n == 1))
                    mm.then_inc(full, 1)

            @block.vector
            def _(dve):
                def replace(j):
                    dve.wait_ge(marked, j + 1)
                    dve.wait_ge(zeroed, j + 1)
                    nc.vector.copy_predicated(z[:, j], wild[:, j], clip[:, j]).then_inc(put, 1)

                for j in range(NT):
                    dve.wait_ge(full, j + 1)
                    nc.vector.tensor_tensor(z[:, j], ps[j][:], rs[:], ALU.mult).then_inc(scaled, 1)
                    dve.wait_ge(scaled, j + 1)
                    nc.vector.tensor_tensor(same[:, j], z[:, j], z[:, j], ALU.is_equal).then_inc(equal, 1)
                    nc.vector.tensor_scalar(clip[:, j], z[:, j], LIMIT, -LIMIT, ALU.min, ALU.max).then_inc(clipped, 1)
                    nc.vector.tensor_scalar(wild[:, j], z[:, j], 0.0, 0.0, ALU.mult, ALU.not_equal).then_inc(marked, 1)
                    if j >= 2:
                        replace(j - 2)
                replace(NT - 2)
                replace(NT - 1)

            @block.gpsimd
            def _(pool):
                for j in range(NT):
                    pool.wait_ge(clipped, j + 1)
                    pool.wait_ge(equal, j + 1)
                    nc.gpsimd.tensor_tensor(clip[:, j], clip[:, j], same[:, j], ALU.mult).then_inc(zeroed, 1)


TQ = T // 4


def stage_qkv(nc, held, a, ws):
    with Stage(nc, "qkv") as st:
        hh, hl = held.hh, held.hl
        wh, wl, bias = ws.wh, ws.wl, ws.bias
        NB = 4
        rest = [st.sb(f"rest{i}", [P, T]) for i in range(NB)]
        part = [st.sb(f"part{i}", [P, 4, 3, TQ], BF16) for i in range(NB)]
        ps = [st.ps(f"ps{i}", [P, T]) for i in range(6)]
        w_lo, b_scaled, full, left, first, again, second, third, halved = (st.sem(n) for n in (
            "w_lo", "b_scaled", "full", "left", "first", "again", "second", "third", "halved"))
        stored = [st.sem(f"stored{i}") for i in range(NB)]
        items = [(w, b, m) for w in QKV_ORDER for b in range(HB) for m in range(KT)]
        place = [(1, 2, 0), (0, 1, 2), (0, 1, 2)]
        key_pairs = ((0, 1), (1, 0), (0, 2))
        stores = [1, 6, 1]
        total, stored_by = [0] * NB, []
        for n, (w, b, m) in enumerate(items):
            total[n % NB] += 16 * stores[w]
            stored_by.append(total[n % NB])
        quarters = lambda buf: buf[:].rearrange("p (q t) -> p q t", q=4)
        with nc.Block() as block:

            @block.sync
            def _(sp):
                for n, (w, b, m) in enumerate(items):
                    sp.wait_ge(third, n + 1)
                    rows = slice(m * P, (m + 1) * P)
                    src = part[n % NB]
                    if w == 1:
                        for i, pair in enumerate(key_pairs):
                            for u in range(2):
                                sp.dma_start(a["ks"][b, i, :, u, rows, :].rearrange("q p t -> p q t"), src[:, :, pair[u]]
                                             ).then_inc(stored[n % NB], 16)
                    else:
                        sp.dma_start(a["qs" if w == 0 else "vs"][b, :, :, rows, :].rearrange("q s p t -> p (q s) t"),
                                     src[:].rearrange("p q s t -> p (q s) t")).then_inc(stored[n % NB], 16)
                for i in range(NB):
                    sp.wait_ge(stored[i], total[i])

            @block.tensor
            def _(pe):
                for n, (w, b, m) in enumerate(items):
                    if n >= 6:
                        pe.wait_ge(first, n - 5)
                    for k in range(KT):
                        if b == 0 and m == 0 and n:
                            pe.wait_ge(w_lo, (QKV_ORDER.index(w) - 1) * KT + k + 1)
                        t, c = slice(b * T, (b + 1) * T), slice(m * P, (m + 1) * P)
                        for i, (wp, hp) in enumerate(((wh, hh), (wh, hl), (wl, hh))):
                            mm = pe.matmul(ps[n % 6][:], wp[:, w, k, c], hp[:, k, t],
                                           start=(k == 0 and i == 0), stop=(k == KT - 1 and i == 2))
                    mm.then_inc(full, 1)

            @block.scalar
            def _(act):
                act.wait_ge(b_scaled, 1)
                for n, (w, b, m) in enumerate(items):
                    act.wait_ge(full, n + 1)
                    if n >= NB:
                        act.wait_ge(third, n - NB + 1)
                        act.wait_ge(stored[n % NB], stored_by[n - NB])
                    how = dict(bias=bias[:, w, m:m + 1], scale=D1 ** -0.5 if w == 0 else 1.0)
                    nc.scalar.activation(rest[n % NB][:], ps[n % 6][:], ACT.Identity, **how).then_inc(left, 1)
                    nc.scalar.activation(part[n % NB][:, :, place[w][0]], quarters(ps[n % 6]), ACT.Identity, **how).then_inc(first, 1)

            @block.vector
            def _(dve):
                nc.vector.tensor_scalar(bias[:, 0], bias[:, 0], D1 ** -0.5, None, ALU.mult).then_inc(b_scaled, 1)
                for n, (w, b, m) in enumerate(items):
                    r, pt = quarters(rest[n % NB]), part[n % NB]
                    dve.wait_ge(first, n + 1)
                    nc.vector.tensor_tensor(r, r, pt[:, :, place[w][0]], ALU.subtract).then_inc(again, 1)
                    dve.wait_ge(again, n + 1)
                    nc.vector.tensor_copy(pt[:, :, place[w][1]], r).then_inc(second, 1)

            @block.gpsimd
            def _(pool):
                def weight_los(w):
                    for k in range(KT):
                        ws.lo_part(w, k).then_inc(w_lo, 1)

                halves = 0
                for n, (w, b, m) in enumerate(items):
                    if n in (1, 9):
                        weight_los(QKV_ORDER[1 + n // 9])
                    r, pt = quarters(rest[n % NB]), part[n % NB]
                    pool.wait_ge(second, n + 1)
                    if w < 2:
                        nc.gpsimd.tensor_tensor(pt[:, :, place[w][2]], r, pt[:, :, place[w][1]], ALU.subtract).then_inc(third, 1)
                    else:
                        halves += 1
                        nc.gpsimd.tensor_tensor(r, r, pt[:, :, place[w][1]], ALU.subtract).then_inc(halved, 1)
                        pool.wait_ge(halved, halves)
                        nc.gpsimd.tensor_scalar(pt[:, :, place[w][2]], r, 0.5, 1.0, ALU.mult, ALU.mult).then_inc(third, 1)


NC_ = 8
TC = TQ // NC_


def load_keys(eng, a, kk, b, sem):
    for i in range(3):
        eng.dma_start(kk[:, i], a["ks"][bass.ds(b, 1), i].rearrange("o q u (d h) t -> (o q u d) h t", h=H1)).then_inc(sem, 16)


def stage_zero_diagonal(nc, a, bd, kk):
    with Stage(nc, "zero") as st:
        zeroed, k_in = st.sem("zeroed"), st.sem("k_in")
        with nc.Block() as block:
            @block.sync
            def _(sp):
                load_keys(sp, a, kk, 0, k_in)
                sp.wait_ge(k_in, 48)

            @block.vector
            def _(dve):
                nc.vector.memset(bd[:, 0].bitcast(F32), 0.0).then_inc(zeroed, 1)

            @block.gpsimd
            def _(pool):
                nc.gpsimd.memset(bd[:, 1].bitcast(F32), 0.0).then_inc(zeroed, 1)


def stage_head_attention(nc, a, bd, kk, b, bnext):
    with Stage(nc, "heads") as st:
        prob = st.sb("prob", [P, TQ, H1])
        pt = st.sb("pt", [P, TQ, H1])
        pp = st.sb("pp", [P, 3, TQ, H1], BF16)
        o = st.sb("o", [P, H1, TQ])
        top = st.sb("top", [P, TQ, 1])
        den = st.sb("den", [P, TQ, 1])
        rden = st.sb("rden", [P, TQ, 1])
        NS = 6
        pS = [st.ps(f"pS{i}", [P, TC, H1]) for i in range(NS)]
        pO = [st.ps(f"pO{i}", [P, TC, H1]) for i in range(2)]
        q_in, k_in, v_in = st.sem("q_in"), st.sem("k_in"), st.sem("v_in")
        s_full, top_done, shifted, exp_done, masked, summed, recip, normed, turned = (st.sem(n) for n in (
            "s_full", "top_done", "shifted", "exp_done", "masked", "summed", "recip", "normed", "turned"))
        first, rest, second, third = (st.sem(n) for n in ("first", "rest", "second", "third"))
        last_rest = st.sem("last_rest")
        ON_POOL = NC_ - 2
        o_full, o_left, o_out = st.sem("o_full"), st.sem("o_left"), st.sem("o_out")
        ch = [slice(c * TC, (c + 1) * TC) for c in range(NC_)]

        def load_queries(eng, q, i):
            s = (1, 0)[i]
            eng.dma_start(bd[32 * q:32 * q + 32, i, 32 * q:32 * q + 32, :],
                          a["qs"][bass.ds(b, 1), q, s:s + 2].rearrange("o u (d h) t -> (o u d) h t", h=H1)).then_inc(q_in, 16)

        def load_values(eng, q, i):
            if i:
                src = a["vs"][bass.ds(b, 1), q, 2].rearrange("o (g d) t -> g o (d t)", d=D1).to_broadcast([H1, 2, D1 * TQ])
            else:
                src = a["vs"][bass.ds(b, 1), q, 0:2].rearrange("o u (g d) t -> (o g) u (d t)", d=D1)
            eng.dma_start(bd[32 * q:32 * q + 32, i, 32 * q:32 * q + 32, :].rearrange("g (u d) t -> g u (d t)", u=2), src
                          ).then_inc(v_in, 16)

        with nc.Block() as block:

            @block.sync
            def _(sp):
                for q in (0, 1):
                    for i in range(2):
                        load_queries(sp, q, i)
                sp.wait_ge(s_full, NC_)
                for q in (0, 2):
                    for i in range(2):
                        load_values(sp, q, i)
                load_keys(sp, a, kk, bnext, k_in)
                sp.wait_ge(o_left, NC_)
                sp.dma_start(a["attn"][bass.ds(b, 1)].rearrange("o q u (d h) t -> (o q u d) h t", h=H1), o[:]).then_inc(o_out, 16)
                sp.wait_ge(k_in, 48)
                sp.wait_ge(o_out, 16)

            @block.tensor
            def _(pe):
                pe.wait_ge(q_in, 128)
                for c in range(NC_):
                    if c >= NS:
                        pe.wait_ge(masked, c - NS + 1)
                    for j in range(TC):
                        t = c * TC + j
                        for i, m in ((0, 0), (0, 1), (1, 2)):
                            mm = pe.matmul(pS[c % NS][:, j, :], bd[:, i, :, t], kk[:, m, :, t], start=(m == 0), stop=(m == 2))
                    mm.then_inc(s_full, 1)
                pe.wait_ge(v_in, 128)
                for c in range(NC_):
                    pe.wait_ge(third, c + 1)
                    if c >= 2:
                        pe.wait_ge(o_left, c - 1)
                    for j in range(TC):
                        t = c * TC + j
                        for n, (i, m) in enumerate(((0, 0), (0, 1), (0, 2), (1, 0))):
                            mm = pe.matmul(pO[c % 2][:, j, :], bd[:, i, :, t], pp[:, m, t, :], start=(n == 0), stop=(n == 3))
                    mm.then_inc(o_full, 1)

            @block.scalar
            def _(act):
                for q in (2, 3):
                    for i in range(2):
                        load_queries(act, q, i)

                def parts(c):
                    act.wait_ge(turned, c + 1)
                    nc.scalar.copy(pp[:, 0, ch[c], :], pt[:, ch[c], :]).then_inc(first, 1)

                LAG = 6

                def output(c):
                    act.wait_ge(o_full, c + 1)
                    nc.scalar.copy(o[:, :, ch[c]], pO[c % 2][:].rearrange("p t h -> p h t")).then_inc(o_left, 1)

                def more_parts(c):
                    if c < ON_POOL:
                        act.wait_ge(rest, c + 1)
                    else:
                        act.wait_ge(last_rest, c - ON_POOL + 1)
                    nc.scalar.copy(pp[:, 1, ch[c], :], pt[:, ch[c], :]).then_inc(second, 1)

                for c in range(NC_ + 3):
                    if c < NC_:
                        act.wait_ge(shifted, c + 1)
                        nc.scalar.activation(prob[:, ch[c], :], prob[:, ch[c], :], ACT.Exp).then_inc(exp_done, 1)
                    if 2 <= c < NC_ + 2:
                        parts(c - 2)
                    if c == 3:
                        act.wait_ge(s_full, NC_)
                        for q in (1, 3):
                            for i in range(2):
                                load_values(act, q, i)
                    if c >= 3:
                        more_parts(c - 3)
                    if c >= LAG:
                        output(c - LAG)
                for c in range(NC_ + 3 - LAG, NC_):
                    output(c)

            @block.vector
            def _(dve):
                wide = [P, TC, H1]

                def scores_down(c):
                    dve.wait_ge(s_full, c + 1)
                    nc.vector.tensor_reduce(top[:, ch[c], :], pS[c % NS][:], AX.X, ALU.max).then_inc(top_done, 1)
                    dve.wait_ge(top_done, c + 1)
                    nc.vector.tensor_tensor(prob[:, ch[c], :], pS[c % NS][:], top[:, ch[c], :].to_broadcast(wide),
                                            ALU.subtract).then_inc(shifted, 1)

                def threshold(c):
                    dve.wait_ge(exp_done, c + 1)
                    nc.vector.scalar_tensor_tensor(prob[:, ch[c], :], pS[c % NS][:], THRESH, prob[:, ch[c], :],
                                                   ALU.is_gt, ALU.mult).then_inc(masked, 1)
                    dve.wait_ge(masked, c + 1)
                    nc.vector.tensor_reduce(den[:, ch[c], :], prob[:, ch[c], :], AX.X, ALU.add).then_inc(summed, 1)
                    dve.wait_ge(summed, c + 1)
                    nc.vector.reciprocal(rden[:, ch[c], :], den[:, ch[c], :]).then_inc(recip, 1)

                def turn(c):
                    dve.wait_ge(normed, c + 1)
                    nc.vector.transpose(pt[:, ch[c], :].rearrange("p t h -> p (t h)"),
                                        prob[:, ch[c], :].rearrange("p t h -> p (t h)")).then_inc(turned, 1)

                def remainder(c):
                    dve.wait_ge(first, c + 1)
                    nc.vector.tensor_tensor(pt[:, ch[c], :], pt[:, ch[c], :], pp[:, 0, ch[c], :], ALU.subtract).then_inc(last_rest, 1)

                for c in range(NC_ + 2):
                    if c < NC_:
                        scores_down(c)
                    if 1 <= c < NC_ + 1:
                        threshold(c - 1)
                    if c >= 2:
                        turn(c - 2)
                for c in range(ON_POOL, NC_):
                    remainder(c)

            @block.gpsimd
            def _(pool):
                for c in range(NC_ + 3):
                    if c < NC_:
                        pool.wait_ge(recip, c + 1)
                        nc.gpsimd.tensor_tensor(prob[:, ch[c], :], prob[:, ch[c], :], rden[:, ch[c], :].to_broadcast([P, TC, H1]),
                                                ALU.mult).then_inc(normed, 1)
                    if 2 <= c < ON_POOL + 2:
                        d = ch[c - 2]
                        pool.wait_ge(first, c - 1)
                        nc.gpsimd.tensor_tensor(pt[:, d, :], pt[:, d, :], pp[:, 0, d, :], ALU.subtract).then_inc(rest, 1)
                    if c >= 3:
                        d = ch[c - 3]
                        pool.wait_ge(second, c - 2)
                        nc.gpsimd.tensor_tensor(pp[:, 2, d, :], pt[:, d, :], pp[:, 1, d, :], ALU.subtract).then_inc(third, 1)


def stage_attention_out(nc, held, a, half):
    with Stage(nc, "wo1") as st:
        y, hh, hl = held.y, held.hh, held.hl
        raw = st.sb("raw", [P, KT, D])
        at = st.sb("at", [P, 2, KT, HB * T])
        wh, wl = st.sb("wh", [P, KT, D], F32R), st.sb("wl", [P, KT, D], F32R)
        bo = st.sb("bo", [P, D])
        ps = [st.ps(f"ps{i}", [P, D]) for i in range(8)]
        w_in, b_in, w_hi, w_lo, summed, hi, lo, full, biased = (st.sem(n) for n in (
            "w_in", "b_in", "w_hi", "w_lo", "summed", "hi", "lo", "full", "biased"))
        odd_summed, gate_in = st.sem("odd_summed"), st.sem("gate_in")
        a_in = [[st.sem(f"a_in{b}{i}") for i in range(KT // 2)] for b in range(HB)]
        with nc.Block() as block:

            @block.sync
            def _(sp):
                for b in range(HB):
                    for k in range(KT):
                        for u in range(2):
                            sp.dma_start(at[:, u, k, b * T:(b + 1) * T].rearrange("p (q t) -> p q t", q=4),
                                         a["attn"][b, :, u, k * P:(k + 1) * P, :].rearrange("q p t -> p q t")).then_inc(a_in[b][k // 2], 16)
                sp.dma_start(bo[:], a["b1o"].rearrange("(o d) -> o d", o=1).to_broadcast([P, D])).then_inc(b_in, 16)
                load_gates(sp, held, a, 2, half, gate_in)

            @block.gpsimd
            def _(pool):
                for k in range(KT):
                    pool.wait_ge(w_hi, k + 1)
                    nc.gpsimd.tensor_tensor(wl[:, k], raw[:, k], wh[:, k].bitcast(F32), ALU.subtract).then_inc(w_lo, 1)
                for i in range(1, HB * KT, 2):
                    b, k = i // KT, i % KT
                    pool.wait_ge(a_in[b][k // 2], 64)
                    nc.gpsimd.tensor_tensor(at[:, 0, k, b * T:(b + 1) * T], at[:, 0, k, b * T:(b + 1) * T],
                                            at[:, 1, k, b * T:(b + 1) * T], ALU.add).then_inc(odd_summed, 1)

            @block.tensor
            def _(pe):
                pe.wait_ge(w_lo, KT)
                for j in range(NT):
                    pe.wait_ge(lo, (j // TT + 1) * KT)
                    for k in range(KT):
                        for i, (hp, wp) in enumerate(((hh, wh), (hh, wl), (hl, wh))):
                            mm = pe.matmul(ps[j][:], hp[:, k, j * P:(j + 1) * P], wp[:, k, :],
                                           start=(k == 0 and i == 0), stop=(k == KT - 1 and i == 2))
                    mm.then_inc(full, 1)

            @block.scalar
            def _(act):
                act.dma_start(raw[:], a["w1o"].rearrange("(k p) n -> p k n", p=P)).then_inc(w_in, 16)
                act.wait_ge(w_in, 16)
                for k in range(KT):
                    nc.scalar.copy(wh[:, k], raw[:, k]).then_inc(w_hi, 1)
                for i in range(HB * KT):
                    b, k = i // KT, i % KT
                    act.wait_ge(odd_summed if i % 2 else summed, i // 2 + 1)
                    nc.scalar.copy(hh[:, k, b * T:(b + 1) * T], at[:, 0, k, b * T:(b + 1) * T]).then_inc(hi, 1)

            @block.vector
            def _(dve):
                for i in range(HB * KT + 1):
                    if i < HB * KT and i % 2 == 0:
                        b, k = i // KT, i % KT
                        dve.wait_ge(a_in[b][k // 2], 64)
                        nc.vector.tensor_tensor(at[:, 0, k, b * T:(b + 1) * T], at[:, 0, k, b * T:(b + 1) * T],
                                                at[:, 1, k, b * T:(b + 1) * T], ALU.add).then_inc(summed, 1)
                    if i:
                        b, k = (i - 1) // KT, (i - 1) % KT
                        dve.wait_ge(hi, i)
                        nc.vector.tensor_tensor(hl[:, k, b * T:(b + 1) * T], at[:, 0, k, b * T:(b + 1) * T],
                                                hh[:, k, b * T:(b + 1) * T].bitcast(F32), ALU.subtract).then_inc(lo, 1)
                dve.wait_ge(b_in, 16)
                for j in range(NT):
                    dve.wait_ge(full, j + 1)
                    nc.vector.tensor_tensor(y[:, j, :], ps[j][:], bo[:], ALU.add).then_inc(biased, 1)


def stage_lora(nc, held, a, ws, half):
    with Stage(nc, "ffn1") as st:
        x, hh, hl = held.x, held.hh, held.hl
        NA, ah, al, bh, bl = ws.NA, ws.ah, ws.al, ws.bh, ws.bl
        gate = st.sb("gate", [P, HB, D])
        hs = st.sb("hs", [P, NT, NA])
        top = st.sb("top", [P, NT, 1])
        rank = st.sb("rank", [P, NT, NE])
        best = st.sb("best", [P, NT, 1])
        route = st.sb("route", [P, NT, NE])
        wt = st.sb("wt", [P, NT, NE * R1])
        wth, wtl = st.sb("wth", [P, NT * P], F32R), st.sb("wtl", [P, NT * P], F32R)
        yg = [st.sb(f"yg{i}", [P, D]) for i in range(2)]
        ps = [st.ps(f"ps{i}", [P, D]) for i in range(4)]
        pT = [st.ps(f"pT{i}", [P, T]) for i in range(2)]
        gate_in = st.sem("gate_in")
        h_full, h_left, pick, routed = (st.sem(n) for n in ("h_full", "h_left", "pick", "routed"))
        turned, hi, lo, full, gated, added, stored = (st.sem(n) for n in ("turned", "hi", "lo", "full", "gated", "added", "stored"))
        with nc.Block() as block:

            @block.sync
            def _(sp):
                for b in range(HB):
                    sp.dma_start(gate[:, b, :], a["gates"][3, bass.ds(half * HB + b, 1), :].to_broadcast([P, D])).then_inc(gate_in, 16)
                for j in range(NT):
                    sp.wait_ge(added, j + 1)
                    sp.dma_start(a["out"][bass.ds(half * HB * T + j * P, P), :], x[:, j, :]).then_inc(stored, 16)
                sp.wait_ge(stored, 16 * NT)

            @block.gpsimd
            def _(pool):
                for j in range(NT):
                    pool.wait_ge(gated, j + 1)
                    nc.gpsimd.tensor_tensor(x[:, j, :], x[:, j, :], yg[j % 2][:], ALU.add).then_inc(added, 1)

            @block.tensor
            def _(pe):
                for j in range(NT):
                    if j >= 4:
                        pe.wait_ge(h_left, j - 3)
                    for k in range(KT):
                        for i, (hp, wp) in enumerate(((hh, ah), (hh, al), (hl, ah))):
                            mm = pe.matmul(ps[j % 4][:, 0:NARROW], hp[:, k, j * P:(j + 1) * P], wp[:, k, :],
                                           start=(k == 0 and i == 0), stop=(k == KT - 1 and i == 2))
                    mm.then_inc(h_full, 1)
                pe.wait_ge(routed, 1)
                for b in range(HB):
                    for j in range(TT):
                        mm = pe.transpose(pT[b][:, j * P:(j + 1) * P], wt[:, b * TT + j, :], held.ident)
                    mm.then_inc(turned, 1)
                for j in range(NT):
                    pe.wait_ge(lo, j // TT + 1)
                    if j < 4:
                        pe.wait_ge(h_left, NT)
                    else:
                        pe.wait_ge(gated, j - 3)
                    for i, (wp, bp) in enumerate(((wth, bh), (wth, bl), (wtl, bh))):
                        mm = pe.matmul(ps[j % 4][:], wp[:, j * P:(j + 1) * P], bp[:], start=(i == 0), stop=(i == 2))
                    mm.then_inc(full, 1)

            @block.scalar
            def _(act):
                for j in range(NT):
                    act.wait_ge(h_full, j + 1)
                    nc.scalar.copy(hs[:, j, :], ps[j % 4][:, 0:NA]).then_inc(h_left, 1)
                for b in range(HB):
                    act.wait_ge(turned, b + 1)
                    nc.scalar.copy(wth[:, b * T:(b + 1) * T], pT[b][:]).then_inc(hi, 1)

            @block.vector
            def _(dve):
                n = [0]

                def link(ins):
                    n[0] += 1
                    ins.then_inc(pick, 1)
                    dve.wait_ge(pick, n[0])

                dve.wait_ge(h_left, NT)
                logits = hs[:, :, NE * R1:]
                wide = [P, NT, NE]
                link(nc.vector.tensor_reduce(top[:], logits, AX.X, ALU.max))
                link(nc.vector.tensor_tensor(rank[:], logits, top[:].to_broadcast(wide), ALU.is_ge))
                for j in range(NT):
                    ins = nc.vector.tensor_tensor(route[:, j, :], rank[:, j, :], held.ranks, ALU.mult)
                link(ins)
                link(nc.vector.tensor_reduce(best[:], route[:], AX.X, ALU.max))
                link(nc.vector.tensor_tensor(rank[:], route[:], best[:].to_broadcast(wide), ALU.is_equal))
                link(nc.vector.tensor_tensor(route[:], rank[:], top[:].to_broadcast(wide), ALU.mult))
                for j in range(NT):
                    ins = nc.vector.tensor_tensor(wt[:, j, :].rearrange("p (e r) -> p e r", e=NE),
                                                  hs[:, j, 0:NE * R1].rearrange("p (e r) -> p e r", e=NE),
                                                  route[:, j, :].rearrange("p (e o) -> p e o", o=1).to_broadcast([P, NE, R1]), ALU.mult)
                ins.then_inc(routed, 1)
                for b in range(HB):
                    dve.wait_ge(hi, b + 1)
                    nc.vector.tensor_tensor(wtl[:, b * T:(b + 1) * T], pT[b][:], wth[:, b * T:(b + 1) * T].bitcast(F32),
                                            ALU.subtract).then_inc(lo, 1)
                dve.wait_ge(gate_in, 16 * HB)
                for j in range(NT):
                    dve.wait_ge(full, j + 1)
                    if j >= 2:
                        dve.wait_ge(added, j - 1)
                    nc.vector.tensor_tensor(yg[j % 2][:], ps[j % 4][:], gate[:, j // TT, :], ALU.mult).then_inc(gated, 1)


def build(nc, a):
    with ExitStack() as ctx:
        sb = lambda n, s, dt=F32: ctx.enter_context(nc.sbuf_tensor(n, s, dt))
        held = Held()
        W = 2 * T + 2 * P + NE
        held.consts = sb("consts", [P, W])
        held.cosT, held.sinT = held.consts[:, 0:T], held.consts[:, T:2 * T]
        held.ident = held.consts[:, 2 * T:2 * T + P]
        held.mask = held.consts[:, 2 * T + P:2 * T + 2 * P]
        held.ranks = held.consts[:, 2 * T + 2 * P:]
        held.identb, held.maskb = sb("identb", [P, P], BF16), sb("maskb", [P, P], BF16)
        held.zerob = sb("zerob", [P, PAD], BF16)
        held.modT = sb("modT", [P, 2, 4, KT, B])
        held.modh = sb("modh", [P, 2, 4, KT, HB])
        stage_modulation(nc, held, a)
        held.x = sb("x", [P, NT, D])

        def working(wctx, name):
            wsb = lambda n, s, dt=F32: wctx.enter_context(nc.sbuf_tensor(f"{name}_{n}", s, dt))
            held.y = wsb("y", [P, NT, D])
            held.gate = wsb("gate", [P, HB, D])
            held.hh, held.hl = wsb("hh", [P, KT, HB * T], F32R), wsb("hl", [P, KT, HB * T], F32R)

        with nc.Fori(0, B // HB) as half:
            stage_half_mod(nc, held, half)
            with ExitStack() as wctx:
                working(wctx, "first")
                with ExitStack() as gctx:
                    wts = GroupWeights(gctx, nc, a)
                    stage_norm(nc, held, a, 0, 0, half, weights=wts)
                    with nc.Fori(0, G // GB) as g:
                        stage_groups(nc, held, a, wts, g * GB)
                with ExitStack() as sctx:
                    signs = SignWeights(sctx, nc, a)
                    stage_norm(nc, held, a, 0, 1, half, residual=0, ahead=signs)
                    stage_sign_ffn(nc, held, a, signs, half)
                with ExitStack() as qctx:
                    qkv = QkvWeights(qctx, nc, a)
                    stage_norm(nc, held, a, 1, 0, half, residual=1, ahead=qkv)
                    stage_qkv(nc, held, a, qkv)
            with nc.sbuf_tensor("bd", [P, 2, P, TQ], BF16) as bd, nc.sbuf_tensor("kk", [P, 3, H1, TQ], BF16) as kk:
                stage_zero_diagonal(nc, a, bd, kk)
                with nc.Fori(0, HB) as b:
                    stage_head_attention(nc, a, bd, kk, b, (b + 1) % HB)
            with ExitStack() as wctx:
                working(wctx, "second")
                stage_attention_out(nc, held, a, half)
                lora = LoraWeights(wctx, nc, a)
                stage_norm(nc, held, a, 1, 1, half, residual=2, ahead=lora)
                stage_lora(nc, held, a, lora, half)


def kernel(**inputs):
    import numpy as _np
    import concourse.bacc as _bacc
    from concourse import mybir as _mybir
    from concourse.bass_utils import run_bass_kernel_spmd as _run

    i = {k: _np.asarray(v) for k, v in inputs.items()}
    wq = i["L0_attn_wq"]
    dim_head = _np.arange(D).reshape(H1, D1).T.reshape(-1)
    arrays = {
        "x": i["L0_attn_x"].reshape(B * T, D), "wq": wq, "wkv": _np.stack([i["L0_attn_wk"], i["L0_attn_wv"]]),
        "wo": i["L0_attn_wo"], "w_sign": i["L0_ffn_weight"], "w_signT": i["L0_ffn_weight"].T,
        "scale_param": i["L0_ffn_scale_param"].reshape(KT, P).T, "c0T": i["L0_c"].T, "c1T": i["L1_c"].T,
        "wmod0": i["L0_wmod"], "wmod1": i["L1_wmod"],
        "w1q": i["L1_attn_Wq"][dim_head].T, "w1k": i["L1_attn_Wk"][dim_head].T, "w1v": i["L1_attn_Wv"].T,
        "w1o": i["L1_attn_Wo"].T[dim_head],
        "b1q": i["L1_attn_bq"][dim_head].reshape(KT, P).T, "b1k": i["L1_attn_bk"][dim_head].reshape(KT, P).T,
        "b1v": i["L1_attn_bv"].reshape(KT, P).T, "b1o": i["L1_attn_bo"],
        "routeT": i["L1_ffn_route_w"].T, "loraAT": i["L1_ffn_A"].reshape(NE * R1, D).T,
        "loraBT": i["L1_ffn_Bw"].transpose(0, 2, 1).reshape(NE * R1, D), "tables": tables(),
    }
    arrays = {f"in_{k}": _np.ascontiguousarray(v) for k, v in arrays.items()}
    nc = _bacc.Bacc("TRN2", target_bir_lowering=False, num_devices=1)
    a = {k[3:]: nc.dram_tensor(k, v.shape, _mybir.dt.from_np(v.dtype), kind="ExternalInput").ap() for k, v in arrays.items()}
    a["out"] = nc.dram_tensor("out", (B * T, D), F32, kind="ExternalOutput").ap()
    a["gates"] = nc.dram_tensor("gates", (4, B, D), F32).ap()
    a["row_scale"] = nc.dram_tensor("row_scale", (D,), F32).ap()
    for n, shape in (("qs", (HB, 4, 3, D, TQ)), ("ks", (HB, 3, 4, 2, D, TQ)), ("vs", (HB, 4, 3, D, TQ))):
        a[n] = nc.dram_tensor(n, shape, BF16).ap()
    a["attn"] = nc.dram_tensor("attn", (HB, 4, 2, D, TQ), F32).ap()
    build(nc, a)
    r = _run(nc, [arrays], core_ids=[0])
    return r.results[0]["out"].reshape(B, T, D)
```
